# Optimizing a Trainium2 kernel written in Bass

```python
import numpy as np
import jax
import jax.numpy as jnp

def _softmax(x, axis=-1):
    return jax.nn.softmax(x, axis=axis)

def _gelu(x):
    return jax.nn.gelu(x, approximate=True)

def _silu(x):
    return jax.nn.silu(x)

def _sigmoid(x):
    return jax.nn.sigmoid(x)

def _layernorm(x, axis=-1, eps=1e-05):
    m = jnp.mean(x, axis=axis, keepdims=True)
    v = jnp.var(x, axis=axis, keepdims=True)
    return (x - m) / jnp.sqrt(v + eps)

def _scatter_add(tgt, idx, src, axis=0):
    return tgt.at[idx].add(src)

def _segment_sum(src, seg, n):
    return jax.ops.segment_sum(src, seg, n)
kernel_name = 'mk_gnn_ffn_d2_gnn_r8_e70db1'

def setup_inputs(seed: int=0):
    np.random.seed(seed)
    _w = jnp.asarray

    def _rec_inputs():
        import jax
        import jax.numpy as jnp
        _gk = jax.random.key(seed)
        x = -0.000202 + 1 * jax.random.normal(jax.random.fold_in(_gk, 1), (6250, 256), jnp.float32)
        _s = jax.random.randint(jax.random.fold_in(_gk, 2), (100000,), 0, 6250, jnp.int32)
        _d = jax.random.randint(jax.random.fold_in(_gk, 3), (100000,), 0, 6250, jnp.int32)
        _loop = jnp.arange(6250, dtype=jnp.int32)
        src = jnp.concatenate([_s, _d, _loop])
        dst = jnp.concatenate([_d, _s, _loop])
        _o = jnp.argsort(dst, stable=True)
        src = src[_o]
        dst = dst[_o]
        edge_type_500 = jax.random.randint(jax.random.fold_in(_gk, 13), (206250,), 0, 500, jnp.int32)
        return (x, src, dst, edge_type_500)
    x, src, dst, edge_type_500 = _rec_inputs()

    def _L0_gnn_setup():
        import jax, jax.numpy as jnp
        import numpy as np
        N_NODES = 3125
        N_EDGES = 50000
        D = 256
        key = jax.random.key(seed)
        k1, k2, k3, k4, k5 = jax.random.split(key, 5)
        feat = jax.random.normal(k1, (N_NODES, D), dtype=jnp.float32)
        src = jax.random.randint(k2, (N_EDGES,), 0, N_NODES, dtype=jnp.int32)
        dst = jax.random.randint(k3, (N_EDGES,), 0, N_NODES, dtype=jnp.int32)
        a = float(np.sqrt(6.0 / (D + D)))
        W1 = jax.random.uniform(k4, (D, D), minval=-a, maxval=a, dtype=jnp.float32)
        W2 = jax.random.uniform(k5, (D, D), minval=-a, maxval=a, dtype=jnp.float32)
        b = jnp.zeros((D,), dtype=jnp.float32)
        return {'feat': feat, 'W1': W1, 'W2': W2, 'b': b, 'src': src, 'dst': dst}
    _L0_gnn_all = _L0_gnn_setup()
    _L0_gnn_in = {k: v for k, v in _L0_gnn_all.items() if k in ('W1', 'W2', 'b')}
    del _L0_gnn_all

    def _L0_ffn_setup():
        import jax, jax.numpy as jnp
        import numpy as np
        IN_CH = 256
        OUT_CH = 256
        key = jax.random.key(seed)
        kx, kw, kb = jax.random.split(key, 3)
        x = jax.random.normal(kx, (8, 512, IN_CH), dtype=jnp.float32)
        bound = 1.0 / np.sqrt(IN_CH)
        weight = jax.random.uniform(kw, (OUT_CH, IN_CH), dtype=jnp.float32, minval=-bound, maxval=bound)
        bias = jax.random.uniform(kb, (OUT_CH,), dtype=jnp.float32, minval=-bound, maxval=bound)
        return {'x': x, 'weight': weight, 'bias': bias}
    _L0_ffn_all = _L0_ffn_setup()
    _L0_ffn_in = {k: v for k, v in _L0_ffn_all.items() if k in ('weight', 'bias')}
    del _L0_ffn_all

    def _L1_gnn_setup():
        import jax, jax.numpy as jnp
        import numpy as np
        G = (1.0, 1.0)

        def to_hypercomplex(x, n_blades):
            return x.reshape(*x.shape[:-1], n_blades, -1).swapaxes(-2, -1)

        def clifford_kernel_2d(w, g):
            g0, g1 = g
            k0 = jnp.concatenate([w[0], g0 * w[1], g1 * w[2], -g0 * g1 * w[3]], axis=1)
            k1 = jnp.concatenate([w[1], w[0], -g1 * w[3], g1 * w[2]], axis=1)
            k2 = jnp.concatenate([w[2], g0 * w[3], w[0], -g0 * w[1]], axis=1)
            k3 = jnp.concatenate([w[3], w[2], w[1], w[0]], axis=1)
            return jnp.concatenate([k0, k1, k2, k3], axis=0)

        def clifford_linear(x, w, b, g=G):
            N = x.shape[0]
            k = clifford_kernel_2d(w, g)
            xf = x.swapaxes(-2, -1).reshape(N, -1)
            out = xf @ k.T + b.reshape(-1)
            C_out = w.shape[1]
            return out.reshape(N, 4, C_out).swapaxes(-2, -1)
        key = jax.random.key(seed)
        ks = jax.random.split(key, 10)
        N, E, R, emb_dim = (12500, 75000, 500, 256)
        C = emb_dim // 4
        s = 0.05
        return {'h': jax.random.normal(ks[0], (N, emb_dim), jnp.float32), 'edge_index': jax.random.randint(ks[1], (2, E), 0, N, jnp.int64), 'edge_type': jax.random.randint(ks[2], (E,), 0, R, jnp.int64), 'relation_emb': jax.random.normal(ks[3], (R, emb_dim), jnp.float32), 'msg_w': jax.random.normal(ks[4], (4, C, C), jnp.float32) * s, 'msg_b': jax.random.normal(ks[5], (4, C), jnp.float32) * s, 'upd_w': jax.random.normal(ks[6], (4, C, C), jnp.float32) * s, 'upd_b': jax.random.normal(ks[7], (4, C), jnp.float32) * s, 'gate_w': jax.random.normal(ks[8], (1, emb_dim), jnp.float32) * s, 'gate_b': jax.random.normal(ks[9], (1,), jnp.float32) * s}
    _L1_gnn_all = _L1_gnn_setup()
    _L1_gnn_in = {k: v for k, v in _L1_gnn_all.items() if k in ('relation_emb', 'msg_w', 'msg_b', 'upd_w', 'upd_b', 'gate_w', 'gate_b')}
    del _L1_gnn_all

    def _L1_ffn_setup():
        import jax, jax.numpy as jnp
        import numpy as np
        B, S, D = (8, 512, 256)
        H = 4 * D
        CAPACITY = 0.5
        key = jax.random.key(seed)
        ks = jax.random.split(key, 6)
        x = jax.random.normal(ks[0], (B, S, D), dtype=jnp.float32)
        attention_mask = jnp.zeros((B, 1, 1, S), dtype=jnp.float32)
        wr = jax.random.normal(ks[1], (D, 1), dtype=jnp.float32) * 0.02
        br = jnp.zeros((1,), dtype=jnp.float32)
        w1 = jax.random.normal(ks[2], (D, H), dtype=jnp.float32) * 0.02
        b1 = jnp.zeros((H,), dtype=jnp.float32)
        w2 = jax.random.normal(ks[3], (H, D), dtype=jnp.float32) * 0.02
        b2 = jnp.zeros((D,), dtype=jnp.float32)
        return {'x': x, 'attention_mask': attention_mask, 'wr': wr, 'br': br, 'w1': w1, 'b1': b1, 'w2': w2, 'b2': b2}
    _L1_ffn_all = _L1_ffn_setup()
    _L1_ffn_in = {k: v for k, v in _L1_ffn_all.items() if k in ('attention_mask', 'wr', 'br', 'w1', 'b1', 'w2', 'b2')}
    del _L1_ffn_all
    return {'x': x, 'src': src, 'dst': dst, 'edge_type_500': edge_type_500, 'L0_gnn_W1': _L0_gnn_in['W1'], 'L0_gnn_W2': _L0_gnn_in['W2'], 'L0_gnn_b': _L0_gnn_in['b'], 'L0_ffn_weight': _L0_ffn_in['weight'], 'L0_ffn_bias': _L0_ffn_in['bias'], 'L1_gnn_relation_emb': _L1_gnn_in['relation_emb'], 'L1_gnn_msg_w': _L1_gnn_in['msg_w'], 'L1_gnn_msg_b': _L1_gnn_in['msg_b'], 'L1_gnn_upd_w': _L1_gnn_in['upd_w'], 'L1_gnn_upd_b': _L1_gnn_in['upd_b'], 'L1_gnn_gate_w': _L1_gnn_in['gate_w'], 'L1_gnn_gate_b': _L1_gnn_in['gate_b'], 'L1_ffn_attention_mask': _L1_ffn_in['attention_mask'], 'L1_ffn_wr': _L1_ffn_in['wr'], 'L1_ffn_br': _L1_ffn_in['br'], 'L1_ffn_w1': _L1_ffn_in['w1'], 'L1_ffn_b1': _L1_ffn_in['b1'], 'L1_ffn_w2': _L1_ffn_in['w2'], 'L1_ffn_b2': _L1_ffn_in['b2']}

def reference(x, src, dst, edge_type_500, L0_gnn_W1, L0_gnn_W2, L0_gnn_b, L0_ffn_weight, L0_ffn_bias, L1_gnn_relation_emb, L1_gnn_msg_w, L1_gnn_msg_b, L1_gnn_upd_w, L1_gnn_upd_b, L1_gnn_gate_w, L1_gnn_gate_b, L1_ffn_attention_mask, L1_ffn_wr, L1_ffn_br, L1_ffn_w1, L1_ffn_b1, L1_ffn_w2, L1_ffn_b2):
    import jax
    import jax.numpy as jnp

    def _L0_gnn_ref(feat, W1, W2, b, src, dst):
        import jax, jax.numpy as jnp
        import numpy as np
        N_NODES = 3125
        N_EDGES = 50000
        D = 256
        n = feat.shape[0]
        ones = jnp.ones(src.shape[0], dtype=feat.dtype)
        out_deg = jnp.maximum(jax.ops.segment_sum(ones, src, num_segments=n), 1.0)
        in_cnt = jax.ops.segment_sum(ones, dst, num_segments=n)
        t1 = feat @ W1
        msg = t1[src] + feat[src] * feat[dst] @ W2
        scale = jnp.sqrt(out_deg[src]) * jnp.sqrt(out_deg[dst])
        msg = msg / scale[:, None]
        agg = jax.ops.segment_sum(msg, dst, num_segments=n)
        embed = jnp.where(in_cnt[:, None] > 0, t1 + agg, jnp.zeros_like(t1))
        embed = embed + b
        embed = jax.nn.leaky_relu(embed, negative_slope=0.01)
        norm = jnp.linalg.norm(embed, axis=1, keepdims=True)
        embed = embed / jnp.maximum(norm, 1e-12)
        return embed

    def _L0_ffn_ref(x, weight, bias):
        import jax, jax.numpy as jnp
        import numpy as np
        IN_CH = 256
        OUT_CH = 256
        return jnp.einsum('bsi,oi->bso', x, weight) + bias

    def _L1_gnn_ref(h, edge_index, edge_type, relation_emb, msg_w, msg_b, upd_w, upd_b, gate_w, gate_b):
        import jax, jax.numpy as jnp
        import numpy as np
        G = (1.0, 1.0)

        def to_hypercomplex(x, n_blades):
            return x.reshape(*x.shape[:-1], n_blades, -1).swapaxes(-2, -1)

        def clifford_kernel_2d(w, g):
            g0, g1 = g
            k0 = jnp.concatenate([w[0], g0 * w[1], g1 * w[2], -g0 * g1 * w[3]], axis=1)
            k1 = jnp.concatenate([w[1], w[0], -g1 * w[3], g1 * w[2]], axis=1)
            k2 = jnp.concatenate([w[2], g0 * w[3], w[0], -g0 * w[1]], axis=1)
            k3 = jnp.concatenate([w[3], w[2], w[1], w[0]], axis=1)
            return jnp.concatenate([k0, k1, k2, k3], axis=0)

        def clifford_linear(x, w, b, g=G):
            N = x.shape[0]
            k = clifford_kernel_2d(w, g)
            xf = x.swapaxes(-2, -1).reshape(N, -1)
            out = xf @ k.T + b.reshape(-1)
            C_out = w.shape[1]
            return out.reshape(N, 4, C_out).swapaxes(-2, -1)
        n_blades = 4
        num_nodes = h.shape[0]
        h_hc = to_hypercomplex(h, n_blades)
        r_hc = to_hypercomplex(relation_emb, n_blades)
        src, dst = (edge_index[0], edge_index[1])
        h_src = h_hc[src]
        r_uv = r_hc[edge_type]
        m = clifford_linear(h_src * r_uv, msg_w, msg_b)
        gate = jax.nn.sigmoid(r_uv.reshape(r_uv.shape[0], -1) @ gate_w.T + gate_b)
        m = m * gate[:, :, None]
        ones = jnp.ones_like(src, dtype=jnp.float32)
        deg_src = jax.ops.segment_sum(ones, src, num_segments=num_nodes)
        deg_dst = jax.ops.segment_sum(ones, dst, num_segments=num_nodes)
        norm = jnp.maximum(deg_src[src] * deg_dst[dst], 1.0) ** (-0.5)
        m = m * norm[:, None, None]
        h_agg = jax.ops.segment_sum(m, dst, num_segments=num_nodes)
        h_out = clifford_linear(h_hc + h_agg, upd_w, upd_b)
        return h_out.reshape(num_nodes, -1)

    def _L1_ffn_ref(x, attention_mask, wr, br, w1, b1, w2, b2):
        import jax, jax.numpy as jnp
        import numpy as np
        B, S, D = (8, 512, 256)
        H = 4 * D
        CAPACITY = 0.5
        b, s, d = x.shape
        weights = (jnp.einsum('bsd,do->bso', x, wr) + br)[..., 0]
        k = max(1, int(CAPACITY * s))
        kk = k - 1 if k > 1 else 1
        _, idx = jax.lax.top_k(weights, k)
        sel_idx = idx[:, :kk]
        sel = jnp.take_along_axis(x, sel_idx[:, :, None], axis=1)
        h = jax.nn.gelu(jnp.einsum('bkd,dh->bkh', sel, w1) + b1)
        y = jnp.einsum('bkh,hd->bkd', h, w2) + b2
        w_sel = jnp.take_along_axis(weights, sel_idx, axis=1)
        y = y * w_sel[..., None]
        batch_idx = jnp.arange(b)[:, None]
        processed = jnp.zeros_like(x).at[batch_idx, sel_idx].set(y)
        return processed + x
    edge_index = jnp.stack([src, dst])
    x = x + _L0_gnn_ref(_layernorm(x, axis=-1), L0_gnn_W1, L0_gnn_W2, L0_gnn_b, src, dst)
    x = x + _L0_ffn_ref(_layernorm(x, axis=-1)[None], L0_ffn_weight, L0_ffn_bias)[0]
    x = x + _L1_gnn_ref(_layernorm(x, axis=-1), edge_index, edge_type_500, L1_gnn_relation_emb, L1_gnn_msg_w, L1_gnn_msg_b, L1_gnn_upd_w, L1_gnn_upd_b, L1_gnn_gate_w, L1_gnn_gate_b)
    x = x + _L1_ffn_ref(_layernorm(x, axis=-1)[None], L1_ffn_attention_mask, L1_ffn_wr, L1_ffn_br, L1_ffn_w1, L1_ffn_b1, L1_ffn_w2, L1_ffn_b2)[0]
    return x

_drawn_inputs = setup_inputs


def setup_inputs(seed=0):
    import zlib

    import numpy as np

    out = dict(_drawn_inputs(seed))
    spreads = {'L0_gnn_b': (0.0, 0.8), 'L1_ffn_b1': (0.0, 0.8), 'L1_ffn_b2': (0.0, 0.8)}
    factors = {'L0_gnn_W2': 5.472,
     'L1_gnn_msg_b': 3.841,
     'L1_gnn_gate_w': 4.249,
     'L1_ffn_wr': 4.848,
     'L1_ffn_w1': 6.583,
     'L1_ffn_w2': 6.133}
    for name, (base, spread) in spreads.items():
        noise = np.random.default_rng([zlib.crc32(name.encode()), seed]).standard_normal(out[name].shape)
        drawn = base * np.exp(spread * noise) if base else spread * noise
        out[name] = jnp.asarray(drawn.astype(out[name].dtype))
    for name, factor in factors.items():
        out[name] = (out[name] * factor).astype(out[name].dtype)
    return out
```

```python
import concourse.bass as bass
from concourse import mybir
from contextlib import ExitStack

F32 = mybir.dt.float32
BF16 = mybir.dt.bfloat16
I32 = mybir.dt.int32
ALU = mybir.AluOpType
ACT = mybir.ActivationFunctionType
AX = mybir.AxisListType.X

P = 128
N = 6250
D = 256
E = 206250
R = 500
H = 1024
NB = -(-N // P)
TAIL = N - (NB - 1) * P
TILES = -(-E // P)
SC = -(-(TILES + NB) // P)
SLOTS = SC * P
FULLC = E // (P * P)
RESTT = (E - FULLC * P * P) // P
RESTE = E - FULLC * P * P - RESTT * P
W = 260
DW = D + 1
PAD_SRC = NB * P - 1
PAD_DST = 1 << 13
HT = H // P
FI = NB // 2 + 1
RING = 16
IT = SLOTS // RING
HG = 16
TOP = N // 2 - 1
BITS = 31
EPS = 1e-5


class Chain:

    def __init__(self, eng, sem):
        self.eng, self.sem, self.base, self.n = eng, sem, 0, 0

    def __call__(self, ins):
        self.n += 1
        ins.then_inc(self.sem, 1)
        self.eng.wait_ge(self.sem, self.base + self.n)

    def enter(self, step, per):
        self.start, self.per = (self.base, self.n), per
        self.base, self.n = self.start[0] + self.start[1] + step * per, 0

    def leave(self, steps):
        assert self.n == self.per, (self.n, self.per)
        self.base, self.n = self.start[0] + self.start[1] + steps * self.per, 0


def program(nc, x, src, dst, etype, w1_0, w2_0, b_0, wf, bf, rel, msg_w, msg_b, upd_w, upd_b,
            gate_w, gate_b, wr, br, w1, b1, w2, b2, out):
    ctx = ExitStack()
    with ctx:
        def sb(name, shape, dt=F32):
            return ctx.enter_context(nc.sbuf_tensor(name, shape, dt))

        def sem(name):
            return ctx.enter_context(nc.semaphore(name))

        edges_d = nc.dram_tensor("edges_d", (SLOTS, 3 * P), I32).ap()
        t1_d = nc.dram_tensor("t1_d", (NB * P, W), F32).ap()
        t2_d = nc.dram_tensor("t2_d", (NB * P, W), F32).ap()
        gr_d = nc.dram_tensor("gr_d", (R, W), F32).ap()

        X = sb("X", [P, NB, D])
        accf = sb("accf", [P, NB * W])
        ringf = sb("ringf", [P, 2 * RING * W])
        srci = sb("srci", [P, SLOTS], I32)
        typi = sb("typi", [P, SLOTS], I32)
        dstf = sb("dstf", [P, SLOTS])
        brow = sb("brow", [1, SLOTS], I32)
        idxs = sb("idxs", [P, 2, RING], I32)
        sel = sb("sel", [P, 4, P])
        acc = accf[:, :].rearrange("p (b w) -> p b w", w=W)
        gath = ringf[:, 0:RING * W].rearrange("p (k w) -> p k w", w=W)
        relg = ringf[:, RING * W:2 * RING * W].rearrange("p (k w) -> p k w", w=W)
        raw = ringf[:, 0:SC * 384].bitcast(I32).rearrange("p (c w) -> p c w", w=384)
        o = SC * 384
        ohlo = ringf[:, o:o + HG * P].bitcast(BF16).rearrange("p (r t l) -> p r t l", r=2, l=P)
        o += HG * P
        ohhi = ringf[:, o:o + HG * NB].bitcast(BF16).rearrange("p (r t l) -> p r t l", r=2, l=NB)
        slot_i = accf[:, 0:SC * 384].bitcast(I32).rearrange("p (c w) -> p c w", w=384)
        slot_f = accf[:, SC * 384:2 * SC * 384].rearrange("p (c w) -> p c w", w=384)
        o = 2 * SC * 384
        wraw = accf[:, o:o + 3 * 2 * D].rearrange("p (m t i) -> p m t i", m=3, t=2)
        hlo = srci[:, :].bitcast(BF16)[:, 0:SLOTS]
        hhi = srci[:, :].bitcast(BF16)[:, SLOTS:2 * SLOTS]
        lo_i = typi[:, :].rearrange("p (c e) -> p c e", e=P)
        hi_i = dstf[:, :].bitcast(I32).rearrange("p (c e) -> p c e", e=P)
        o = 2 * H
        f1 = ringf[:, 0:o].rearrange("p (t n) -> p t n", t=2)
        f2 = ringf[:, o:o + HT * D].rearrange("p (t n) -> p t n", t=HT)
        o += HT * D
        hid = ringf[:, o:o + 2 * HT * 2 * P].rearrange("p (r t n) -> p r t n", r=2, t=HT)
        rel_sb = sb("rel_sb", [P, 4, W])
        gw = sb("gw", [P, D])
        gprod = sb("gprod", [P, D])
        gb = sb("gb", [P, 1])
        glog = sb("glog", [P, 4])

        ident = sb("ident", [P, P])
        ones = sb("ones", [P, P])
        iof = sb("iof", [P, P])
        iob = sb("iob", [P, P], BF16)
        zb = sb("zb", [P, P], BF16)
        pidx = sb("pidx", [P, SC])
        w1s = sb("w1s", [P, 2, D])
        w2s = sb("w2s", [P, 2, D])
        wt = sb("wt", [P, 3, 2, D])
        b0s = sb("b0s", [P, D])
        bfs = sb("bfs", [P, D])
        mbs = sb("mbs", [P, D])
        ubs = sb("ubs", [P, D])
        zst = sb("zst", [P, 2, 2 * D])
        zts = sb("zts", [P, 2, 2 * D])
        tmp = sb("tmp", [P, 2, D])
        st = sb("st", [P, NB, 6])
        mean = sb("mean", [P, NB])
        rstd = sb("rstd", [P, NB])
        sm0 = sb("sm0", [P, NB])
        sm1 = sb("sm1", [P, NB])
        deg = sb("deg", [P, NB])
        degu = sb("degu", [P, NB])
        has = sb("has", [P, NB])
        inq = sb("inq", [P, NB])
        ssq = sb("ssq", [P, NB])
        b128 = sb("b128", [P, NB])
        cmp1 = sb("cmp1", [P, NB, SC])
        cmp2 = sb("cmp2", [P, SC, NB - 1])
        last = sb("last", [P, SC])
        cnt = sb("cnt", [P, NB])
        sbs = sb("sbs", [P, NB])
        bp = sb("bp", [P, SC])
        bp128 = sb("bp128", [P, SC])
        tpf = sb("tpf", [P, SC])
        tpi = sb("tpi", [P, SC], I32)
        bti = sb("bti", [SC, P], I32)
        wrs = sb("wrs", [P, D])
        brs = sb("brs", [P, 1])
        b1s = sb("b1s", [P, HT])
        b2s = sb("b2s", [P, D])
        tri = sb("tri", [P, P])
        valid = sb("valid", [P, NB])
        score = sb("score", [P, NB])
        keyed = sb("keyed", [P, NB])
        flag = sb("flag", [P, NB])
        tie = sb("tie", [P, NB])
        pick = sb("pick", [P, NB])
        shift = sb("shift", [P, BITS], I32)
        bit = sb("bit", [P, BITS], I32)
        bitf = sb("bitf", [P, BITS])
        found = sb("found", [P, 1], I32)
        trial = sb("trial", [P, 1], I32)
        step = sb("step", [P, 1], I32)
        hits = sb("hits", [P, 1])
        sign = sb("sign", [P, 1])
        want = sb("want", [P, 1])
        thr = sb("thr", [P, 1])
        need = sb("need", [P, 1])

        def bank(name):
            return ctx.enter_context(nc.psum_tensor(name, [P, 512], F32))

        psE = ctx.enter_context(nc.psum_tensor("psE", [P, 4, 512], F32))
        psT = ctx.enter_context(nc.psum_tensor("psT", [P, 2, 512], F32))
        psY = ctx.enter_context(nc.psum_tensor("psY", [P, 2, 512], F32))

        s_const = sem("s_const")
        s_pool = sem("s_pool")
        s_dve = sem("s_dve")
        s_pad = sem("s_pad")
        s_x = sem("s_x")
        s_raw = sem("s_raw")
        s_w = sem("s_w")
        s_gw = sem("s_gw")
        s_ed = sem("s_ed")
        s_oh = sem("s_oh")
        s_hmm = sem("s_hmm")
        s_hist = sem("s_hist")
        s_cnt = sem("s_cnt")
        s_lo = sem("s_lo")
        s_tp = sem("s_tp")
        s_bt = sem("s_bt")
        s_bti = sem("s_bti")
        s_brow = sem("s_brow")
        s_slot = sem("s_slot")
        s_cv = sem("s_cv")
        s_st = sem("s_st")
        s_sc = sem("s_sc")
        s_kneg = sem("s_kneg")
        s_wt = sem("s_wt")
        s_wc = sem("s_wc")
        s_sq = sem("s_sq")
        s_sqd = sem("s_sqd")
        s_gr = sem("s_gr")
        s_grd = sem("s_grd")
        s_trow = sem("s_trow")
        s_td = sem("s_td")
        s_zero = sem("s_zero")
        s_turn = sem("s_turn")
        s_idx = sem("s_idx")
        s_g = [sem(f"s_g{k}") for k in range(RING)]
        s_r = [sem(f"s_r{k}") for k in range(RING)]
        s_sel = sem("s_sel")
        s_prod = sem("s_prod")
        s_mm = sem("s_mm")
        s_add = sem("s_add")
        s_z = sem("s_z")
        s_ztp = sem("s_ztp")
        s_zts = sem("s_zts")
        s_y = sem("s_y")
        s_yo = sem("s_yo")
        s_fw = sem("s_fw")
        s_hits = sem("s_hits")
        s_total = sem("s_total")
        s_fz = sem("s_fz")
        s_ftp = sem("s_ftp")
        s_fts = sem("s_fts")
        s_hp = sem("s_hp")
        s_hs = sem("s_hs")
        s_fy = sem("s_fy")
        s_fo = sem("s_fo")
        s_out = sem("s_out")
        STAGES = 4

        block = ctx.enter_context(nc.Block())

        src_t = edges_d.rearrange("(c p) w -> p c w", p=P)

        @block.sync
        def _(sp):
            sp.dma_start(X[:, 0:NB - 1, :], x[0:(NB - 1) * P, :].rearrange("(b p) d -> p b d", p=P)).then_inc(s_x, 16)
            sp.wait_ge(s_pad, 1)
            sp.dma_start(X[0:TAIL, NB - 1, :], x[(NB - 1) * P:N, :]).then_inc(s_x, 16)
            for n, a in enumerate((src, dst, etype)):
                c0, c1 = n * P, (n + 1) * P
                sp.dma_start(raw[:, 0:FULLC, c0:c1],
                             a[0:FULLC * P * P].rearrange("(c p e) -> p c e", p=P, e=P)).then_inc(s_raw, 16)
                e0 = FULLC * P * P
                sp.dma_start(raw[0:RESTT, FULLC, c0:c1],
                             a[e0:e0 + RESTT * P].rearrange("(p e) -> p e", e=P)).then_inc(s_raw, 16)
                sp.dma_start(raw[RESTT:RESTT + 1, FULLC, c0:c0 + RESTE],
                             a[e0 + RESTT * P:E].rearrange("(p e) -> p e", p=1)).then_inc(s_raw, 16)
            sp.dma_start(w1s[:, :, :], w1_0.rearrange("(t p) n -> p t n", p=P)).then_inc(s_w, 16)
            sp.dma_start(w2s[:, :, :], w2_0.rearrange("(t p) n -> p t n", p=P)).then_inc(s_w, 16)
            sp.dma_start(wraw[:, 0, :, :], wf.rearrange("(t p) n -> p t n", p=P)).then_inc(s_w, 16)
            for m, a in ((1, msg_w), (2, upd_w)):
                for bo in range(4):
                    for bi in range(4):
                        p0 = 64 * (bo % 2)
                        sp.dma_start(wraw[p0:p0 + 64, m, bo // 2, 64 * bi:64 * bi + 64], a[bo ^ bi, :, :]).then_inc(s_w, 16)
            for t, a in ((b0s, b_0), (bfs, bf)):
                sp.dma_start(t[:, :], a.rearrange("(o d) -> o d", o=1).broadcast_to([P, D])).then_inc(s_w, 16)
            sp.dma_start(b2s[:, :], b2.rearrange("(o d) -> o d", o=1).broadcast_to([P, D])).then_inc(s_w, 16)
            sp.dma_start(wrs[:, :], wr.rearrange("d o -> o d").broadcast_to([P, D])).then_inc(s_w, 16)
            sp.dma_start(brs[:, :], br.rearrange("(o d) -> o d", o=1).broadcast_to([P, 1])).then_inc(s_w, 16)
            sp.dma_start(b1s[:, :], b1.rearrange("(t p) -> p t", p=P), allow_slow_non_contiguous=True).then_inc(s_w, 16)
            for t, a in ((mbs, msg_b), (ubs, upd_b)):
                sp.dma_start(t[:, :], a.rearrange("(o a) c -> o (a c)", o=1).broadcast_to([P, D])).then_inc(s_w, 16)
            sp.dma_start(rel_sb[0:R // 4, :, 0:D], rel.rearrange("(k p) d -> p k d", k=4)).then_inc(s_gw, 16)
            sp.dma_start(gw[:, :], gate_w.broadcast_to([P, D])).then_inc(s_gw, 16)
            sp.dma_start(gb[:, :], gate_b.rearrange("(o d) -> o d", o=1).broadcast_to([P, 1])).then_inc(s_gw, 16)
            sp.wait_ge(s_raw, 16 * 9)
            sp.dma_start(src_t, raw[:, :, :]).then_inc(s_ed, 16)
            sp.wait_ge(s_bti, 1)
            sp.dma_start(brow[0:1, :].rearrange("o (c p) -> o c p", p=P), bti[:, :]).then_inc(s_brow, 16)
            sp.wait_ge(s_gr, 1)
            sp.dma_start(gr_d.rearrange("(k p) w -> p k w", k=4), rel_sb[0:R // 4, :, :]).then_inc(s_grd, 16)
            for layer, table in enumerate((t1_d, t2_d)):
                for c in range(NB // 7):
                    sp.wait_ge(s_trow, layer * NB + 7 * (c + 1))
                    sp.dma_start(table.rearrange("(b p) w -> p b w", p=P)[:, 7 * c:7 * c + 7, :],
                                 acc[:, 7 * c:7 * c + 7, :]).then_inc(s_td, 16)
            sp.wait_ge(s_add, 2 * SLOTS + 4)
            sp.dma_start(f1, w1.rearrange("(t p) n -> p t n", p=P)).then_inc(s_fw, 16)
            sp.dma_start(f2, w2.rearrange("(t p) n -> p t n", p=P)).then_inc(s_fw, 16)
            for c in range(NB // 7):
                sp.wait_ge(s_fo, 2 + 7 * (c + 1))
                b0, full = 7 * c, min(7 * c + 7, NB - 1)
                sp.dma_start(out[b0 * P:full * P, :].rearrange("(b p) d -> p b d", p=P), acc[:, b0:full, 0:D]).then_inc(s_out, 16)
            sp.dma_start(out[(NB - 1) * P:N, :], acc[0:TAIL, NB - 1, 0:D]).then_inc(s_out, 16)
            sp.wait_ge(s_out, 16 * (NB // 7 + 1))

        @block.gpsimd
        def _(pool):
            pool.memset(ident[:, :], 0.0).then_inc(s_pool, 1)
            pool.memset(ones[:, :], 1.0).then_inc(s_const, 1)
            pool.iota(iof[:, :], [[1, P]], base=0, channel_multiplier=0, allow_small_or_imprecise_dtypes=True).then_inc(s_const, 1)
            pool.iota(iob[:, :], [[1, P]], base=0, channel_multiplier=0, allow_small_or_imprecise_dtypes=True).then_inc(s_const, 1)
            pool.iota(pidx[:, :], [[P, SC]], base=0, channel_multiplier=1, allow_small_or_imprecise_dtypes=True).then_inc(s_const, 1)
            pool.memset(zb[:, :], 0.0).then_inc(s_const, 1)
            pool.memset(tri[:, :], 1.0).then_inc(s_pool, 1)
            pool.iota(valid[:, :], [[P, NB]], base=0, channel_multiplier=1, allow_small_or_imprecise_dtypes=True).then_inc(s_const, 1)
            pool.iota(shift[:, :], [[-1, BITS]], base=BITS - 1, channel_multiplier=0).then_inc(s_const, 1)
            pool.wait_ge(s_pool, 2)
            pool.affine_select(out=tri[:, :], in_=tri[:, :], compare_op=ALU.is_gt, fill=0.0, base=0,
                               pattern=[[1, P]], channel_multiplier=-1).then_inc(s_const, 1)
            pool.affine_select(out=ident[:, :], in_=ident[:, :], compare_op=ALU.not_equal, fill=1.0, base=0,
                               pattern=[[-1, P]], channel_multiplier=1).then_inc(s_const, 1)
            pool.wait_ge(s_ed, 16)
            pool.wait_ge(s_tp, 1)
            for c in range(SC):
                pool.indirect_dma_start(slot_i[:, c, :], None, edges_d,
                                        bass.IndirectOffsetOnAxis(ap=tpi[:, c:c + 1], axis=0)).then_inc(s_slot, 16)

            def gathers(i, first_item, table, relations):
                in_dram = 16 * (NB // 7) * (1 + relations)
                for k in range(RING):
                    if k % 8 == 0:
                        pool.wait_ge(s_idx, (first_item // 8 + k // 8 + 1) + 2 * i)
                    pool.wait_ge(s_mm, first_item + k + 1 + RING * i)
                    pool.sem_inc(s_turn, 1)
                    pool.wait_ge(s_td, in_dram)
                    pool.indirect_dma_start(gath[:, k, :], None, table, bass.IndirectOffsetOnAxis(
                        ap=idxs[:, 0, k:k + 1], axis=0)).then_inc(s_g[k], 16)
                    if relations:
                        pool.wait_ge(s_grd, 16)
                        pool.indirect_dma_start(relg[:, k, :], None, gr_d, bass.IndirectOffsetOnAxis(
                            ap=idxs[:, 1, k:k + 1], axis=0)).then_inc(s_r[k], 16)

            with pool.Fori(0, IT) as i:
                gathers(i, 0, t1_d, False)
            with pool.Fori(0, IT) as i:
                gathers(i, SLOTS, t2_d, True)

        @block.tensor
        def _(pe):
            pe.sem_inc(s_hmm, 2)
            pe.sem_inc(s_st, 2)
            pe.sem_inc(s_mm, RING)
            pe.sem_inc(s_ztp, 2)
            pe.sem_inc(s_y, 2)
            pe.sem_inc(s_ftp, 2)
            pe.sem_inc(s_fy, 2)
            pe.wait_ge(s_const, 9)
            pe.wait_ge(s_kneg, 1)
            for m in range(3):
                for it in range(2):
                    for ot in range(2):
                        ins = nc.tensor.transpose(psE[:, m, it * D + ot * P:it * D + ot * P + P],
                                                  wraw[:, m, ot, it * P:it * P + P], ident[:, :])
            ins.then_inc(s_wt, 1)
            nc.tensor.matmul(psY[:, 0, 0:NB], zb[:, :], zb[:, 0:NB], start=True, stop=False)
            with pe.Fori(0, SLOTS // HG) as i:
                pe.wait_ge(s_oh, 2 * i + 2)
                for t in range(HG):
                    ins = nc.tensor.matmul(psY[:, 0, 0:NB], ohlo[:, i & 1, t, :], ohhi[:, i & 1, t, :],
                                           start=False, stop=False)
                ins.then_inc(s_hmm, 1)
            nc.tensor.matmul(psY[:, 0, 0:NB], zb[:, :], zb[:, 0:NB], start=False, stop=True).then_inc(s_hist, 1)
            pe.wait_ge(s_cnt, 1)
            nc.tensor.matmul(psY[:, 1, 0:NB], ones[:, :], cnt[:, :], start=True, stop=True).then_inc(s_lo, 1)
            pe.wait_ge(s_tp, 1)
            nc.tensor.transpose(psE[0:SC, 3, 0:P], bp[:, :], ident[:, :]).then_inc(s_bt, 1)
            pe.wait_ge(s_cv, 1)
            for c in range(SC):
                pe.wait_ge(s_sc, c + 1)
                for n in range(3):
                    ins = nc.tensor.transpose(psT[:, c % 2, n * P:n * P + P], slot_f[:, c, n * P:n * P + P], ident[:, :])
                ins.then_inc(s_st, 1)

            def edge_pass(first_item, products):
                with pe.Fori(0, IT) as i:
                    for k in range(RING):
                        n = first_item + k + RING * i
                        pe.wait_ge(s_sel, n + 1)
                        if products:
                            pe.wait_ge(s_prod, n + 1 - first_item)
                        else:
                            pe.wait_ge(s_g[k], 16 * i + 16)
                        pe.wait_ge(s_add, n + 1)
                        nc.tensor.matmul(psE[:, k % 4, 0:DW], sel[:, k % 4, :], gath[:, k, 0:DW],
                                         start=True, stop=True).then_inc(s_mm, 1)

            def dense(stage, nk, weights):
                first = stage * NB

                def turn(n, par, gap=1):
                    pe.wait_ge(s_z, n + 3)
                    pe.wait_ge(s_zts, n + gap)
                    for t in range(nk):
                        ins = nc.tensor.transpose(psT[:, par, t * P:t * P + P], zst[:, par, t * P:t * P + P], ident[:, :])
                    ins.then_inc(s_ztp, 1)

                def product(n, par, gap=1):
                    pe.wait_ge(s_zts, n + 3)
                    pe.wait_ge(s_yo, n + gap)
                    for t in range(nk):
                        ins = nc.tensor.matmul(psY[:, par, 0:D], zts[:, par, t * P:t * P + P], weights(t),
                                               start=(t == 0), stop=(t == nk - 1))
                    ins.then_inc(s_y, 1)

                turn(first, 0, gap=2)
                turn(first + 1, 1)
                product(first, 0, gap=2)
                with pe.Fori(0, NB // 2 - 1) as i:
                    n = first + 1 + 2 * i
                    turn(n + 1, 0)
                    product(n, 1)
                    turn(n + 2, 1)
                    product(n + 1, 0)
                turn(first + NB - 1, 0)
                product(first + NB - 2, 1)
                product(first + NB - 1, 0)

            edge_pass(0, False)
            dense(0, 4, lambda t: (w1s if t < 2 else w2s)[:, t % 2, :])
            dense(1, 2, lambda t: wt[:, 0, t, :])
            edge_pass(SLOTS, True)
            dense(2, 2, lambda t: wt[:, 1, t, :])
            dense(3, 2, lambda t: wt[:, 2, t, :])

            with pe.Fori(0, BITS + 2) as i:
                pe.wait_ge(s_hits, i + 1)
                nc.tensor.matmul(psE[:, 0, 0:1], ones[:, :], hits[:, :], start=True, stop=True).then_inc(s_total, 1)
            pe.wait_ge(s_hits, BITS + 3)
            nc.tensor.matmul(psE[:, 1, 0:NB], tri[:, :], tie[:, :], start=True, stop=True)
            nc.tensor.matmul(psE[:, 2, 0:NB], ones[:, :], tie[:, :], start=True, stop=True).then_inc(s_total, 1)

            def turn(m, par, blocks=2):
                pe.wait_ge(s_fz, m + 3)
                pe.wait_ge(s_fts, m + 1)
                for t in range(2):
                    for q in range(blocks):
                        ins = nc.tensor.transpose(psT[:, par, (2 * t + q) * P:(2 * t + q) * P + P],
                                                  zst[:, par, q * D + t * P:q * D + t * P + P], ident[:, :])
                ins.then_inc(s_ftp, 1)

            def feed(m, par, blocks=2):
                w = blocks * P
                pe.wait_ge(s_fts, m + 3)
                for ht in range(HT):
                    pe.wait_ge(s_hs, HT * m + ht + 1)
                    for t in range(2):
                        ins = nc.tensor.matmul(psE[:, ht % 4, 0:w], f1[:, t, ht * P:ht * P + P],
                                               zts[:, par, 2 * t * P:2 * t * P + w], start=(t == 0), stop=(t == 1))
                    ins.then_inc(s_hp, 1)
                for q in range(blocks):
                    pe.wait_ge(s_fo, 2 * m + q + 1)
                    for ht in range(HT):
                        pe.wait_ge(s_hs, HT * m + ht + 5)
                        ins = nc.tensor.matmul(psY[:, q, 0:D], hid[:, par, ht, q * P:q * P + P], f2[:, ht, :],
                                               start=(ht == 0), stop=(ht == HT - 1))
                    ins.then_inc(s_fy, 1)

            pe.wait_ge(s_fw, 32)
            turn(0, 0)
            with pe.Fori(0, FI // 2 - 1) as i:
                turn(2 * i + 1, 1)
                feed(2 * i, 0)
                turn(2 * i + 2, 0)
                feed(2 * i + 1, 1)
            turn(FI - 2, 1)
            feed(FI - 3, 0)
            turn(FI - 1, 0, 1)
            feed(FI - 2, 1)
            feed(FI - 1, 0, 1)

        @block.scalar
        def _(act):
            act.sem_inc(s_sc, 2)
            act.sem_inc(s_zts, 2)
            act.sem_inc(s_fts, 2)
            act.sem_inc(s_hs, 4)
            act.wait_ge(s_sq, 1)
            nc.scalar.activation(glog[0:R // 4, :], glog[0:R // 4, :], ACT.Sigmoid, bias=gb[0:R // 4, :]).then_inc(s_sqd, 1)
            act.wait_ge(s_hist, 1)
            for c in range(SC):
                act.wait_ge(s_st, c + 3)
                nc.scalar.copy(srci[:, bass.ts(c, P)], psT[:, c % 2, 0:P])
                nc.scalar.copy(dstf[:, bass.ts(c, P)], psT[:, c % 2, P:2 * P])
                nc.scalar.copy(typi[:, bass.ts(c, P)], psT[:, c % 2, 2 * P:3 * P]).then_inc(s_sc, 1)
            act.wait_ge(s_sq, 2)
            nc.scalar.activation(degu[:, :], degu[:, :], ACT.Sqrt).then_inc(s_sqd, 1)
            act.wait_ge(s_sq, 3)
            nc.scalar.activation(rstd[:, :], rstd[:, :], ACT.Sqrt).then_inc(s_sqd, 1)

            def indices(first_item, relations):
                with act.Fori(0, IT) as i:
                    for h in range(2):
                        act.wait_ge(s_mm, first_item + 8 * h + 8 + RING * i)
                        for m, t in enumerate((srci, typi)[:1 + relations]):
                            ins = nc.scalar.copy(idxs[:, m, 8 * h:8 * h + 8], t[:, bass.ds(RING * i + 8 * h, 8)])
                        ins.then_inc(s_idx, 1)

            def dense(stage, nk):
                def copy(n, par, gap=1):
                    act.wait_ge(s_ztp, n + 3)
                    act.wait_ge(s_y, n + gap)
                    nc.scalar.copy(zts[:, par, 0:nk * P], psT[:, par, 0:nk * P]).then_inc(s_zts, 1)

                copy(stage * NB, 0, gap=2)
                with act.Fori(0, NB // 2) as i:
                    copy(stage * NB + 1 + 2 * i, 1)
                    copy(stage * NB + 2 + 2 * i, 0)

            act.wait_ge(s_sc, SC + 2)
            indices(0, False)
            act.wait_ge(s_sq, 4)
            nc.scalar.activation(inq[:, :], inq[:, :], ACT.Sqrt).then_inc(s_sqd, 1)
            dense(0, 4)
            act.wait_ge(s_sq, 5)
            nc.scalar.activation(ssq[:, :], ssq[:, :], ACT.Sqrt).then_inc(s_sqd, 1)
            act.wait_ge(s_sq, 6)
            nc.scalar.activation(rstd[:, :], rstd[:, :], ACT.Sqrt).then_inc(s_sqd, 1)
            dense(1, 2)
            act.wait_ge(s_sq, 7)
            nc.scalar.activation(rstd[:, :], rstd[:, :], ACT.Sqrt).then_inc(s_sqd, 1)
            indices(SLOTS, True)
            dense(2, 2)
            dense(3, 2)
            act.wait_ge(s_sq, 8)
            nc.scalar.activation(rstd[:, :], rstd[:, :], ACT.Sqrt).then_inc(s_sqd, 1)

            def feed(m, par, blocks=2):
                w = blocks * P
                act.wait_ge(s_ftp, m + 3)
                act.wait_ge(s_fy, 2 * m + 1)
                nc.scalar.copy(zts[:, par, :].rearrange("p (t n) -> p t n", t=2)[:, :, 0:w],
                               psT[:, par, :].rearrange("p (t n) -> p t n", t=2)[:, :, 0:w]).then_inc(s_fts, 1)
                for ht in range(HT):
                    act.wait_ge(s_hp, HT * m + ht + 1)
                    nc.scalar.activation(hid[:, par, ht, 0:w], psE[:, ht % 4, 0:w], ACT.Gelu_apprx_tanh,
                                         bias=b1s[:, ht:ht + 1]).then_inc(s_hs, 1)

            with act.Fori(0, FI // 2) as i:
                feed(2 * i, 0)
                feed(2 * i + 1, 1)
            feed(FI - 1, 0, 1)

        @block.vector
        def _(dve):
            v = nc.vector
            link = Chain(dve, s_dve)
            roots = [0]

            def root(t, ahead):
                roots[0] += 1
                ahead.then_inc(s_sq, 1)
                dve.wait_ge(s_sqd, roots[0] + 1)
                link(v.reciprocal(t, t))

            dve.sem_inc(s_add, 4)
            dve.sem_inc(s_z, 2)
            dve.sem_inc(s_yo, 2)
            dve.sem_inc(s_fz, 2)
            dve.sem_inc(s_fo, 2)
            v.memset(X[:, NB - 1, :], 0.0)
            v.memset(raw[:, FULLC, 0:P], PAD_SRC)
            v.memset(raw[:, FULLC, P:2 * P], PAD_DST)
            v.memset(raw[:, FULLC, 2 * P:3 * P], 0).then_inc(s_pad, 1)
            link(v.memset(rel_sb[:, :, D:W], 0.0))

            dve.wait_ge(s_w, 16 * (3 + 32 + 8))
            for m in (1, 2):
                for bo, bi in ((0, 3), (1, 2), (2, 3)):
                    p0 = 64 * (bo % 2)
                    a = wraw[p0:p0 + 64, m, bo // 2, 64 * bi:64 * bi + 64]
                    ins = v.tensor_scalar(a, a, -1.0, None, ALU.mult)
            ins.then_inc(s_kneg, 1)

            dve.wait_ge(s_gw, 16 * 3)
            q = R // 4
            for k in range(4):
                link(v.tensor_tensor(gprod[0:q, :].rearrange("p (b c) -> p b c", b=4),
                                     rel_sb[0:q, k, 0:D].rearrange("p (b c) -> p b c", b=4),
                                     gw[0:q, :].rearrange("p (c b) -> p b c", b=4), ALU.mult))
                ins = v.tensor_reduce(glog[0:q, k:k + 1], gprod[0:q, :], AX, ALU.add)
                if k < 3:
                    link(ins)
            ins.then_inc(s_sq, 1)
            dve.wait_ge(s_sqd, 1)
            for k in range(4):
                v.tensor_scalar(rel_sb[0:q, k, 0:D], rel_sb[0:q, k, 0:D], glog[0:q, k:k + 1], None, ALU.mult)
                ins = v.tensor_copy(rel_sb[0:q, k, D:DW], glog[0:q, k:k + 1])
            ins.then_inc(s_gr, 1)

            dve.wait_ge(s_wt, 1)
            v.tensor_copy(wt[:, :, :, :].rearrange("p m t i -> p m (t i)"), psE[:, 0:3, :]).then_inc(s_wc, 1)

            def moments():
                link(v.tensor_tensor(sm0[:, :], st[:, :, 1], st[:, :, 4], ALU.add))
                link(v.tensor_scalar(mean[:, :], sm0[:, :], 0.5, None, ALU.mult))
                link(v.tensor_tensor(sm0[:, :], st[:, :, 1], st[:, :, 4], ALU.subtract))
                link(v.tensor_tensor(sm0[:, :], sm0[:, :], sm0[:, :], ALU.mult))
                link(v.tensor_tensor(sm1[:, :], st[:, :, 2], st[:, :, 5], ALU.add))
                link(v.tensor_scalar(sm1[:, :], sm1[:, :], 1.0 / D, EPS, ALU.mult, ALU.add))
                root(rstd[:, :], v.scalar_tensor_tensor(rstd[:, :], sm0[:, :], 0.25, sm1[:, :], ALU.mult, ALU.add))

            def normed(out, b):
                return v.tensor_scalar(out, X[:, b, :], mean[:, bass.ds(b, 1)], rstd[:, bass.ds(b, 1)],
                                       ALU.subtract, ALU.mult)

            dve.wait_ge(s_x, 32)
            with dve.Fori(0, NB - 1) as b:
                v.bn_stats(st[:, b, :], X[:, b, :])
            link(v.bn_stats(st[:, NB - 1, :], X[:, NB - 1, :]))

            dve.wait_ge(s_const, 9)
            dve.wait_ge(s_raw, 16 * 9)
            link(v.tensor_scalar(lo_i, raw[:, :, 0:P], P - 1, None, ALU.bitwise_and))
            link(v.tensor_scalar(hi_i, raw[:, :, 0:P], 7, None, ALU.logical_shift_right))
            v.tensor_copy(hlo, typi[:, :])
            link(v.tensor_copy(hhi, dstf[:, :].bitcast(I32)))
            with dve.Fori(0, SLOTS // HG) as i:
                dve.wait_ge(s_hmm, i + 1)
                v.tensor_tensor(ohlo[:, i & 1, :, :], hlo[:, bass.ds(HG * i, HG)].unsqueeze(2).broadcast_to([P, HG, P]),
                                iob[:, :].unsqueeze(1).broadcast_to([P, HG, P]), ALU.is_equal).then_inc(s_oh, 1)
                v.tensor_tensor(ohhi[:, i & 1, :, :], hhi[:, bass.ds(HG * i, HG)].unsqueeze(2).broadcast_to([P, HG, NB]),
                                iob[:, 0:NB].unsqueeze(1).broadcast_to([P, HG, NB]), ALU.is_equal).then_inc(s_oh, 1)

            v.tensor_copy(last[:, :], raw[:, :, 2 * P - 1])
            link(v.tensor_scalar(b128[:, :], iof[:, 0:NB], float(P), None, ALU.mult))
            link(v.tensor_tensor(cmp1[:, :, :], last[:, :].unsqueeze(1).broadcast_to([P, NB, SC]),
                                 b128[:, :].unsqueeze(2).broadcast_to([P, NB, SC]), ALU.is_lt))
            v.tensor_reduce(cnt[:, :], cmp1[:, :, :], AX, ALU.add).then_inc(s_cnt, 1)
            dve.wait_ge(s_lo, 1)
            link(v.tensor_tensor(sbs[:, :], psY[:, 1, 0:NB], iof[:, 0:NB], ALU.add))
            link(v.tensor_tensor(cmp2[:, :, :], sbs[:, 1:NB].unsqueeze(1).broadcast_to([P, SC, NB - 1]),
                                 pidx[:, :].unsqueeze(2).broadcast_to([P, SC, NB - 1]), ALU.is_le))
            link(v.tensor_reduce(bp[:, :], cmp2[:, :, :], AX, ALU.add))
            link(v.tensor_tensor(tpf[:, :], pidx[:, :], bp[:, :], ALU.subtract))
            v.tensor_scalar(bp128[:, :], bp[:, :], float(P), None, ALU.mult)
            v.tensor_copy(tpi[:, :], tpf[:, :]).then_inc(s_tp, 1)
            dve.wait_ge(s_bt, 1)
            v.tensor_copy(bti[:, :], psE[0:SC, 3, 0:P]).then_inc(s_bti, 1)
            dve.wait_ge(s_slot, 16 * SC)
            link(v.tensor_copy(slot_f, slot_i))
            v.tensor_tensor(slot_f[:, :, P:2 * P], slot_f[:, :, P:2 * P],
                            bp128[:, :].unsqueeze(2).broadcast_to([P, SC, P]), ALU.subtract).then_inc(s_cv, 1)

            dve.wait_ge(s_hist, 1)
            root(degu[:, :], v.tensor_scalar(degu[:, :], psY[:, 0, 0:NB], 1.0, None, ALU.max))
            moments()

            dve.wait_ge(s_sc, SC + 2)
            dve.wait_ge(s_wc, 1)
            link(v.memset(acc[:, :, D:W], 1.0))
            with dve.Fori(0, NB) as b:
                link.enter(b, 1)
                link(normed(acc[:, b, 0:D], b))
                v.tensor_scalar(acc[:, b, 0:D], acc[:, b, 0:D], degu[:, bass.ds(b, 1)], None, ALU.mult).then_inc(s_trow, 1)
                link.leave(NB)
            dve.wait_ge(s_td, 16 * (NB // 7))
            v.memset(accf[:, :], 0.0).then_inc(s_zero, 1)
            dve.wait_ge(s_zero, 1)
            dve.wait_ge(s_brow, 16)

            def edge_pass(first_item, products):
                with dve.Fori(0, IT) as i:
                    def ahead(k):
                        n = first_item + k + RING * i
                        dve.wait_ge(s_mm, n - 4 + RING + 1)
                        v.tensor_scalar(sel[:, k % 4, :], iof[:, :], dstf[:, bass.ds(RING * i + k, 1)], None,
                                        ALU.is_equal).then_inc(s_sel, 1)
                        if products:
                            dve.wait_ge(s_g[k], 16 * IT + 16 * i + 16)
                            dve.wait_ge(s_r[k], 16 * i + 16)
                            v.tensor_tensor(gath[:, k, 0:DW], gath[:, k, 0:DW], relg[:, k, 0:DW],
                                            ALU.mult).then_inc(s_prod, 1)

                    ahead(0)
                    ahead(1)
                    for k in range(RING):
                        if k + 2 < RING:
                            ahead(k + 2)
                        n = first_item + k + RING * i
                        b = dve.value_load(brow[0:1, bass.ds(RING * i + k, 1)], min_val=0, max_val=NB - 1)
                        dve.wait_ge(s_mm, n + RING + 1)
                        dve.wait_ge(s_add, n + 4)
                        v.tensor_tensor(acc[:, b, 0:DW], acc[:, b, 0:DW], psE[:, k % 4, 0:DW],
                                        ALU.add).then_inc(s_add, 1)

            def item(n, stage):
                return n - stage * NB

            edge_pass(0, False)
            dve.wait_ge(s_add, SLOTS + 4)

            v.tensor_scalar(has[:, :], acc[:, :, D], 0.0, None, ALU.is_gt)
            root(inq[:, :], v.tensor_scalar(inq[:, :], acc[:, :, D], 1.0, None, ALU.max))

            def dense(stage, rows, links_rows, use, links_use):
                first = stage * NB
                per = 2 * (links_rows + links_use)

                def ahead(j, par, gap=1):
                    dve.wait_ge(s_ztp, first + j + gap)
                    rows(par, j)

                def take(j, par):
                    dve.wait_ge(s_y, first + j + 3)
                    use(par, j)

                ahead(0, 0, gap=2)
                with dve.Fori(0, NB // 2) as i:
                    link.enter(i, per)
                    ahead(2 * i + 1, 1)
                    take(2 * i, 0)
                    ahead(2 * i + 2, 0)
                    take(2 * i + 1, 1)
                    link.leave(NB // 2)
                take(NB - 1, 0)

            def rows0(par, b):
                link(normed(tmp[:, par, :], b))
                v.scalar_tensor_tensor(zst[:, par, 0:D], acc[:, b, 0:D], degu[:, bass.ds(b, 1)], tmp[:, par, :],
                                       ALU.mult, ALU.add)
                v.scalar_tensor_tensor(zst[:, par, D:2 * D], acc[:, b, 0:D], degu[:, bass.ds(b, 1)], tmp[:, par, :],
                                       ALU.mult, ALU.mult).then_inc(s_z, 1)

            def use0(par, b):
                link(v.scalar_tensor_tensor(gprod[:, :], psY[:, par, 0:D], has[:, bass.ds(b, 1)], b0s[:, :],
                                            ALU.mult, ALU.add))
                dve.sem_inc(s_yo, 1)
                link(v.scalar_tensor_tensor(acc[:, b, 0:D], gprod[:, :], 0.01, gprod[:, :], ALU.mult, ALU.max))
                link(v.scalar_tensor_tensor(gprod[:, :], acc[:, b, 0:D], 1.0, acc[:, b, 0:D], ALU.mult, ALU.mult,
                                            accum_out=ssq[:, bass.ds(b, 1)]))

            dense(0, rows0, 1, use0, 3)

            roots[0] += 1
            dve.sem_inc(s_sq, 1)
            dve.wait_ge(s_sqd, roots[0] + 1)
            link(v.tensor_scalar(ssq[:, :], ssq[:, :], 1e-12, None, ALU.max))
            link(v.reciprocal(ssq[:, :], ssq[:, :]))
            with dve.Fori(0, NB) as b:
                link.enter(b, 2)
                link(v.scalar_tensor_tensor(X[:, b, :], acc[:, b, 0:D], ssq[:, bass.ds(b, 1)], X[:, b, :],
                                            ALU.mult, ALU.add))
                link(v.bn_stats(st[:, b, :], X[:, b, :]))
                link.leave(NB)
            moments()

            def rows1(par, b):
                normed(zst[:, par, 0:D], b).then_inc(s_z, 1)

            def use1(par, b):
                link(v.tensor_tensor(gprod[:, :], psY[:, par, 0:D], bfs[:, :], ALU.add))
                dve.sem_inc(s_yo, 1)
                link(v.tensor_tensor(X[:, b, :], X[:, b, :], gprod[:, :], ALU.add))
                link(v.bn_stats(st[:, b, :], X[:, b, :]))

            dense(1, rows1, 0, use1, 3)
            moments()

            link(v.tensor_copy(acc[:, :, D], degu[:, :]))
            with dve.Fori(0, NB) as b:
                link.enter(b, 1)
                link(normed(acc[:, b, 0:D], b))
                v.tensor_scalar(acc[:, b, 0:D], acc[:, b, 0:D], degu[:, bass.ds(b, 1)], None, ALU.mult).then_inc(s_trow, 1)
                link.leave(NB)
            dve.wait_ge(s_td, 2 * 16 * (NB // 7))
            v.memset(accf[:, :], 0.0).then_inc(s_zero, 1)
            dve.wait_ge(s_zero, 2)
            edge_pass(SLOTS, True)
            dve.wait_ge(s_add, 2 * SLOTS + 4)

            def rows2(par, b):
                v.tensor_copy(zst[:, par, 0:D], acc[:, b, 0:D]).then_inc(s_z, 1)

            def use2(par, b):
                link(v.scalar_tensor_tensor(gprod[:, :], mbs[:, :], acc[:, b, D:DW], psY[:, par, 0:D], ALU.mult, ALU.add))
                dve.sem_inc(s_yo, 1)
                link(normed(tmp[:, par, :], b))
                link(v.scalar_tensor_tensor(acc[:, b, 0:D], gprod[:, :], inq[:, bass.ds(b, 1)], tmp[:, par, :],
                                            ALU.mult, ALU.add))

            dense(2, rows2, 0, use2, 3)

            def use3(par, b):
                link(v.tensor_tensor(gprod[:, :], psY[:, par, 0:D], ubs[:, :], ALU.add))
                dve.sem_inc(s_yo, 1)
                xb = X[:, b, :].rearrange("p (c a) -> p c a", a=4)
                link(v.tensor_tensor(xb, xb, gprod[:, :].rearrange("p (a c) -> p c a", a=4), ALU.add))
                link(v.bn_stats(st[:, b, :], X[:, b, :]))

            dense(3, rows2, 0, use3, 3)
            moments()

            with dve.Fori(0, NB) as b:
                link.enter(b, 2)
                link(normed(tmp[:, 0, :], b))
                link(v.scalar_tensor_tensor(gprod[:, :], tmp[:, 0, :], 1.0, wrs[:, :], ALU.mult, ALU.mult,
                                            accum_out=score[:, bass.ds(b, 1)]))
                link.leave(NB)
            link(v.tensor_scalar(valid[:, :], valid[:, :], float(N), None, ALU.is_lt))
            link(v.tensor_scalar(score[:, :], score[:, :], brs[:, :], None, ALU.add))
            v.memset(trial[:, :], 1)
            v.memset(found[:, :], 0)
            link(v.memset(thr[:, :], 0.0))
            link(v.tensor_tensor(bit[:, :], trial[:, :].broadcast_to([P, BITS]), shift[:, :], ALU.logical_shift_left))
            link(v.tensor_copy(bitf[:, :], bit[:, :]))

            v.scalar_tensor_tensor(flag[:, :], score[:, :], thr[:, :], valid[:, :], ALU.is_ge, ALU.mult,
                                   accum_out=hits[:, :]).then_inc(s_hits, 1)
            dve.wait_ge(s_total, 1)
            link(v.tensor_scalar(need[:, :], psE[:, 0, 0:1], float(TOP), None, ALU.is_ge))
            v.tensor_scalar(sign[:, :], need[:, :], 2.0, -1.0, ALU.mult, ALU.add)
            link(v.tensor_scalar(want[:, :], need[:, :], float(2 * TOP - N - 1), float(N - TOP + 1), ALU.mult, ALU.add))
            link(v.tensor_scalar(keyed[:, :], score[:, :], sign[:, :], None, ALU.mult))
            with dve.Fori(0, BITS) as i:
                link.enter(i, 3)
                link(v.tensor_tensor(trial[:, :], found[:, :], bit[:, bass.ds(i, 1)], ALU.bitwise_or))
                v.scalar_tensor_tensor(flag[:, :], keyed[:, :], trial[:, :].bitcast(F32), valid[:, :], ALU.is_ge, ALU.mult,
                                       accum_out=hits[:, :]).then_inc(s_hits, 1)
                dve.wait_ge(s_total, i + 2)
                link(v.scalar_tensor_tensor(step[:, :], psE[:, 0, 0:1], want[:, :], bitf[:, bass.ds(i, 1)],
                                            ALU.is_ge, ALU.mult))
                link(v.tensor_tensor(found[:, :], found[:, :], step[:, :], ALU.bitwise_or))
                link.leave(BITS)
            link(v.tensor_tensor(thr[:, :], found[:, :].bitcast(F32), sign[:, :], ALU.mult))
            v.scalar_tensor_tensor(pick[:, :], score[:, :], thr[:, :], valid[:, :], ALU.is_gt, ALU.mult,
                                   accum_out=hits[:, :]).then_inc(s_hits, 1)
            dve.wait_ge(s_total, BITS + 2)
            v.tensor_scalar(need[:, :], psE[:, 0, 0:1], -1.0, float(TOP), ALU.mult, ALU.add)
            v.scalar_tensor_tensor(tie[:, :], score[:, :], thr[:, :], valid[:, :], ALU.is_equal, ALU.mult).then_inc(s_hits, 1)
            dve.wait_ge(s_total, BITS + 3)
            link(v.tensor_copy(sm0[:, :], psE[:, 2, 0:NB]))
            link(v.tensor_tensor_scan(sm1[:, :], ones[:, 0:NB], sm0[:, :], 0.0, ALU.mult, ALU.add))
            link(v.tensor_tensor(sm1[:, :], sm1[:, :], sm0[:, :], ALU.subtract))
            link(v.tensor_tensor(sm1[:, :], sm1[:, :], psE[:, 1, 0:NB], ALU.add))
            link(v.scalar_tensor_tensor(sm1[:, :], sm1[:, :], need[:, :], tie[:, :], ALU.is_lt, ALU.mult))
            link(v.tensor_tensor(pick[:, :], pick[:, :], sm1[:, :], ALU.add))
            link(v.tensor_tensor(pick[:, :], pick[:, :], score[:, :], ALU.mult))

            def rows(m, par, blocks=2):
                dve.wait_ge(s_ftp, m + 1)
                for q in range(blocks):
                    ins = normed(zst[:, par, q * D:(q + 1) * D], 2 * m + q)
                ins.then_inc(s_fz, 1)

            def finish(m, blocks=2):
                for q in range(blocks):
                    b = 2 * m + q
                    dve.wait_ge(s_fy, b + 3)
                    v.tensor_tensor(gprod[:, :], psY[:, q, 0:D], b2s[:, :], ALU.add)
                    link(normed(tmp[:, q, :], b))
                    link(v.scalar_tensor_tensor(gprod[:, :], gprod[:, :], pick[:, bass.ds(b, 1)], X[:, b, :],
                                                ALU.mult, ALU.add))
                    v.tensor_tensor(acc[:, b, 0:D], gprod[:, :], tmp[:, q, :], ALU.add).then_inc(s_fo, 1)
                    dve.wait_ge(s_fo, b + 3)

            rows(0, 0)
            with dve.Fori(0, FI // 2 - 1) as i:
                link.enter(i, 8)
                rows(2 * i + 1, 1)
                finish(2 * i)
                rows(2 * i + 2, 0)
                finish(2 * i + 1)
                link.leave(FI // 2 - 1)
            rows(FI - 2, 1)
            finish(FI - 3)
            rows(FI - 1, 0, 1)
            finish(FI - 2)
            finish(FI - 1, 1)


_INS = ['x', 'src', 'dst', 'edge_type_500', 'L0_gnn_W1', 'L0_gnn_W2', 'L0_gnn_b', 'L0_ffn_weight', 'L0_ffn_bias',
        'L1_gnn_relation_emb', 'L1_gnn_msg_w', 'L1_gnn_msg_b', 'L1_gnn_upd_w', 'L1_gnn_upd_b', 'L1_gnn_gate_w',
        'L1_gnn_gate_b', 'L1_ffn_wr', 'L1_ffn_br', 'L1_ffn_w1', 'L1_ffn_b1', 'L1_ffn_w2', 'L1_ffn_b2']


def kernel(**inputs):
    import numpy as _np
    import concourse.bacc as _bacc
    from concourse.bass_utils import run_bass_kernel_spmd as _run

    nc = _bacc.Bacc("TRN2", target_bir_lowering=False, num_devices=1)
    arrays, args = {}, []
    for name in _INS:
        a = _np.ascontiguousarray(inputs[name])
        arrays[f"in_{name}"] = a
        args.append(nc.dram_tensor(f"in_{name}", a.shape, mybir.dt.from_np(a.dtype), kind="ExternalInput").ap())
    args.append(nc.dram_tensor("out_0", (N, D), F32, kind="ExternalOutput").ap())
    program(nc, *args)
    r = _run(nc, [arrays], core_ids=[0])
    return r.results[0]["out_0"]
```

```python
import concourse.bass as bass
from concourse import mybir
from contextlib import ExitStack

F32 = mybir.dt.float32
BF16 = mybir.dt.bfloat16
F16 = mybir.dt.float16
I32 = mybir.dt.int32
ALU = mybir.AluOpType
ACT = mybir.ActivationFunctionType
AX = mybir.AxisListType.X

P = 128
N = 6250
D = 256
E = 206250
R = 500
H = 1024
NB = -(-N // P)
TAIL = N - (NB - 1) * P
TILES = -(-E // P)
SC = -(-(TILES + NB) // P)
SLOTS = SC * P
FULLC = E // (P * P)
RESTT = (E - FULLC * P * P) // P
RESTE = E - FULLC * P * P - RESTT * P
W = 260
DW = D + 1
PAD_SRC = NB * P - 1
PAD_DST = 1 << 13
HT = H // P
FI = NB // 2 + 1
RING = 16
LEAD = 2
RK = 4
RP = R // RK
REL = RING // 2
HALF = REL // 2
IT = SLOTS // RING
HG = 16
TOP = N // 2 - 1
BITS = 31
EPS = 1e-5


class Chain:

    def __init__(self, eng, sem):
        self.eng, self.sem, self.base, self.n = eng, sem, 0, 0

    def __call__(self, ins):
        self.n += 1
        ins.then_inc(self.sem, 1)
        self.eng.wait_ge(self.sem, self.base + self.n)

    def enter(self, step, per):
        self.start, self.per = (self.base, self.n), per
        self.base, self.n = self.start[0] + self.start[1] + step * per, 0

    def leave(self, steps):
        assert self.n == self.per, (self.n, self.per)
        self.base, self.n = self.start[0] + self.start[1] + steps * self.per, 0


def program(nc, x, src, dst, etype, w1_0, w2_0, b_0, wf, bf, rel, msg_w, msg_b, upd_w, upd_b,
            gate_w, gate_b, wr, br, w1, b1, w2, b2, out):
    ctx = ExitStack()
    with ctx:
        def sb(name, shape, dt=F32):
            return ctx.enter_context(nc.sbuf_tensor(name, shape, dt))

        def sem(name):
            return ctx.enter_context(nc.semaphore(name))

        edges_d = nc.dram_tensor("edges_d", (SLOTS, 3 * P), I32).ap()
        t1_d = nc.dram_tensor("t1_d", (NB * P, W), F32).ap()
        t2_d = nc.dram_tensor("t2_d", (NB * P, W), F32).ap()
        types_d = nc.dram_tensor("types_d", (SLOTS, P), F16).ap()
        rel_d = nc.dram_tensor("rel_d", (2 * IT, P, HALF * DW), F32).ap()

        X = sb("X", [P, NB, D])
        accf = sb("accf", [P, NB * W])
        work = sb("work", [P, RING * W + REL * DW + RING * P // 2 + RK * REL * P // 2])
        srci = sb("srci", [P, SLOTS + RING], I32)
        dstf = sb("dstf", [P, SLOTS])
        brow = sb("brow", [1, SLOTS], I32)
        idxs = sb("idxs", [P, RING], I32)
        sel = sb("sel", [P, 4, P])
        acc = accf[:, :].rearrange("p (b w) -> p b w", w=W)
        gath = work[:, 0:RING * W].rearrange("p (k w) -> p k w", w=W)
        o = RING * W
        relg = work[:, o:o + REL * DW].rearrange("p (h k w) -> p h k w", h=2, w=DW)
        o += REL * DW
        types = work[:, o:o + RING * P // 2].bitcast(F16).rearrange("p (h j r e) -> p h r j e", h=2, r=2, e=P)
        types_w = work[:, o:o + RING * P // 2].bitcast(F16).rearrange("p (h n) -> p h n", h=2)
        o += RING * P // 2
        oht = work[:, o:o + RK * REL * P // 2].bitcast(BF16).rearrange("p (h t j e) -> p h t j e", h=2, t=RK, e=P)
        raw = work[:, 0:SC * 384].bitcast(I32).rearrange("p (c w) -> p c w", w=384)
        o = SC * 384
        ohlo = work[:, o:o + HG * P].bitcast(BF16).rearrange("p (r t l) -> p r t l", r=2, l=P)
        o += HG * P
        ohhi = work[:, o:o + HG * NB].bitcast(BF16).rearrange("p (r t l) -> p r t l", r=2, l=NB)
        slot_i = accf[:, 0:SC * 384].bitcast(I32).rearrange("p (c w) -> p c w", w=384)
        slot_f = accf[:, SC * 384:2 * SC * 384].rearrange("p (c w) -> p c w", w=384)
        o = 2 * SC * 384
        wraw = accf[:, o:o + 3 * 2 * D].rearrange("p (m t i) -> p m t i", m=3, t=2)
        o += 3 * 2 * D
        rel_sb = accf[:, o:o + RK * DW].rearrange("p (k w) -> p k w", w=DW)
        types_h = slot_f[:, :, 0:P].bitcast(F16)[:, :, 0:P]
        hlo = srci[:, :].bitcast(BF16)[:, 0:SLOTS]
        hhi = srci[:, :].bitcast(BF16)[:, SLOTS:2 * SLOTS]
        lo_i = slot_f[:, :, 0:P].bitcast(I32)
        hi_i = dstf[:, :].bitcast(I32).rearrange("p (c e) -> p c e", e=P)
        o = 2 * H
        f1 = work[:, 0:o].rearrange("p (t n) -> p t n", t=2)
        f2 = work[:, o:o + HT * D].rearrange("p (t n) -> p t n", t=HT)
        o += HT * D
        hid = work[:, o:o + 2 * HT * 2 * P].rearrange("p (r t n) -> p r t n", r=2, t=HT)
        relb = sb("relb", [P, 3, RK, DW + 1], BF16)
        tid = sb("tid", [P, RK])
        gw = sb("gw", [P, D])
        gprod = sb("gprod", [P, D])
        gb = sb("gb", [P, 1])
        glog = sb("glog", [P, RK])

        ident = sb("ident", [P, P])
        ones = sb("ones", [P, P])
        iof = sb("iof", [P, P])
        iob = sb("iob", [P, P], BF16)
        zb = sb("zb", [P, P], BF16)
        pidx = sb("pidx", [P, SC])
        w1s = sb("w1s", [P, 2, D])
        w2s = sb("w2s", [P, 2, D])
        wt = sb("wt", [P, 3, 2, D])
        b0s = sb("b0s", [P, D])
        bfs = sb("bfs", [P, D])
        mbs = sb("mbs", [P, D])
        ubs = sb("ubs", [P, D])
        zst = sb("zst", [P, 2, 2 * D])
        zts = sb("zts", [P, 2, 2 * D])
        tmp = sb("tmp", [P, 2, D])
        st = sb("st", [P, NB, 6])
        mean = sb("mean", [P, NB])
        rstd = sb("rstd", [P, NB])
        sm0 = sb("sm0", [P, NB])
        sm1 = sb("sm1", [P, NB])
        deg = sb("deg", [P, NB])
        degu = sb("degu", [P, NB])
        has = sb("has", [P, NB])
        inq = sb("inq", [P, NB])
        ssq = sb("ssq", [P, NB])
        b128 = sb("b128", [P, NB])
        cmp1 = zst[:, :, :].rearrange("p r d -> p (r d)")[:, 0:NB * SC].rearrange("p (b c) -> p b c", c=SC)
        cmp2 = zts[:, :, :].rearrange("p r d -> p (r d)")[:, 0:SC * (NB - 1)].rearrange("p (c b) -> p c b", b=NB - 1)
        last = sb("last", [P, SC])
        cnt = sb("cnt", [P, NB])
        sbs = sb("sbs", [P, NB])
        bp = sb("bp", [P, SC])
        bp128 = sb("bp128", [P, SC])
        tpf = sb("tpf", [P, SC])
        tpi = sb("tpi", [P, SC], I32)
        bti = sb("bti", [SC, P], I32)
        wrs = sb("wrs", [P, D])
        brs = sb("brs", [P, 1])
        b1s = sb("b1s", [P, HT])
        b2s = sb("b2s", [P, D])
        tri = sb("tri", [P, P])
        valid = sb("valid", [P, NB])
        score = sb("score", [P, NB])
        keyed = sb("keyed", [P, NB])
        flag = sb("flag", [P, NB])
        tie = sb("tie", [P, NB])
        pick = sb("pick", [P, NB])
        shift = sb("shift", [P, BITS], I32)
        bit = sb("bit", [P, BITS], I32)
        bitf = sb("bitf", [P, BITS])
        found = sb("found", [P, 1], I32)
        trial = sb("trial", [P, 1], I32)
        step = sb("step", [P, 1], I32)
        hits = sb("hits", [P, 1])
        sign = sb("sign", [P, 1])
        want = sb("want", [P, 1])
        thr = sb("thr", [P, 1])
        need = sb("need", [P, 1])

        def bank(name):
            return ctx.enter_context(nc.psum_tensor(name, [P, 512], F32))

        psE = ctx.enter_context(nc.psum_tensor("psE", [P, 4, 512], F32))
        psT = ctx.enter_context(nc.psum_tensor("psT", [P, 2, 512], F32))
        psY = ctx.enter_context(nc.psum_tensor("psY", [P, 2, 512], F32))

        psR = [psT[:, 0, :], psT[:, 1, :], psY[:, 0, :], psY[:, 1, :]]

        s_const = sem("s_const")
        s_pool = sem("s_pool")
        s_dve = sem("s_dve")
        s_pad = sem("s_pad")
        s_x = sem("s_x")
        s_raw = sem("s_raw")
        s_w = sem("s_w")
        s_gw = sem("s_gw")
        s_ed = sem("s_ed")
        s_oh = sem("s_oh")
        s_hmm = sem("s_hmm")
        s_hist = sem("s_hist")
        s_cnt = sem("s_cnt")
        s_lo = sem("s_lo")
        s_tp = sem("s_tp")
        s_bt = sem("s_bt")
        s_bti = sem("s_bti")
        s_brow = sem("s_brow")
        s_slot = sem("s_slot")
        s_cv = sem("s_cv")
        s_st = sem("s_st")
        s_sc = sem("s_sc")
        s_kneg = sem("s_kneg")
        s_wt = sem("s_wt")
        s_wc = sem("s_wc")
        s_sq = sem("s_sq")
        s_sqd = sem("s_sqd")
        s_typ = sem("s_typ")
        s_typd = sem("s_typd")
        s_tb = [sem(f"s_tb{h}") for h in range(2)]
        s_oht = sem("s_oht")
        s_rel = sem("s_rel")
        s_relc = sem("s_relc")
        s_rst = [sem(f"s_rst{h}") for h in range(2)]
        s_rfree = sem("s_rfree")
        s_rl = [sem(f"s_rl{h}") for h in range(2)]
        s_trow = sem("s_trow")
        s_td = sem("s_td")
        s_zero = sem("s_zero")
        s_turn = sem("s_turn")
        s_idx = sem("s_idx")
        s_g = [sem(f"s_g{k}") for k in range(RING)]
        s_sel = sem("s_sel")
        s_prod = sem("s_prod")
        s_mm = sem("s_mm")
        s_add = sem("s_add")
        s_z = sem("s_z")
        s_ztp = sem("s_ztp")
        s_zts = sem("s_zts")
        s_y = sem("s_y")
        s_yo = sem("s_yo")
        s_fw = sem("s_fw")
        s_hits = sem("s_hits")
        s_total = sem("s_total")
        s_fz = sem("s_fz")
        s_ftp = sem("s_ftp")
        s_fts = sem("s_fts")
        s_hp = sem("s_hp")
        s_hs = sem("s_hs")
        s_fy = sem("s_fy")
        s_fo = sem("s_fo")
        s_out = sem("s_out")
        STAGES = 4

        block = ctx.enter_context(nc.Block())

        src_t = edges_d.rearrange("(c p) w -> p c w", p=P)

        @block.sync
        def _(sp):
            sp.sem_inc(s_rfree, 2)
            sp.dma_start(X[:, 0:NB - 1, :], x[0:(NB - 1) * P, :].rearrange("(b p) d -> p b d", p=P)).then_inc(s_x, 16)
            sp.wait_ge(s_pad, 1)
            sp.dma_start(X[0:TAIL, NB - 1, :], x[(NB - 1) * P:N, :]).then_inc(s_x, 16)
            for n, a in enumerate((src, dst, etype)):
                c0, c1 = n * P, (n + 1) * P
                sp.dma_start(raw[:, 0:FULLC, c0:c1],
                             a[0:FULLC * P * P].rearrange("(c p e) -> p c e", p=P, e=P)).then_inc(s_raw, 16)
                e0 = FULLC * P * P
                sp.dma_start(raw[0:RESTT, FULLC, c0:c1],
                             a[e0:e0 + RESTT * P].rearrange("(p e) -> p e", e=P)).then_inc(s_raw, 16)
                sp.dma_start(raw[RESTT:RESTT + 1, FULLC, c0:c0 + RESTE],
                             a[e0 + RESTT * P:E].rearrange("(p e) -> p e", p=1)).then_inc(s_raw, 16)
            sp.dma_start(w1s[:, :, :], w1_0.rearrange("(t p) n -> p t n", p=P)).then_inc(s_w, 16)
            sp.dma_start(w2s[:, :, :], w2_0.rearrange("(t p) n -> p t n", p=P)).then_inc(s_w, 16)
            sp.dma_start(wraw[:, 0, :, :], wf.rearrange("(t p) n -> p t n", p=P)).then_inc(s_w, 16)
            for m, a in ((1, msg_w), (2, upd_w)):
                for bo in range(4):
                    for bi in range(4):
                        p0 = 64 * (bo % 2)
                        sp.dma_start(wraw[p0:p0 + 64, m, bo // 2, 64 * bi:64 * bi + 64], a[bo ^ bi, :, :]).then_inc(s_w, 16)
            for t, a in ((b0s, b_0), (bfs, bf)):
                sp.dma_start(t[:, :], a.rearrange("(o d) -> o d", o=1).broadcast_to([P, D])).then_inc(s_w, 16)
            sp.dma_start(b2s[:, :], b2.rearrange("(o d) -> o d", o=1).broadcast_to([P, D])).then_inc(s_w, 16)
            sp.dma_start(wrs[:, :], wr.rearrange("d o -> o d").broadcast_to([P, D])).then_inc(s_w, 16)
            sp.dma_start(brs[:, :], br.rearrange("(o d) -> o d", o=1).broadcast_to([P, 1])).then_inc(s_w, 16)
            sp.dma_start(b1s[:, :], b1.rearrange("(t p) -> p t", p=P), allow_slow_non_contiguous=True).then_inc(s_w, 16)
            for t, a in ((mbs, msg_b), (ubs, upd_b)):
                sp.dma_start(t[:, :], a.rearrange("(o a) c -> o (a c)", o=1).broadcast_to([P, D])).then_inc(s_w, 16)
            sp.dma_start(rel_sb[0:RP, :, 0:D], rel.rearrange("(k p) d -> p k d", k=4)).then_inc(s_gw, 16)
            sp.dma_start(gw[:, :], gate_w.broadcast_to([P, D])).then_inc(s_gw, 16)
            sp.dma_start(gb[:, :], gate_b.rearrange("(o d) -> o d", o=1).broadcast_to([P, 1])).then_inc(s_gw, 16)
            sp.wait_ge(s_raw, 16 * 9)
            sp.dma_start(src_t, raw[:, :, :]).then_inc(s_ed, 16)
            sp.wait_ge(s_bti, 1)
            sp.dma_start(brow[0:1, :].rearrange("o (c p) -> o c p", p=P), bti[:, :]).then_inc(s_brow, 16)
            sp.wait_ge(s_typ, 1)
            sp.dma_start(types_d[0:SLOTS, :].rearrange("(c p) e -> p c e", p=P), types_h).then_inc(s_typd, 16)

            def table(layer, dram):
                for c in range(NB // 7):
                    sp.wait_ge(s_trow, layer * NB + 7 * (c + 1))
                    sp.dma_start(dram.rearrange("(b p) w -> p b w", p=P)[:, 7 * c:7 * c + 7, :],
                                 acc[:, 7 * c:7 * c + 7, :]).then_inc(s_td, 16)

            def load_types(p, i, h):
                sp.wait_ge(s_oht, p * 2 * IT + 2 * i + h + 1)
                sp.dma_start(types_w[0:RP, h, :], types_d[bass.ds(RING * i + REL * h, REL), :].rearrange(
                    "(o s) e -> o (s e)", o=1).broadcast_to([RP, REL * P])).then_inc(s_tb[h], 16)

            def store_rows(i, h):
                sp.wait_ge(s_relc, 4 + REL * i + HALF * h + HALF)
                sp.dma_start(rel_d[bass.ds(2 * i + h, 1), :, :].rearrange("o p w -> (o p) w"),
                             relg[:, h, :, :].rearrange("p k w -> p (k w)")).then_inc(s_rst[h], 16)

            def stored(i, h):
                sp.wait_ge(s_rst[h], 16 * i + 16)
                sp.sem_inc(s_rfree, 1)

            def load_rows(i, h):
                sp.wait_ge(s_prod, RING * i + REL * h)
                sp.dma_start(relg[:, h, :, :].rearrange("p k w -> p (k w)"),
                             rel_d[bass.ds(2 * i + h, 1), :, :].rearrange("o p w -> (o p) w")).then_inc(s_rl[h], 16)

            table(0, t1_d)
            sp.wait_ge(s_typd, 16)
            load_types(0, 0, 0)
            load_types(0, 0, 1)
            load_types(0, 1, 0)
            store_rows(0, 0)
            load_types(0, 1, 1)
            stored(0, 0)
            store_rows(0, 1)
            with sp.Fori(1, IT - 1) as i:
                load_types(0, i + 1, 0)
                stored(i - 1, 1)
                store_rows(i, 0)
                load_types(0, i + 1, 1)
                stored(i, 0)
                store_rows(i, 1)
            stored(IT - 2, 1)
            store_rows(IT - 1, 0)
            stored(IT - 1, 0)
            store_rows(IT - 1, 1)
            stored(IT - 1, 1)
            table(1, t2_d)
            load_types(1, 0, 0)
            load_types(1, 0, 1)
            sp.wait_ge(s_add, SLOTS + 4)
            for h in range(2):
                sp.dma_start(relg[:, h, :, :].rearrange("p k w -> p (k w)"), rel_d[h, :, :]).then_inc(s_rl[h], 16)
            with sp.Fori(0, IT - 1) as i:
                load_types(1, i + 1, 0)
                load_rows(i + 1, 0)
                load_types(1, i + 1, 1)
                load_rows(i + 1, 1)
            sp.wait_ge(s_add, 2 * SLOTS + 4)
            sp.wait_ge(s_oht, 2 * 2 * IT + 2)
            sp.dma_start(f1, w1.rearrange("(t p) n -> p t n", p=P)).then_inc(s_fw, 16)
            sp.dma_start(f2, w2.rearrange("(t p) n -> p t n", p=P)).then_inc(s_fw, 16)
            for c in range(NB // 7):
                sp.wait_ge(s_fo, 2 + 7 * (c + 1))
                b0, full = 7 * c, min(7 * c + 7, NB - 1)
                sp.dma_start(out[b0 * P:full * P, :].rearrange("(b p) d -> p b d", p=P), acc[:, b0:full, 0:D]).then_inc(s_out, 16)
            sp.dma_start(out[(NB - 1) * P:N, :], acc[0:TAIL, NB - 1, 0:D]).then_inc(s_out, 16)
            sp.wait_ge(s_out, 16 * (NB // 7 + 1))

        @block.gpsimd
        def _(pool):
            pool.memset(ident[:, :], 0.0).then_inc(s_pool, 1)
            pool.memset(ones[:, :], 1.0).then_inc(s_const, 1)
            pool.iota(iof[:, :], [[1, P]], base=0, channel_multiplier=0, allow_small_or_imprecise_dtypes=True).then_inc(s_const, 1)
            pool.iota(iob[:, :], [[1, P]], base=0, channel_multiplier=0, allow_small_or_imprecise_dtypes=True).then_inc(s_const, 1)
            pool.iota(pidx[:, :], [[P, SC]], base=0, channel_multiplier=1, allow_small_or_imprecise_dtypes=True).then_inc(s_const, 1)
            pool.memset(zb[:, :], 0.0).then_inc(s_const, 1)
            pool.memset(tri[:, :], 1.0).then_inc(s_pool, 1)
            pool.iota(valid[:, :], [[P, NB]], base=0, channel_multiplier=1, allow_small_or_imprecise_dtypes=True).then_inc(s_const, 1)
            pool.iota(shift[:, :], [[-1, BITS]], base=BITS - 1, channel_multiplier=0).then_inc(s_const, 1)
            pool.iota(tid[:, :], [[RP, RK]], base=0, channel_multiplier=1, allow_small_or_imprecise_dtypes=True).then_inc(s_const, 1)
            pool.wait_ge(s_pool, 2)
            pool.affine_select(out=tri[:, :], in_=tri[:, :], compare_op=ALU.is_gt, fill=0.0, base=0,
                               pattern=[[1, P]], channel_multiplier=-1).then_inc(s_const, 1)
            pool.affine_select(out=ident[:, :], in_=ident[:, :], compare_op=ALU.not_equal, fill=1.0, base=0,
                               pattern=[[-1, P]], channel_multiplier=1).then_inc(s_const, 1)
            pool.wait_ge(s_ed, 16)
            pool.wait_ge(s_tp, 1)
            for c in range(SC):
                pool.indirect_dma_start(slot_i[:, c, :], None, edges_d,
                                        bass.IndirectOffsetOnAxis(ap=tpi[:, c:c + 1], axis=0)).then_inc(s_slot, 16)

            def gathers(i, layer, table):
                first = layer * SLOTS
                for k in range(RING):
                    if k % 8 == 0:
                        pool.wait_ge(s_idx, layer * (2 * IT + 2) + k // 8 + 1 + 2 * i)
                    pool.wait_ge(s_mm, first + k + 1 + RING * i)
                    pool.sem_inc(s_turn, 1)
                    pool.wait_ge(s_td, 16 * (NB // 7) * (1 + layer))
                    pool.indirect_dma_start(gath[:, k, :], None, table, bass.IndirectOffsetOnAxis(
                        ap=idxs[:, k:k + 1], axis=0)).then_inc(s_g[k], 16)

            with pool.Fori(0, IT) as i:
                gathers(i, 0, t1_d)
            with pool.Fori(0, IT) as i:
                gathers(i, 1, t2_d)

        @block.tensor
        def _(pe):
            pe.sem_inc(s_hmm, 2)
            pe.sem_inc(s_st, 2)
            pe.sem_inc(s_mm, RING)
            pe.sem_inc(s_rel, REL)
            pe.sem_inc(s_ztp, 2)
            pe.sem_inc(s_y, 2)
            pe.sem_inc(s_ftp, 2)
            pe.sem_inc(s_fy, 2)
            pe.wait_ge(s_const, 10)
            pe.wait_ge(s_kneg, 1)
            for m in range(3):
                for it in range(2):
                    for ot in range(2):
                        ins = nc.tensor.transpose(psE[:, m, it * D + ot * P:it * D + ot * P + P],
                                                  wraw[:, m, ot, it * P:it * P + P], ident[:, :])
            ins.then_inc(s_wt, 1)
            nc.tensor.matmul(psY[:, 0, 0:NB], zb[:, :], zb[:, 0:NB], start=True, stop=False)
            with pe.Fori(0, SLOTS // HG) as i:
                pe.wait_ge(s_oh, 2 * i + 2)
                for t in range(HG):
                    ins = nc.tensor.matmul(psY[:, 0, 0:NB], ohlo[:, i & 1, t, :], ohhi[:, i & 1, t, :],
                                           start=False, stop=False)
                ins.then_inc(s_hmm, 1)
            nc.tensor.matmul(psY[:, 0, 0:NB], zb[:, :], zb[:, 0:NB], start=False, stop=True).then_inc(s_hist, 1)
            pe.wait_ge(s_cnt, 1)
            nc.tensor.matmul(psY[:, 1, 0:NB], ones[:, :], cnt[:, :], start=True, stop=True).then_inc(s_lo, 1)
            pe.wait_ge(s_tp, 1)
            nc.tensor.transpose(psE[0:SC, 3, 0:P], bp[:, :], ident[:, :]).then_inc(s_bt, 1)
            pe.wait_ge(s_cv, 1)
            for c in range(SC):
                pe.wait_ge(s_sc, c + 1)
                for n in range(2):
                    ins = nc.tensor.transpose(psT[:, c % 2, n * P:n * P + P], slot_f[:, c, (n + 1) * P:(n + 2) * P], ident[:, :])
                ins.then_inc(s_st, 1)

            def relation(layer, i, j):
                m = REL * i + j
                if j % HALF == 0:
                    pe.wait_ge(s_oht, 2 + layer * 2 * IT + 2 * i + j // HALF + 1)
                if layer == 0:
                    pe.wait_ge(s_relc, m + 1)
                else:
                    pe.wait_ge(s_prod, RING * i + 2 * j + 2)
                for t in range(RK):
                    for part in range(3):
                        ins = nc.tensor.matmul(psR[j % 4][:, 0:DW], oht[0:RP, j // HALF, t, j % HALF, :],
                                               relb[0:RP, part, t, 0:DW], start=(t == part == 0),
                                               stop=(t == RK - 1 and part == 2))
                ins.then_inc(s_rel, 1)

            def edge_pass(layer):
                def iteration(i, last=False):
                    for k in range(RING):
                        n = layer * SLOTS + k + RING * i
                        if layer == 1 and k % 2 == 0 and k < RING - 2:
                            relation(1, i, k // 2 + 1)
                        elif layer == 1 and k == RING - 2 and not last:
                            relation(1, i + 1, 0)
                        pe.wait_ge(s_sel, n + 1)
                        if layer == 1:
                            pe.wait_ge(s_prod, 8 + RING * i + k + 1)
                        else:
                            pe.wait_ge(s_g[k], 16 * i + 16)
                        pe.wait_ge(s_add, n + 1)
                        nc.tensor.matmul(psE[:, k % 4, 0:DW], sel[:, k % 4, :], gath[:, k, 0:DW],
                                         start=True, stop=True).then_inc(s_mm, 1)
                        if layer == 0 and k % 2 == 0:
                            relation(0, i, k // 2)

                if layer == 1:
                    relation(1, 0, 0)
                with pe.Fori(0, IT - 1) as i:
                    iteration(i)
                iteration(IT - 1, last=True)

            def dense(stage, nk, weights):
                first = stage * NB

                def turn(n, par, gap=1):
                    pe.wait_ge(s_z, n + 3)
                    pe.wait_ge(s_zts, n + gap)
                    for t in range(nk):
                        ins = nc.tensor.transpose(psT[:, par, t * P:t * P + P], zst[:, par, t * P:t * P + P], ident[:, :])
                    ins.then_inc(s_ztp, 1)

                def product(n, par, gap=1):
                    pe.wait_ge(s_zts, n + 3)
                    pe.wait_ge(s_yo, n + gap)
                    for t in range(nk):
                        ins = nc.tensor.matmul(psY[:, par, 0:D], zts[:, par, t * P:t * P + P], weights(t),
                                               start=(t == 0), stop=(t == nk - 1))
                    ins.then_inc(s_y, 1)

                turn(first, 0, gap=2)
                turn(first + 1, 1)
                product(first, 0, gap=2)
                with pe.Fori(0, NB // 2 - 1) as i:
                    n = first + 1 + 2 * i
                    turn(n + 1, 0)
                    product(n, 1)
                    turn(n + 2, 1)
                    product(n + 1, 0)
                turn(first + NB - 1, 0)
                product(first + NB - 2, 1)
                product(first + NB - 1, 0)

            pe.wait_ge(s_sc, SC + 2)
            edge_pass(0)
            pe.wait_ge(s_relc, REL * IT + 4)
            dense(0, 4, lambda t: (w1s if t < 2 else w2s)[:, t % 2, :])
            dense(1, 2, lambda t: wt[:, 0, t, :])
            pe.wait_ge(s_zts, 2 * NB + 2)
            pe.wait_ge(s_yo, 2 * NB + 2)
            edge_pass(1)
            dense(2, 2, lambda t: wt[:, 1, t, :])
            dense(3, 2, lambda t: wt[:, 2, t, :])

            with pe.Fori(0, BITS + 2) as i:
                pe.wait_ge(s_hits, i + 1)
                nc.tensor.matmul(psE[:, 0, 0:1], ones[:, :], hits[:, :], start=True, stop=True).then_inc(s_total, 1)
            pe.wait_ge(s_hits, BITS + 3)
            nc.tensor.matmul(psE[:, 1, 0:NB], tri[:, :], tie[:, :], start=True, stop=True)
            nc.tensor.matmul(psE[:, 2, 0:NB], ones[:, :], tie[:, :], start=True, stop=True).then_inc(s_total, 1)

            def turn(m, par, blocks=2):
                pe.wait_ge(s_fz, m + 3)
                pe.wait_ge(s_fts, m + 1)
                for t in range(2):
                    for q in range(blocks):
                        ins = nc.tensor.transpose(psT[:, par, (2 * t + q) * P:(2 * t + q) * P + P],
                                                  zst[:, par, q * D + t * P:q * D + t * P + P], ident[:, :])
                ins.then_inc(s_ftp, 1)

            def feed(m, par, blocks=2):
                w = blocks * P
                pe.wait_ge(s_fts, m + 3)
                for ht in range(HT):
                    pe.wait_ge(s_hs, HT * m + ht + 1)
                    for t in range(2):
                        ins = nc.tensor.matmul(psE[:, ht % 4, 0:w], f1[:, t, ht * P:ht * P + P],
                                               zts[:, par, 2 * t * P:2 * t * P + w], start=(t == 0), stop=(t == 1))
                    ins.then_inc(s_hp, 1)
                for q in range(blocks):
                    pe.wait_ge(s_fo, 2 * m + q + 1)
                    for ht in range(HT):
                        pe.wait_ge(s_hs, HT * m + ht + 5)
                        ins = nc.tensor.matmul(psY[:, q, 0:D], hid[:, par, ht, q * P:q * P + P], f2[:, ht, :],
                                               start=(ht == 0), stop=(ht == HT - 1))
                    ins.then_inc(s_fy, 1)

            pe.wait_ge(s_fw, 32)
            turn(0, 0)
            with pe.Fori(0, FI // 2 - 1) as i:
                turn(2 * i + 1, 1)
                feed(2 * i, 0)
                turn(2 * i + 2, 0)
                feed(2 * i + 1, 1)
            turn(FI - 2, 1)
            feed(FI - 3, 0)
            turn(FI - 1, 0, 1)
            feed(FI - 2, 1)
            feed(FI - 1, 0, 1)

        @block.scalar
        def _(act):
            act.sem_inc(s_sc, 2)
            act.sem_inc(s_zts, 2)
            act.sem_inc(s_fts, 2)
            act.sem_inc(s_hs, 4)
            act.sem_inc(s_relc, 4)
            act.wait_ge(s_const, 10)
            act.wait_ge(s_sq, 1)
            nc.scalar.activation(glog[0:RP, :], glog[0:RP, :], ACT.Sigmoid, bias=gb[0:RP, :]).then_inc(s_sqd, 1)
            act.wait_ge(s_hist, 1)
            nc.scalar.copy(srci[:, SLOTS:SLOTS + RING], zb[:, 0:RING])
            for c in range(SC):
                act.wait_ge(s_st, c + 3)
                nc.scalar.copy(srci[:, bass.ts(c, P)], psT[:, c % 2, 0:P])
                nc.scalar.copy(dstf[:, bass.ts(c, P)], psT[:, c % 2, P:2 * P]).then_inc(s_sc, 1)
            act.wait_ge(s_sq, 2)
            nc.scalar.activation(degu[:, :], degu[:, :], ACT.Sqrt).then_inc(s_sqd, 1)
            act.wait_ge(s_sq, 3)
            nc.scalar.activation(rstd[:, :], rstd[:, :], ACT.Sqrt).then_inc(s_sqd, 1)

            def edge_pass(layer):
                def indices(i, h):
                    act.wait_ge(s_mm, layer * SLOTS + 8 * h + 8 + RING * i)
                    nc.scalar.copy(idxs[:, 8 * h:8 * h + 8], srci[:, bass.ds(RING * i + 8 * h, 8)]).then_inc(s_idx, 1)

                indices(0, 0)
                indices(0, 1)
                with act.Fori(0, IT) as i:
                    for h in range(2):
                        if layer == 0:
                            act.wait_ge(s_rfree, 2 * i + h + 1)
                            for j in range(HALF):
                                m = REL * i + HALF * h + j
                                act.wait_ge(s_rel, REL + m + 1)
                                nc.scalar.copy(relg[:, h, j, :], psR[j][:, 0:DW]).then_inc(s_relc, 1)
                        indices(i + 1, h)

            def dense(stage, nk):
                def copy(n, par, gap=1):
                    act.wait_ge(s_ztp, n + 3)
                    act.wait_ge(s_y, n + gap)
                    nc.scalar.copy(zts[:, par, 0:nk * P], psT[:, par, 0:nk * P]).then_inc(s_zts, 1)

                copy(stage * NB, 0, gap=2)
                with act.Fori(0, NB // 2) as i:
                    copy(stage * NB + 1 + 2 * i, 1)
                    copy(stage * NB + 2 + 2 * i, 0)

            act.wait_ge(s_sc, SC + 2)
            edge_pass(0)
            act.wait_ge(s_sq, 4)
            nc.scalar.activation(inq[:, :], inq[:, :], ACT.Sqrt).then_inc(s_sqd, 1)
            dense(0, 4)
            act.wait_ge(s_sq, 5)
            nc.scalar.activation(ssq[:, :], ssq[:, :], ACT.Sqrt).then_inc(s_sqd, 1)
            act.wait_ge(s_sq, 6)
            nc.scalar.activation(rstd[:, :], rstd[:, :], ACT.Sqrt).then_inc(s_sqd, 1)
            dense(1, 2)
            act.wait_ge(s_sq, 7)
            nc.scalar.activation(rstd[:, :], rstd[:, :], ACT.Sqrt).then_inc(s_sqd, 1)
            edge_pass(1)
            dense(2, 2)
            dense(3, 2)
            act.wait_ge(s_sq, 8)
            nc.scalar.activation(rstd[:, :], rstd[:, :], ACT.Sqrt).then_inc(s_sqd, 1)

            def feed(m, par, blocks=2):
                w = blocks * P
                act.wait_ge(s_ftp, m + 3)
                act.wait_ge(s_fy, 2 * m + 1)
                nc.scalar.copy(zts[:, par, :].rearrange("p (t n) -> p t n", t=2)[:, :, 0:w],
                               psT[:, par, :].rearrange("p (t n) -> p t n", t=2)[:, :, 0:w]).then_inc(s_fts, 1)
                for ht in range(HT):
                    act.wait_ge(s_hp, HT * m + ht + 1)
                    nc.scalar.activation(hid[:, par, ht, 0:w], psE[:, ht % 4, 0:w], ACT.Gelu_apprx_tanh,
                                         bias=b1s[:, ht:ht + 1]).then_inc(s_hs, 1)

            with act.Fori(0, FI // 2) as i:
                feed(2 * i, 0)
                feed(2 * i + 1, 1)
            feed(FI - 1, 0, 1)

        @block.vector
        def _(dve):
            v = nc.vector
            link = Chain(dve, s_dve)
            roots = [0]
            places = [dve.alloc_register(f"place{k}") for k in range(RING)]

            def root(t, ahead):
                roots[0] += 1
                ahead.then_inc(s_sq, 1)
                dve.wait_ge(s_sqd, roots[0] + 1)
                link(v.reciprocal(t, t))

            dve.sem_inc(s_add, 4)
            dve.sem_inc(s_z, 2)
            dve.sem_inc(s_yo, 2)
            dve.sem_inc(s_fz, 2)
            dve.sem_inc(s_fo, 2)
            dve.sem_inc(s_oht, 2)
            dve.sem_inc(s_prod, 8)
            v.memset(X[:, NB - 1, :], 0.0)
            v.memset(raw[:, FULLC, 0:P], PAD_SRC)
            v.memset(raw[:, FULLC, P:2 * P], PAD_DST)
            v.memset(raw[:, FULLC, 2 * P:3 * P], 0).then_inc(s_pad, 1)

            dve.wait_ge(s_w, 16 * (3 + 32 + 8))
            for m in (1, 2):
                for bo, bi in ((0, 3), (1, 2), (2, 3)):
                    p0 = 64 * (bo % 2)
                    a = wraw[p0:p0 + 64, m, bo // 2, 64 * bi:64 * bi + 64]
                    ins = v.tensor_scalar(a, a, -1.0, None, ALU.mult)
            ins.then_inc(s_kneg, 1)

            dve.wait_ge(s_gw, 16 * 3)
            q = RP
            for k in range(4):
                link(v.tensor_tensor(gprod[0:q, :].rearrange("p (b c) -> p b c", b=4),
                                     rel_sb[0:q, k, 0:D].rearrange("p (b c) -> p b c", b=4),
                                     gw[0:q, :].rearrange("p (c b) -> p b c", b=4), ALU.mult))
                ins = v.tensor_reduce(glog[0:q, k:k + 1], gprod[0:q, :], AX, ALU.add)
                if k < 3:
                    link(ins)
            ins.then_inc(s_sq, 1)
            dve.wait_ge(s_sqd, 1)
            for k in range(4):
                v.tensor_scalar(rel_sb[0:q, k, 0:D], rel_sb[0:q, k, 0:D], glog[0:q, k:k + 1], None, ALU.mult)
                ins = v.tensor_copy(rel_sb[0:q, k, D:DW], glog[0:q, k:k + 1])
            link(ins)
            for part in range(3):
                link(v.tensor_copy(relb[0:q, part, :, 0:DW], rel_sb[0:q, :, :]))
                if part < 2:
                    link(v.tensor_tensor(rel_sb[0:q, :, :], rel_sb[0:q, :, :], relb[0:q, part, :, 0:DW], ALU.subtract))

            dve.wait_ge(s_wt, 1)
            v.tensor_copy(wt[:, :, :, :].rearrange("p m t i -> p m (t i)"), psE[:, 0:3, :]).then_inc(s_wc, 1)

            def moments():
                link(v.tensor_tensor(sm0[:, :], st[:, :, 1], st[:, :, 4], ALU.add))
                link(v.tensor_scalar(mean[:, :], sm0[:, :], 0.5, None, ALU.mult))
                link(v.tensor_tensor(sm0[:, :], st[:, :, 1], st[:, :, 4], ALU.subtract))
                link(v.tensor_tensor(sm0[:, :], sm0[:, :], sm0[:, :], ALU.mult))
                link(v.tensor_tensor(sm1[:, :], st[:, :, 2], st[:, :, 5], ALU.add))
                link(v.tensor_scalar(sm1[:, :], sm1[:, :], 1.0 / D, EPS, ALU.mult, ALU.add))
                root(rstd[:, :], v.scalar_tensor_tensor(rstd[:, :], sm0[:, :], 0.25, sm1[:, :], ALU.mult, ALU.add))

            def normed(out, b):
                return v.tensor_scalar(out, X[:, b, :], mean[:, bass.ds(b, 1)], rstd[:, bass.ds(b, 1)],
                                       ALU.subtract, ALU.mult)

            dve.wait_ge(s_x, 32)
            with dve.Fori(0, NB - 1) as b:
                v.bn_stats(st[:, b, :], X[:, b, :])
            link(v.bn_stats(st[:, NB - 1, :], X[:, NB - 1, :]))

            dve.wait_ge(s_const, 10)
            dve.wait_ge(s_raw, 16 * 9)
            link(v.tensor_scalar(lo_i, raw[:, :, 0:P], P - 1, None, ALU.bitwise_and))
            link(v.tensor_scalar(hi_i, raw[:, :, 0:P], 7, None, ALU.logical_shift_right))
            v.tensor_copy(hlo.rearrange("p (c e) -> p c e", e=P), lo_i)
            link(v.tensor_copy(hhi, dstf[:, :].bitcast(I32)))
            with dve.Fori(0, SLOTS // HG) as i:
                dve.wait_ge(s_hmm, i + 1)
                v.tensor_tensor(ohlo[:, i & 1, :, :], hlo[:, bass.ds(HG * i, HG)].unsqueeze(2).broadcast_to([P, HG, P]),
                                iob[:, :].unsqueeze(1).broadcast_to([P, HG, P]), ALU.is_equal).then_inc(s_oh, 1)
                v.tensor_tensor(ohhi[:, i & 1, :, :], hhi[:, bass.ds(HG * i, HG)].unsqueeze(2).broadcast_to([P, HG, NB]),
                                iob[:, 0:NB].unsqueeze(1).broadcast_to([P, HG, NB]), ALU.is_equal).then_inc(s_oh, 1)

            v.tensor_copy(last[:, :], raw[:, :, 2 * P - 1])
            link(v.tensor_scalar(b128[:, :], iof[:, 0:NB], float(P), None, ALU.mult))
            link(v.tensor_tensor(cmp1[:, :, :], last[:, :].unsqueeze(1).broadcast_to([P, NB, SC]),
                                 b128[:, :].unsqueeze(2).broadcast_to([P, NB, SC]), ALU.is_lt))
            v.tensor_reduce(cnt[:, :], cmp1[:, :, :], AX, ALU.add).then_inc(s_cnt, 1)
            dve.wait_ge(s_lo, 1)
            link(v.tensor_tensor(sbs[:, :], psY[:, 1, 0:NB], iof[:, 0:NB], ALU.add))
            link(v.tensor_tensor(cmp2[:, :, :], sbs[:, 1:NB].unsqueeze(1).broadcast_to([P, SC, NB - 1]),
                                 pidx[:, :].unsqueeze(2).broadcast_to([P, SC, NB - 1]), ALU.is_le))
            link(v.tensor_reduce(bp[:, :], cmp2[:, :, :], AX, ALU.add))
            link(v.tensor_tensor(tpf[:, :], pidx[:, :], bp[:, :], ALU.subtract))
            v.tensor_scalar(bp128[:, :], bp[:, :], float(P), None, ALU.mult)
            v.tensor_copy(tpi[:, :], tpf[:, :]).then_inc(s_tp, 1)
            dve.wait_ge(s_bt, 1)
            v.tensor_copy(bti[:, :], psE[0:SC, 3, 0:P]).then_inc(s_bti, 1)
            dve.wait_ge(s_slot, 16 * SC)
            link(v.tensor_copy(slot_f[:, :, P:3 * P], slot_i[:, :, 0:2 * P]))
            v.tensor_copy(types_h, slot_i[:, :, 2 * P:3 * P]).then_inc(s_typ, 1)
            v.tensor_tensor(slot_f[:, :, 2 * P:3 * P], slot_f[:, :, 2 * P:3 * P],
                            bp128[:, :].unsqueeze(2).broadcast_to([P, SC, P]), ALU.subtract).then_inc(s_cv, 1)

            dve.wait_ge(s_hist, 1)
            root(degu[:, :], v.tensor_scalar(degu[:, :], psY[:, 0, 0:NB], 1.0, None, ALU.max))
            moments()

            dve.wait_ge(s_sc, SC + 2)
            dve.wait_ge(s_wc, 1)
            dve.wait_ge(s_typd, 16)
            link(v.memset(acc[:, :, D:W], 1.0))
            with dve.Fori(0, NB) as b:
                link.enter(b, 1)
                link(normed(acc[:, b, 0:D], b))
                v.tensor_scalar(acc[:, b, 0:D], acc[:, b, 0:D], degu[:, bass.ds(b, 1)], None, ALU.mult).then_inc(s_trow, 1)
                link.leave(NB)
            dve.wait_ge(s_td, 16 * (NB // 7))
            v.memset(accf[:, :], 0.0).then_inc(s_zero, 1)
            dve.wait_ge(s_zero, 1)
            dve.wait_ge(s_brow, 16)

            def edge_pass(layer):
                def one_hots(i, h):
                    dve.wait_ge(s_tb[h], 16 * (layer * IT + i + 1))
                    dve.wait_ge(s_rel, layer * REL * IT + REL * i + HALF * h + HALF)
                    for t in range(RK):
                        ins = v.tensor_scalar(oht[0:RP, h, t, :, :], types[0:RP, h, layer, :, :], tid[0:RP, t:t + 1],
                                              None, ALU.is_equal)
                    ins.then_inc(s_oht, 1)

                def ahead(i, k):
                    n = layer * SLOTS + k + RING * i
                    dve.wait_ge(s_mm, n - 4 + RING + 1)
                    v.tensor_scalar(sel[:, k % 4, :], iof[:, :], dstf[:, bass.ds(RING * i + k, 1)], None,
                                    ALU.is_equal).then_inc(s_sel, 1)
                    if layer == 1:
                        dve.wait_ge(s_g[k], 16 * IT + 16 * i + 16)
                        if k % 2 == 0:
                            dve.wait_ge(s_rl[k // REL], 16 * i + 16)
                            factor = relg[:, k // REL, k % REL // 2, :]
                        else:
                            dve.wait_ge(s_rel, REL + REL * IT + REL * i + k // 2 + 1)
                            factor = psR[k // 2 % 4][:, 0:DW]
                        v.tensor_tensor(gath[:, k, 0:DW], gath[:, k, 0:DW], factor, ALU.mult).then_inc(s_prod, 1)

                def iteration(i, last=False):
                    dve.load(places, brow[0:1, bass.ds(RING * i, RING)])
                    for k in range(RING):
                        if k < RING - LEAD:
                            ahead(i, k + LEAD)
                        elif not last:
                            ahead(i + 1, k + LEAD - RING)
                        n = layer * SLOTS + k + RING * i
                        b = dve.snap(places[k], min_val=0, max_val=NB - 1)
                        dve.wait_ge(s_mm, n + RING + 1)
                        dve.wait_ge(s_add, n + 4)
                        v.tensor_tensor(acc[:, b, 0:DW], acc[:, b, 0:DW], psE[:, k % 4, 0:DW],
                                        ALU.add).then_inc(s_add, 1)
                        if k == 1:
                            one_hots(i, 1)
                        if k == 9 and not last:
                            one_hots(i + 1, 0)

                one_hots(0, 0)
                for k in range(LEAD):
                    ahead(0, k)
                with dve.Fori(0, IT - 1) as i:
                    iteration(i)
                iteration(IT - 1, last=True)

            edge_pass(0)
            dve.wait_ge(s_add, SLOTS + 4)

            v.tensor_scalar(has[:, :], acc[:, :, D], 0.0, None, ALU.is_gt)
            root(inq[:, :], v.tensor_scalar(inq[:, :], acc[:, :, D], 1.0, None, ALU.max))

            def dense(stage, rows, links_rows, use, links_use):
                first = stage * NB
                per = 2 * (links_rows + links_use)

                def ahead(j, par, gap=1):
                    dve.wait_ge(s_ztp, first + j + gap)
                    rows(par, j)

                def take(j, par):
                    dve.wait_ge(s_y, first + j + 3)
                    use(par, j)

                ahead(0, 0, gap=2)
                with dve.Fori(0, NB // 2) as i:
                    link.enter(i, per)
                    ahead(2 * i + 1, 1)
                    take(2 * i, 0)
                    ahead(2 * i + 2, 0)
                    take(2 * i + 1, 1)
                    link.leave(NB // 2)
                take(NB - 1, 0)

            def rows0(par, b):
                link(normed(tmp[:, par, :], b))
                v.scalar_tensor_tensor(zst[:, par, 0:D], acc[:, b, 0:D], degu[:, bass.ds(b, 1)], tmp[:, par, :],
                                       ALU.mult, ALU.add)
                v.scalar_tensor_tensor(zst[:, par, D:2 * D], acc[:, b, 0:D], degu[:, bass.ds(b, 1)], tmp[:, par, :],
                                       ALU.mult, ALU.mult).then_inc(s_z, 1)

            def use0(par, b):
                link(v.scalar_tensor_tensor(gprod[:, :], psY[:, par, 0:D], has[:, bass.ds(b, 1)], b0s[:, :],
                                            ALU.mult, ALU.add))
                dve.sem_inc(s_yo, 1)
                link(v.scalar_tensor_tensor(acc[:, b, 0:D], gprod[:, :], 0.01, gprod[:, :], ALU.mult, ALU.max))
                link(v.scalar_tensor_tensor(gprod[:, :], acc[:, b, 0:D], 1.0, acc[:, b, 0:D], ALU.mult, ALU.mult,
                                            accum_out=ssq[:, bass.ds(b, 1)]))

            dense(0, rows0, 1, use0, 3)

            roots[0] += 1
            dve.sem_inc(s_sq, 1)
            dve.wait_ge(s_sqd, roots[0] + 1)
            link(v.tensor_scalar(ssq[:, :], ssq[:, :], 1e-12, None, ALU.max))
            link(v.reciprocal(ssq[:, :], ssq[:, :]))
            with dve.Fori(0, NB) as b:
                link.enter(b, 2)
                link(v.scalar_tensor_tensor(X[:, b, :], acc[:, b, 0:D], ssq[:, bass.ds(b, 1)], X[:, b, :],
                                            ALU.mult, ALU.add))
                link(v.bn_stats(st[:, b, :], X[:, b, :]))
                link.leave(NB)
            moments()

            def rows1(par, b):
                normed(zst[:, par, 0:D], b).then_inc(s_z, 1)

            def use1(par, b):
                link(v.tensor_tensor(gprod[:, :], psY[:, par, 0:D], bfs[:, :], ALU.add))
                dve.sem_inc(s_yo, 1)
                link(v.tensor_tensor(X[:, b, :], X[:, b, :], gprod[:, :], ALU.add))
                link(v.bn_stats(st[:, b, :], X[:, b, :]))

            dense(1, rows1, 0, use1, 3)
            moments()

            link(v.tensor_copy(acc[:, :, D], degu[:, :]))
            with dve.Fori(0, NB) as b:
                link.enter(b, 1)
                link(normed(acc[:, b, 0:D], b))
                v.tensor_scalar(acc[:, b, 0:D], acc[:, b, 0:D], degu[:, bass.ds(b, 1)], None, ALU.mult).then_inc(s_trow, 1)
                link.leave(NB)
            dve.wait_ge(s_td, 2 * 16 * (NB // 7))
            v.memset(accf[:, :], 0.0).then_inc(s_zero, 1)
            dve.wait_ge(s_zero, 2)
            edge_pass(1)
            dve.wait_ge(s_add, 2 * SLOTS + 4)

            def rows2(par, b):
                v.tensor_copy(zst[:, par, 0:D], acc[:, b, 0:D]).then_inc(s_z, 1)

            def use2(par, b):
                link(v.scalar_tensor_tensor(gprod[:, :], mbs[:, :], acc[:, b, D:DW], psY[:, par, 0:D], ALU.mult, ALU.add))
                dve.sem_inc(s_yo, 1)
                link(normed(tmp[:, par, :], b))
                link(v.scalar_tensor_tensor(acc[:, b, 0:D], gprod[:, :], inq[:, bass.ds(b, 1)], tmp[:, par, :],
                                            ALU.mult, ALU.add))

            dense(2, rows2, 0, use2, 3)

            def use3(par, b):
                link(v.tensor_tensor(gprod[:, :], psY[:, par, 0:D], ubs[:, :], ALU.add))
                dve.sem_inc(s_yo, 1)
                xb = X[:, b, :].rearrange("p (c a) -> p c a", a=4)
                link(v.tensor_tensor(xb, xb, gprod[:, :].rearrange("p (a c) -> p c a", a=4), ALU.add))
                link(v.bn_stats(st[:, b, :], X[:, b, :]))

            dense(3, rows2, 0, use3, 3)
            moments()

            with dve.Fori(0, NB) as b:
                link.enter(b, 2)
                link(normed(tmp[:, 0, :], b))
                link(v.scalar_tensor_tensor(gprod[:, :], tmp[:, 0, :], 1.0, wrs[:, :], ALU.mult, ALU.mult,
                                            accum_out=score[:, bass.ds(b, 1)]))
                link.leave(NB)
            link(v.tensor_scalar(valid[:, :], valid[:, :], float(N), None, ALU.is_lt))
            link(v.tensor_scalar(score[:, :], score[:, :], brs[:, :], None, ALU.add))
            v.memset(trial[:, :], 1)
            v.memset(found[:, :], 0)
            link(v.memset(thr[:, :], 0.0))
            link(v.tensor_tensor(bit[:, :], trial[:, :].broadcast_to([P, BITS]), shift[:, :], ALU.logical_shift_left))
            link(v.tensor_copy(bitf[:, :], bit[:, :]))

            v.scalar_tensor_tensor(flag[:, :], score[:, :], thr[:, :], valid[:, :], ALU.is_ge, ALU.mult,
                                   accum_out=hits[:, :]).then_inc(s_hits, 1)
            dve.wait_ge(s_total, 1)
            link(v.tensor_scalar(need[:, :], psE[:, 0, 0:1], float(TOP), None, ALU.is_ge))
            v.tensor_scalar(sign[:, :], need[:, :], 2.0, -1.0, ALU.mult, ALU.add)
            link(v.tensor_scalar(want[:, :], need[:, :], float(2 * TOP - N - 1), float(N - TOP + 1), ALU.mult, ALU.add))
            link(v.tensor_scalar(keyed[:, :], score[:, :], sign[:, :], None, ALU.mult))
            with dve.Fori(0, BITS) as i:
                link.enter(i, 3)
                link(v.tensor_tensor(trial[:, :], found[:, :], bit[:, bass.ds(i, 1)], ALU.bitwise_or))
                v.scalar_tensor_tensor(flag[:, :], keyed[:, :], trial[:, :].bitcast(F32), valid[:, :], ALU.is_ge, ALU.mult,
                                       accum_out=hits[:, :]).then_inc(s_hits, 1)
                dve.wait_ge(s_total, i + 2)
                link(v.scalar_tensor_tensor(step[:, :], psE[:, 0, 0:1], want[:, :], bitf[:, bass.ds(i, 1)],
                                            ALU.is_ge, ALU.mult))
                link(v.tensor_tensor(found[:, :], found[:, :], step[:, :], ALU.bitwise_or))
                link.leave(BITS)
            link(v.tensor_tensor(thr[:, :], found[:, :].bitcast(F32), sign[:, :], ALU.mult))
            v.scalar_tensor_tensor(pick[:, :], score[:, :], thr[:, :], valid[:, :], ALU.is_gt, ALU.mult,
                                   accum_out=hits[:, :]).then_inc(s_hits, 1)
            dve.wait_ge(s_total, BITS + 2)
            v.tensor_scalar(need[:, :], psE[:, 0, 0:1], -1.0, float(TOP), ALU.mult, ALU.add)
            v.scalar_tensor_tensor(tie[:, :], score[:, :], thr[:, :], valid[:, :], ALU.is_equal, ALU.mult).then_inc(s_hits, 1)
            dve.wait_ge(s_total, BITS + 3)
            link(v.tensor_copy(sm0[:, :], psE[:, 2, 0:NB]))
            link(v.tensor_tensor_scan(sm1[:, :], ones[:, 0:NB], sm0[:, :], 0.0, ALU.mult, ALU.add))
            link(v.tensor_tensor(sm1[:, :], sm1[:, :], sm0[:, :], ALU.subtract))
            link(v.tensor_tensor(sm1[:, :], sm1[:, :], psE[:, 1, 0:NB], ALU.add))
            link(v.scalar_tensor_tensor(sm1[:, :], sm1[:, :], need[:, :], tie[:, :], ALU.is_lt, ALU.mult))
            link(v.tensor_tensor(pick[:, :], pick[:, :], sm1[:, :], ALU.add))
            link(v.tensor_tensor(pick[:, :], pick[:, :], score[:, :], ALU.mult))

            def rows(m, par, blocks=2):
                dve.wait_ge(s_ftp, m + 1)
                for q in range(blocks):
                    ins = normed(zst[:, par, q * D:(q + 1) * D], 2 * m + q)
                ins.then_inc(s_fz, 1)

            def finish(m, blocks=2):
                for q in range(blocks):
                    b = 2 * m + q
                    dve.wait_ge(s_fy, b + 3)
                    v.tensor_tensor(gprod[:, :], psY[:, q, 0:D], b2s[:, :], ALU.add)
                    link(normed(tmp[:, q, :], b))
                    link(v.scalar_tensor_tensor(gprod[:, :], gprod[:, :], pick[:, bass.ds(b, 1)], X[:, b, :],
                                                ALU.mult, ALU.add))
                    v.tensor_tensor(acc[:, b, 0:D], gprod[:, :], tmp[:, q, :], ALU.add).then_inc(s_fo, 1)
                    dve.wait_ge(s_fo, b + 3)

            rows(0, 0)
            with dve.Fori(0, FI // 2 - 1) as i:
                link.enter(i, 8)
                rows(2 * i + 1, 1)
                finish(2 * i)
                rows(2 * i + 2, 0)
                finish(2 * i + 1)
                link.leave(FI // 2 - 1)
            rows(FI - 2, 1)
            finish(FI - 3)
            rows(FI - 1, 0, 1)
            finish(FI - 2)
            finish(FI - 1, 1)


_INS = ['x', 'src', 'dst', 'edge_type_500', 'L0_gnn_W1', 'L0_gnn_W2', 'L0_gnn_b', 'L0_ffn_weight', 'L0_ffn_bias',
        'L1_gnn_relation_emb', 'L1_gnn_msg_w', 'L1_gnn_msg_b', 'L1_gnn_upd_w', 'L1_gnn_upd_b', 'L1_gnn_gate_w',
        'L1_gnn_gate_b', 'L1_ffn_wr', 'L1_ffn_br', 'L1_ffn_w1', 'L1_ffn_b1', 'L1_ffn_w2', 'L1_ffn_b2']


def kernel(**inputs):
    import numpy as _np
    import concourse.bacc as _bacc
    from concourse.bass_utils import run_bass_kernel_spmd as _run

    nc = _bacc.Bacc("TRN2", target_bir_lowering=False, num_devices=1)
    arrays, args = {}, []
    for name in _INS:
        a = _np.ascontiguousarray(inputs[name])
        arrays[f"in_{name}"] = a
        args.append(nc.dram_tensor(f"in_{name}", a.shape, mybir.dt.from_np(a.dtype), kind="ExternalInput").ap())
    args.append(nc.dram_tensor("out_0", (N, D), F32, kind="ExternalOutput").ap())
    program(nc, *args)
    r = _run(nc, [arrays], core_ids=[0])
    return r.results[0]["out_0"]
```

```python
import concourse.bass as bass
from concourse import mybir
from contextlib import ExitStack

F32 = mybir.dt.float32
BF16 = mybir.dt.bfloat16
F16 = mybir.dt.float16
I32 = mybir.dt.int32
ALU = mybir.AluOpType
ACT = mybir.ActivationFunctionType
AX = mybir.AxisListType.X

P = 128
N = 6250
D = 256
E = 206250
R = 500
H = 1024
NB = -(-N // P)
TAIL = N - (NB - 1) * P
TILES = -(-E // P)
SC = -(-(TILES + NB) // P)
SLOTS = SC * P
FULLC = E // (P * P)
RESTT = (E - FULLC * P * P) // P
RESTE = E - FULLC * P * P - RESTT * P
W = 260
ZW = 22 * W
DW = D + 1
PAD_SRC = NB * P - 1
PAD_DST = 1 << 13
HT = H // P
RING = 16
LEAD = 3
RK = 4
RP = R // RK
REL = RING // 2
HALF = REL // 2
IT = SLOTS // RING
HG = 16
TOP = N // 2 - 1
CB = -(-TOP // P)
CTAIL = TOP - (CB - 1) * P
FI = CB // 2 + 1
OUT_OF_REACH = 1 << 13
DIGITS = 10
TRIALS = 7
COUNTS = DIGITS + 3
EPS = 1e-5
SK = 4
U = 7
G = 8


class Chain:

    def __init__(self, eng, sem):
        self.eng, self.sem, self.base, self.n = eng, sem, 0, 0

    def __call__(self, ins):
        self.n += 1
        ins.then_inc(self.sem, 1)
        self.eng.wait_ge(self.sem, self.base + self.n)

    def enter(self, step, per):
        self.start, self.per = (self.base, self.n), per
        self.base, self.n = self.start[0] + self.start[1] + step * per, 0

    def leave(self, steps):
        assert self.n == self.per, (self.n, self.per)
        self.base, self.n = self.start[0] + self.start[1] + steps * self.per, 0


def program(nc, x, src, dst, etype, w1_0, w2_0, b_0, wf, bf, rel, msg_w, msg_b, upd_w, upd_b,
            gate_w, gate_b, wr, br, w1, b1, w2, b2, out):
    ctx = ExitStack()
    with ctx:
        def sb(name, shape, dt=F32):
            return ctx.enter_context(nc.sbuf_tensor(name, shape, dt))

        def sem(name):
            return ctx.enter_context(nc.semaphore(name))

        edges_d = nc.dram_tensor("edges_d", (SLOTS, 3 * P), I32).ap()
        t1_d = nc.dram_tensor("t1_d", (NB * P, W), F32).ap()
        t2_d = nc.dram_tensor("t2_d", (NB * P, W), F32).ap()
        types_d = nc.dram_tensor("types_d", (SLOTS, P), F16).ap()
        rel_d = nc.dram_tensor("rel_d", (2 * IT, P, HALF * DW), F32).ap()

        relw_d = nc.dram_tensor("relw_d", (R, DW), F32).ap()
        acc_d = nc.dram_tensor("acc_d", (NB * P, W), F32).ap()

        h_d = nc.dram_tensor("h_d", (NB * P, W), F32).ap()

        X = sb("X", [P, NB, D])
        accf = sb("accf", [P, NB * W])
        work = sb("work", [P, RING * W + REL * DW + RING * P // 2 + RK * REL * P // 2])
        srci = sb("srci", [P, SLOTS + RING], I32)
        dstf = sb("dstf", [P, SLOTS])
        brow = sb("brow", [1, SLOTS], I32)
        idxs = sb("idxs", [P, RING], I32)
        sel = sb("sel", [P, 4, P])
        acc = accf[:, :].rearrange("p (b w) -> p b w", w=W)
        gath = work[:, 0:RING * W].rearrange("p (k w) -> p k w", w=W)
        o = RING * W
        u_rows, u_rel, u_old = gath[:, 0, :], gath[:, 1, :], gath[:, 2, :]
        u_edge = gath[:, 3, :].bitcast(I32)[:, P:P + 3]
        u_dst = gath[:, 3, :].bitcast(I32)[:, 0:P]
        u_dstf, u_own = gath[:, 4, 0:P], gath[:, 4, P:P + 1]
        relg = work[:, o:o + REL * DW].rearrange("p (h k w) -> p h k w", h=2, w=DW)
        o += REL * DW
        types = work[:, o:o + RING * P // 2].bitcast(F16).rearrange("p (h j r e) -> p h r j e", h=2, r=2, e=P)
        types_w = work[:, o:o + RING * P // 2].bitcast(F16).rearrange("p (h n) -> p h n", h=2)
        o += RING * P // 2
        oht = work[:, o:o + RK * REL * P // 2].bitcast(BF16).rearrange("p (h t j e) -> p h t j e", h=2, t=RK, e=P)
        raw = work[:, 0:SC * 384].bitcast(I32).rearrange("p (c w) -> p c w", w=384)
        o = SC * 384
        ohlo = work[:, o:o + HG * P].bitcast(BF16).rearrange("p (r l t) -> p r l t", r=2, l=P)
        o += HG * P
        ohhi = work[:, o:o + HG * NB].bitcast(BF16).rearrange("p (r l t) -> p r l t", r=2, l=NB)
        descent = dstf[:, 0:SC * (P - 1)].rearrange("p (c e) -> p c e", e=P - 1)
        slot_i = accf[:, 0:SC * 384].bitcast(I32).rearrange("p (c w) -> p c w", w=384)
        slot_f = accf[:, SC * 384:2 * SC * 384].rearrange("p (c w) -> p c w", w=384)
        o = 2 * SC * 384
        wraw = accf[:, o:o + 3 * 2 * D].rearrange("p (m t i) -> p m t i", m=3, t=2)
        o += 3 * 2 * D
        rel_sb = accf[:, o:o + RK * DW].rearrange("p (k w) -> p k w", w=DW)
        types_h = slot_f[:, :, 0:P].bitcast(F16)[:, :, 0:P]
        o = SC * 384 + HG * P + HG * NB
        hhi = work[:, o:o + SLOTS // 2].bitcast(BF16)
        o += SLOTS // 2
        hlo = srci[:, 0:SLOTS // 2].bitcast(BF16)
        lo_i = slot_f[:, :, 0:P].bitcast(I32)
        hi_i = dstf[:, :].bitcast(I32).rearrange("p (c e) -> p c e", e=P)
        o = 2 * H
        f1 = work[:, 0:o].rearrange("p (t n) -> p t n", t=2)
        f2 = work[:, o:o + HT * D].rearrange("p (t n) -> p t n", t=HT)
        o += HT * D
        hid = work[:, o:o + 2 * HT * 2 * P].rearrange("p (r t n) -> p r t n", r=2, t=HT)
        o = 2 * H + HT * D
        place_lo = work[:, o:o + NB * P // 2].bitcast(BF16).rearrange("p (b l) -> p b l", l=P)
        o += NB * P // 2
        place_w = work[:, o:o + NB * CB].bitcast(BF16).rearrange("p (b q h) -> p b q h", q=2, h=CB)
        o += NB * CB
        place_hi = work[:, o:o + NB * CB // 2 + 1].bitcast(BF16)[:, 0:NB * CB].rearrange("p (b h) -> p b h", h=CB)
        hg = accf[:, 0:CB * W].rearrange("p (c w) -> p c w", w=W)
        base = X[:, 0:CB, :]
        relb = sb("relb", [P, 3, RK, DW + 1], BF16)
        tid = sb("tid", [P, RK])
        gw = sb("gw", [P, D])
        gprod = sb("gprod", [P, 2, D])
        gb = sb("gb", [P, 1])
        glog = sb("glog", [P, RK])

        ident = sb("ident", [P, P])
        ones = sb("ones", [P, P])
        iof = sb("iof", [P, P])
        iob = sb("iob", [P, P], BF16)
        zb = sb("zb", [P, P], BF16)
        pidx = sb("pidx", [P, SC])
        w1s = sb("w1s", [P, 2, D])
        w2s = sb("w2s", [P, 2, D])
        wt = sb("wt", [P, 3, 2, D])
        b0s = sb("b0s", [P, D])
        bfs = sb("bfs", [P, D])
        mbs = sb("mbs", [P, D])
        ubs = sb("ubs", [P, D])
        zst = sb("zst", [P, 2, 2 * D])
        zts = sb("zts", [P, 2, 2 * D])
        tmp = sb("tmp", [P, 2, D])
        st = sb("st", [P, NB, 6])
        mean = sb("mean", [P, NB])
        rstd = sb("rstd", [P, NB])
        sm0 = sb("sm0", [P, NB])
        sm1 = sb("sm1", [P, NB])
        rdeg = sb("rdeg", [P, NB])
        degu = sb("degu", [P, NB])
        has = sb("has", [P, NB])
        inq = sb("inq", [P, NB])
        ssq = sb("ssq", [P, NB])
        b128 = sb("b128", [P, NB])
        counted = zts[:, :, :].rearrange("p r d -> p (r d)")[:, 0:HG * P // 2].bitcast(BF16).rearrange("p (l t) -> p l t", l=P)
        cmp1 = zst[:, :, :].rearrange("p r d -> p (r d)")[:, 0:NB * SC].rearrange("p (b c) -> p b c", c=SC)
        cmp2 = zst[:, :, :].rearrange("p r d -> p (r d)")[:, 0:SC * (NB - 1)].rearrange("p (c b) -> p c b", b=NB - 1)
        last = sb("last", [P, SC])
        cnt = sb("cnt", [P, NB + 1])
        prv = sb("prv", [P, SC])
        drops = sb("drops", [P, 2])
        unsorted = sb("unsorted", [P, 1], I32)
        sbs = sb("sbs", [P, NB])
        junk = zts[:, :, :].rearrange("p r (g d) -> p (r g) d", d=D)
        junk2 = zst[:, :, :].rearrange("p r (g d) -> p (r g) d", d=D)
        bp = sb("bp", [P, SC])
        bp128 = sb("bp128", [P, SC])
        tpf = sb("tpf", [P, SC])
        tpi = sb("tpi", [P, SC], I32)
        bti = sb("bti", [SC, P], I32)
        sqj = sb("sqj", [P, D])
        wrs = sb("wrs", [P, D])
        brs = sb("brs", [P, 1])
        b1s = sb("b1s", [P, HT])
        b2s = sb("b2s", [P, D])
        tri = sb("tri", [P, P])
        valid = sb("valid", [P, NB])
        score = sb("score", [P, NB])
        keyed = sb("keyed", [P, NB])
        flag = sb("flag", [P, NB])
        tie = sb("tie", [P, NB])
        pick = sb("pick", [P, NB])
        place = sb("place", [P, NB], I32)
        part_i = sb("part_i", [P, 2, NB], I32)
        part_b = sb("part_b", [P, 2, NB], BF16)
        picked = sb("picked", [P, CB], I32)
        shift = sb("shift", [P, DIGITS], I32)
        digit = sb("digit", [P, TRIALS], I32)
        digits = sb("digits", [P, DIGITS, TRIALS], I32)
        unit = sb("unit", [P, DIGITS])
        found = sb("found", [P, 1])
        trial = sb("trial", [P, TRIALS], I32)
        gain = sb("gain", [P, 1])
        gain_i = sb("gain_i", [P, 1], I32)
        reach = gprod[:, :, :].rearrange("p r d -> p (r d)")[:, 0:TRIALS * NB].rearrange("p (t b) -> p t b", b=NB)
        hits = sb("hits", [P, TRIALS])
        sign = sb("sign", [P, 1])
        want = sb("want", [P, 1])
        thr = sb("thr", [P, 1])
        need = sb("need", [P, 1])

        psE = ctx.enter_context(nc.psum_tensor("psE", [P, 4, 512], F32))
        psT = ctx.enter_context(nc.psum_tensor("psT", [P, 2, 512], F32))
        psY = ctx.enter_context(nc.psum_tensor("psY", [P, 2, 512], F32))

        psR = [psT[:, 0, :], psT[:, 1, :], psY[:, 0, :], psY[:, 1, :]]

        s_const = sem("s_const")
        s_pool = sem("s_pool")
        s_dve = sem("s_dve")
        s_pad = sem("s_pad")
        s_x = sem("s_x")
        s_raw = sem("s_raw")
        s_w = sem("s_w")
        s_gw = sem("s_gw")
        s_ed = sem("s_ed")
        s_oh = sem("s_oh")
        s_hl = sem("s_hl")
        s_cvf = sem("s_cvf")
        s_hmm = sem("s_hmm")
        s_hist = sem("s_hist")
        s_cnt = sem("s_cnt")
        s_lo = sem("s_lo")
        s_tp = sem("s_tp")
        s_bt = sem("s_bt")
        s_bti = sem("s_bti")
        s_brow = sem("s_brow")
        s_slot = sem("s_slot")
        s_cv = sem("s_cv")
        s_st = sem("s_st")
        s_sc = sem("s_sc")
        s_kneg = sem("s_kneg")
        s_wt = sem("s_wt")
        s_wc = sem("s_wc")
        s_sq = sem("s_sq")
        s_sqd = sem("s_sqd")
        s_typ = sem("s_typ")
        s_typd = sem("s_typd")
        s_tb = [sem(f"s_tb{h}") for h in range(2)]
        s_oht = sem("s_oht")
        s_rel = sem("s_rel")
        s_relc = sem("s_relc")
        s_rst = [sem(f"s_rst{h}") for h in range(2)]
        s_rfree = sem("s_rfree")
        s_rl = [sem(f"s_rl{h}") for h in range(2)]
        s_trow = sem("s_trow")
        s_td = sem("s_td")
        s_zero = sem("s_zero")
        s_turn = sem("s_turn")
        s_idx = sem("s_idx")
        s_g = [sem(f"s_g{k}") for k in range(RING)]
        s_sel = sem("s_sel")
        s_prod = sem("s_prod")
        s_mm = sem("s_mm")
        s_add = sem("s_add")
        s_emb = sem("s_emb")
        s_ssq = sem("s_ssq")
        s_z = sem("s_z")
        s_ztp = sem("s_ztp")
        s_zts = sem("s_zts")
        s_y = sem("s_y")
        s_yo = sem("s_yo")
        s_acc = sem("s_acc")
        s_uz = sem("s_uz")
        s_uztp = sem("s_uztp")
        s_uzts = sem("s_uzts")
        s_uy = sem("s_uy")
        s_uyo = sem("s_uyo")
        s_fw = sem("s_fw")
        s_hits = sem("s_hits")
        s_total = sem("s_total")
        s_fz = sem("s_fz")
        s_ftp = sem("s_ftp")
        s_fts = sem("s_fts")
        s_hp = sem("s_hp")
        s_hs = sem("s_hs")
        s_fy = sem("s_fy")
        s_fc = sem("s_fc")
        s_fo = sem("s_fo")
        s_hrow = sem("s_hrow")
        s_hd = sem("s_hd")
        s_xh = sem("s_xh")
        s_place = sem("s_place")
        s_list = sem("s_list")
        s_picked = sem("s_picked")
        s_h = [sem(f"s_h{k}") for k in range(4)]
        s_base = [sem(f"s_base{k}") for k in range(4)]
        s_put = sem("s_put")
        s_out = sem("s_out")
        s_prv = sem("s_prv")
        s_relw = sem("s_relw")
        s_relwd = sem("s_relwd")
        s_uzero = sem("s_uzero")
        s_uacc = sem("s_uacc")
        s_uload = [sem(f"s_uload{k}") for k in range(SK)]
        s_urows = [sem(f"s_urows{k}") for k in range(SK)]
        s_uold = [sem(f"s_uold{k}") for k in range(SK)]
        s_uput = [sem(f"s_uput{k}") for k in range(SK)]
        s_uto = sem("s_uto")
        s_uown = sem("s_uown")
        s_utile = sem("s_utile")
        s_usel = sem("s_usel")
        s_uprod = sem("s_uprod")
        s_umm = sem("s_umm")
        s_uadd = sem("s_uadd")

        def steps(eng, step):
            first = 3
            turns = (NB - first) // G
            for j in range(first):
                step(j, j % 2)
            with eng.Fori(0, turns) as i:
                for k in range(G):
                    step(first + G * i + k, (first + k) % 2)
            for j in range(first + G * turns, NB + 3):
                step(j, j % 2)

        def there(j):
            return not isinstance(j, int) or 0 <= j < NB

        block = ctx.enter_context(nc.Block())

        src_t = edges_d.rearrange("(c p) w -> p c w", p=P)

        @block.sync
        def _(sp):
            sp.sem_inc(s_rfree, 2)
            sp.dma_start(rel_sb[0:RP, :, 0:D], rel.rearrange("(k p) d -> p k d", k=4)).then_inc(s_gw, 16)
            sp.dma_start(gw[:, :], gate_w.broadcast_to([P, D])).then_inc(s_gw, 16)
            sp.dma_start(gb[:, :], gate_b.rearrange("(o d) -> o d", o=1).broadcast_to([P, 1])).then_inc(s_gw, 16)
            sp.wait_ge(s_pad, 1)
            for n, a in enumerate((src, dst, etype)):
                c0, c1 = n * P, (n + 1) * P
                sp.dma_start(raw[:, 0:FULLC, c0:c1],
                             a[0:FULLC * P * P].rearrange("(c p e) -> p c e", p=P, e=P)).then_inc(s_raw, 16)
                e0 = FULLC * P * P
                sp.dma_start(raw[0:RESTT, FULLC, c0:c1],
                             a[e0:e0 + RESTT * P].rearrange("(p e) -> p e", e=P)).then_inc(s_raw, 16)
                sp.dma_start(raw[RESTT:RESTT + 1, FULLC, c0:c0 + RESTE],
                             a[e0 + RESTT * P:E].rearrange("(p e) -> p e", p=1)).then_inc(s_raw, 16)
            sp.dma_start(X[:, 0:NB - 1, :], x[0:(NB - 1) * P, :].rearrange("(b p) d -> p b d", p=P)).then_inc(s_x, 16)
            sp.dma_start(X[0:TAIL, NB - 1, :], x[(NB - 1) * P:N, :]).then_inc(s_x, 16)
            sp.wait_ge(s_relw, 1)
            sp.dma_start(relw_d.rearrange("(k p) d -> p k d", k=RK), rel_sb[0:RP, :, :]).then_inc(s_relwd, 16)
            sp.wait_ge(s_raw, 16 * 9)
            sp.dma_start(src_t, raw[:, :, :]).then_inc(s_ed, 16)
            sp.dma_start(prv[1:P, :].bitcast(I32), raw[0:P - 1, :, 2 * P - 1],
                         allow_slow_non_contiguous=True).then_inc(s_prv, 16)
            sp.dma_start(prv[0:1, 1:SC].bitcast(I32), raw[P - 1:P, 0:SC - 1, 2 * P - 1],
                         allow_slow_non_contiguous=True).then_inc(s_prv, 16)
            sp.dma_start(w1s[:, :, :], w1_0.rearrange("(t p) n -> p t n", p=P)).then_inc(s_w, 16)
            sp.dma_start(w2s[:, :, :], w2_0.rearrange("(t p) n -> p t n", p=P)).then_inc(s_w, 16)
            sp.dma_start(wraw[:, 0, :, :], wf.rearrange("(t p) n -> p t n", p=P)).then_inc(s_w, 16)
            for m, a in ((1, msg_w), (2, upd_w)):
                for bo in range(4):
                    for bi in range(4):
                        p0 = 64 * (bo % 2)
                        sp.dma_start(wraw[p0:p0 + 64, m, bo // 2, 64 * bi:64 * bi + 64], a[bo ^ bi, :, :]).then_inc(s_w, 16)
            for t, a in ((b0s, b_0), (bfs, bf)):
                sp.dma_start(t[:, :], a.rearrange("(o d) -> o d", o=1).broadcast_to([P, D])).then_inc(s_w, 16)
            sp.dma_start(b2s[:, :], b2.rearrange("(o d) -> o d", o=1).broadcast_to([P, D])).then_inc(s_w, 16)
            sp.dma_start(wrs[:, :], wr.rearrange("d o -> o d").broadcast_to([P, D])).then_inc(s_w, 16)
            sp.dma_start(brs[:, :], br.rearrange("(o d) -> o d", o=1).broadcast_to([P, 1])).then_inc(s_w, 16)
            sp.dma_start(b1s[:, :], b1.rearrange("(t p) -> p t", p=P), allow_slow_non_contiguous=True).then_inc(s_w, 16)
            for t, a in ((mbs, msg_b), (ubs, upd_b)):
                sp.dma_start(t[:, :], a.rearrange("(o a) c -> o (a c)", o=1).broadcast_to([P, D])).then_inc(s_w, 16)
            sp.wait_ge(s_bti, 1)
            sp.dma_start(brow[0:1, :].rearrange("o (c p) -> o c p", p=P), bti[:, :]).then_inc(s_brow, 16)
            sp.wait_ge(s_typ, 1)
            sp.dma_start(types_d[0:SLOTS, :].rearrange("(c p) e -> p c e", p=P), types_h).then_inc(s_typd, 16)


            def table(layer, dram):
                for c in range(NB // 7):
                    sp.wait_ge(s_trow, layer * NB + 7 * (c + 1))
                    sp.dma_start(dram.rearrange("(b p) w -> p b w", p=P)[:, 7 * c:7 * c + 7, :],
                                 acc[:, 7 * c:7 * c + 7, :]).then_inc(s_td, 16)

            def load_types(p, i, h):
                sp.wait_ge(s_oht, p * 2 * IT + 2 * i + h + 1)
                sp.dma_start(types_w[0:RP, h, :], types_d[bass.ds(RING * i + REL * h, REL), :].rearrange(
                    "(o s) e -> o (s e)", o=1).broadcast_to([RP, REL * P])).then_inc(s_tb[h], 16)

            def store_rows(i, h):
                sp.wait_ge(s_relc, 4 + REL * i + HALF * h + HALF)
                sp.dma_start(rel_d[bass.ds(2 * i + h, 1), :, :].rearrange("o p w -> (o p) w"),
                             relg[:, h, :, :].rearrange("p k w -> p (k w)")).then_inc(s_rst[h], 16)

            def stored(i, h):
                sp.wait_ge(s_rst[h], 16 * i + 16)
                sp.sem_inc(s_rfree, 1)

            def load_rows(i, h):
                sp.wait_ge(s_prod, RING * i + REL * h)
                sp.dma_start(relg[:, h, :, :].rearrange("p k w -> p (k w)"),
                             rel_d[bass.ds(2 * i + h, 1), :, :].rearrange("o p w -> (o p) w")).then_inc(s_rl[h], 16)

            def unordered(layer):
                sp.load(any_drop, unsorted[0:1, 0:1])
                with sp.If_ne(any_drop, 0):
                    sp.wait_ge(s_uzero, layer + 1)
                    sp.dma_start(acc_d.rearrange("(b p) w -> p b w", p=P), acc[:, :, :]).then_inc(s_uacc, 16)
                    sp.wait_ge(s_uacc, 32 * layer + 16)
                    with sp.Fori(0, SLOTS // SK) as i:
                        for k in range(SK):
                            t = SK * i + k
                            edge = edges_d[bass.ds(t, 1), :]
                            sp.dma_start(u_edge, edge.rearrange("o (n e) -> (o e) n", e=P),
                                         allow_slow_non_contiguous=True).then_inc(s_uload[k], 16)
                            sp.dma_start(u_dst, edge[:, P:2 * P].broadcast_to([P, P])).then_inc(s_uload[k], 16)
                            sp.wait_ge(s_uput[k], 16 * (layer * (SLOTS // SK) + i) + 16)
                            sp.sem_inc(s_utile, 1)
                    sp.dma_start(acc[:, :, :], acc_d.rearrange("(b p) w -> p b w", p=P)).then_inc(s_uacc, 16)
                    sp.wait_ge(s_uacc, 32 * layer + 32)

            any_drop = sp.alloc_register("any_drop_sp")
            table(0, t1_d)
            sp.wait_ge(s_typd, 16)
            load_types(0, 0, 0)
            load_types(0, 0, 1)
            load_types(0, 1, 0)
            store_rows(0, 0)
            load_types(0, 1, 1)
            stored(0, 0)
            store_rows(0, 1)
            with sp.Fori(1, IT - 1) as i:
                load_types(0, i + 1, 0)
                stored(i - 1, 1)
                store_rows(i, 0)
                load_types(0, i + 1, 1)
                stored(i, 0)
                store_rows(i, 1)
            stored(IT - 2, 1)
            store_rows(IT - 1, 0)
            stored(IT - 1, 0)
            store_rows(IT - 1, 1)
            stored(IT - 1, 1)
            unordered(0)
            table(1, t2_d)
            load_types(1, 0, 0)
            load_types(1, 0, 1)
            sp.wait_ge(s_add, SLOTS + 4)
            for h in range(2):
                sp.dma_start(relg[:, h, :, :].rearrange("p k w -> p (k w)"), rel_d[h, :, :]).then_inc(s_rl[h], 16)
            with sp.Fori(0, IT - 1) as i:
                load_types(1, i + 1, 0)
                load_rows(i + 1, 0)
                load_types(1, i + 1, 1)
                load_rows(i + 1, 1)
            unordered(1)
            sp.wait_ge(s_add, 2 * SLOTS + 4)
            sp.wait_ge(s_oht, 2 * 2 * IT + 2)
            sp.dma_start(f1, w1.rearrange("(t p) n -> p t n", p=P)).then_inc(s_fw, 16)
            sp.dma_start(f2, w2.rearrange("(t p) n -> p t n", p=P)).then_inc(s_fw, 16)
            sp.wait_ge(s_hrow, 1)
            sp.dma_start(h_d.rearrange("(b p) w -> p b w", p=P), acc[:, :, :]).then_inc(s_hd, 16)
            for c in range(NB // 7):
                sp.wait_ge(s_xh, c + 1)
                b0, full = 7 * c, min(7 * c + 7, NB - 1)
                sp.dma_start(out[b0 * P:full * P, :].rearrange("(b p) d -> p b d", p=P), X[:, b0:full, :]).then_inc(s_out, 16)
            sp.dma_start(out[(NB - 1) * P:N, :], X[0:TAIL, NB - 1, :]).then_inc(s_out, 16)
            sp.wait_ge(s_out, 16 * (NB // 7 + 1))
            sp.wait_ge(s_put, 16 * CB)

        @block.gpsimd
        def _(pool):
            pool.memset(ident[:, :], 0.0).then_inc(s_pool, 1)
            pool.memset(ones[:, :], 1.0).then_inc(s_const, 1)
            pool.iota(iof[:, :], [[1, P]], base=0, channel_multiplier=0, allow_small_or_imprecise_dtypes=True).then_inc(s_const, 1)
            pool.iota(iob[:, :], [[1, P]], base=0, channel_multiplier=0, allow_small_or_imprecise_dtypes=True).then_inc(s_const, 1)
            pool.iota(pidx[:, :], [[P, SC]], base=0, channel_multiplier=1, allow_small_or_imprecise_dtypes=True).then_inc(s_const, 1)
            pool.memset(zb[:, :], 0.0).then_inc(s_const, 1)
            pool.iota(counted, [[1, P], [0, HG]], base=0, channel_multiplier=0, allow_small_or_imprecise_dtypes=True).then_inc(s_const, 1)
            pool.memset(tri[:, :], 1.0).then_inc(s_pool, 1)
            pool.iota(valid[:, :], [[P, NB]], base=0, channel_multiplier=1, allow_small_or_imprecise_dtypes=True).then_inc(s_const, 1)
            pool.iota(shift[:, :], [[-3, DIGITS]], base=3 * (DIGITS - 1), channel_multiplier=0).then_inc(s_const, 1)
            pool.iota(digit[:, :], [[1, TRIALS]], base=1, channel_multiplier=0).then_inc(s_const, 1)
            pool.iota(tid[:, :], [[RP, RK]], base=0, channel_multiplier=1, allow_small_or_imprecise_dtypes=True).then_inc(s_const, 1)
            pool.wait_ge(s_pool, 2)
            pool.affine_select(out=tri[:, :], in_=tri[:, :], compare_op=ALU.is_gt, fill=0.0, base=0,
                               pattern=[[1, P]], channel_multiplier=-1).then_inc(s_const, 1)
            pool.affine_select(out=ident[:, :], in_=ident[:, :], compare_op=ALU.not_equal, fill=1.0, base=0,
                               pattern=[[-1, P]], channel_multiplier=1).then_inc(s_const, 1)
            pool.wait_ge(s_ed, 16)
            pool.wait_ge(s_tp, 1)
            for c in range(SC):
                pool.indirect_dma_start(slot_i[:, c, :], None, edges_d,
                                        bass.IndirectOffsetOnAxis(ap=tpi[:, c:c + 1], axis=0)).then_inc(s_slot, 16)

            pool.wait_ge(s_cvf, SC)
            pool.tensor_tensor(slot_f[:, :, 2 * P:3 * P], slot_f[:, :, 2 * P:3 * P],
                               bp128[:, :].unsqueeze(2).broadcast_to([P, SC, P]), ALU.subtract).then_inc(s_cv, 1)
            def gathers(i, layer, table):
                first = layer * SLOTS
                for k in range(RING):
                    if k % 8 == 0:
                        pool.wait_ge(s_idx, layer * (2 * IT + 2) + k // 8 + 1 + 2 * i)
                    pool.wait_ge(s_mm, first + k + 1 + RING * i)
                    pool.sem_inc(s_turn, 1)
                    pool.wait_ge(s_td, 16 * (NB // 7) * (1 + layer))
                    pool.indirect_dma_start(gath[:, k, :], None, table, bass.IndirectOffsetOnAxis(
                        ap=idxs[:, k:k + 1], axis=0)).then_inc(s_g[k], 16)

            any_drop = pool.alloc_register("any_drop_pool")

            def unordered(layer, table):
                pool.load(any_drop, unsorted[0:1, 0:1])
                with pool.If_ne(any_drop, 0):
                    with pool.Fori(0, SLOTS // SK) as i:
                        for k in range(SK):
                            n = layer * (SLOTS // SK) + i
                            pool.wait_ge(s_uload[k], 32 * n + 32)
                            pool.sem_inc(s_turn, 1)
                            pool.wait_ge(s_td, 16 * (NB // 7) * (1 + layer))
                            pool.indirect_dma_start(u_rows, None, table, bass.IndirectOffsetOnAxis(
                                ap=u_edge[:, 0:1], axis=0)).then_inc(s_urows[k], 16)
                            if layer == 1:
                                pool.wait_ge(s_relwd, 16)
                                pool.indirect_dma_start(u_rel[:, 0:DW], None, relw_d, bass.IndirectOffsetOnAxis(
                                    ap=u_edge[:, 2:3], axis=0)).then_inc(s_urows[k], 16)
                            pool.wait_ge(s_uto, layer * SLOTS + SK * i + k + 1)
                            pool.sem_inc(s_turn, 1)
                            pool.wait_ge(s_uacc, 32 * layer + 16)
                            pool.indirect_dma_start(u_old, None, acc_d, bass.IndirectOffsetOnAxis(
                                ap=u_edge[:, 1:2], axis=0)).then_inc(s_uold[k], 16)
                            pool.wait_ge(s_uadd, layer * SLOTS + SK * i + k + 1)
                            pool.sem_inc(s_turn, 1)
                            pool.wait_ge(s_uacc, 32 * layer + 16)
                            pool.indirect_dma_start(acc_d, bass.IndirectOffsetOnAxis(ap=u_edge[:, 1:2], axis=0),
                                                    u_old, None).then_inc(s_uput[k], 16)

            with pool.Fori(0, IT) as i:
                gathers(i, 0, t1_d)
            unordered(0, t1_d)
            with pool.Fori(0, IT) as i:
                gathers(i, 1, t2_d)
            unordered(1, t2_d)
            pool.wait_ge(s_hrow, 1)
            for c in range(NB // 7):
                pool.tensor_tensor(X[:, 7 * c:7 * c + 7, :], X[:, 7 * c:7 * c + 7, :], acc[:, 7 * c:7 * c + 7, 0:D],
                                   ALU.add).then_inc(s_xh, 1)
            pool.wait_ge(s_xh, NB // 7)
            pool.wait_ge(s_picked, 1)
            pool.wait_ge(s_hd, 16)
            for c in range(CB):
                if c >= 4:
                    pool.wait_ge(s_h[c % 4], 16 * (c // 4))
                pool.indirect_dma_start(hg[:, c, :], None, h_d, bass.IndirectOffsetOnAxis(
                    ap=picked[:, c:c + 1], axis=0)).then_inc(s_h[c % 4], 16)
            pool.wait_ge(s_out, 16 * (NB // 7 + 1))
            for c in range(CB):
                if c >= 4:
                    pool.wait_ge(s_base[c % 4], 16 * (c // 4))
                pool.indirect_dma_start(base[:, c, :], None, out, bass.IndirectOffsetOnAxis(
                    ap=picked[:, c:c + 1], axis=0)).then_inc(s_base[c % 4], 16)
            for k in range(4):
                pool.wait_ge(s_base[k], 16 * -(-(CB - k) // 4))
            for c in range(CB):
                rows = P if c < CB - 1 else CTAIL
                pool.wait_ge(s_fo, c + 3)
                pool.indirect_dma_start(out, bass.IndirectOffsetOnAxis(ap=picked[0:rows, c:c + 1], axis=0),
                                        base[0:rows, c, :], None).then_inc(s_put, 16)

        @block.tensor
        def _(pe):
            pe.sem_inc(s_hmm, 2)
            pe.sem_inc(s_st, 2)
            pe.sem_inc(s_mm, RING)
            pe.sem_inc(s_rel, REL)
            pe.sem_inc(s_ztp, 2)
            pe.sem_inc(s_y, 2)
            pe.sem_inc(s_uztp, 2)
            pe.sem_inc(s_uy, 2)
            pe.sem_inc(s_ftp, 2)
            pe.sem_inc(s_fy, 2)
            pe.wait_ge(s_const, 12)
            pe.wait_ge(s_cnt, 1)
            nc.tensor.matmul(psY[:, 1, 0:NB + 1], ones[:, :], cnt[:, :], start=True, stop=True).then_inc(s_lo, 1)
            pe.wait_ge(s_tp, 1)
            nc.tensor.transpose(psE[0:SC, 3, 0:P], bp[:, :], ident[:, :]).then_inc(s_bt, 1)
            nc.tensor.matmul(psY[:, 0, 0:NB], zb[:, :], zb[:, 0:NB], start=True, stop=False)
            with pe.Fori(0, SLOTS // HG // 2) as i:
                for r in range(2):
                    pe.wait_ge(s_oh, 2 * i + r + 1)
                    for t in range(HG):
                        ins = nc.tensor.matmul(psY[:, 0, 0:NB], ohlo[:, r, :, t], ohhi[:, r, :, t],
                                               start=False, stop=False)
                    ins.then_inc(s_hmm, 1)
            nc.tensor.matmul(psY[:, 0, 0:NB], zb[:, :], zb[:, 0:NB], start=False, stop=True).then_inc(s_hist, 1)
            pe.wait_ge(s_cv, 1)
            for c in range(SC):
                pe.wait_ge(s_sc, c + 1)
                for n in range(2):
                    ins = nc.tensor.transpose(psT[:, c % 2, n * P:n * P + P], slot_f[:, c, (n + 1) * P:(n + 2) * P], ident[:, :])
                ins.then_inc(s_st, 1)

            pe.wait_ge(s_kneg, 1)
            for m in range(3):
                for it in range(2):
                    for ot in range(2):
                        ins = nc.tensor.transpose(psE[:, m, it * D + ot * P:it * D + ot * P + P],
                                                  wraw[:, m, ot, it * P:it * P + P], ident[:, :])
            ins.then_inc(s_wt, 1)

            def relation(layer, i, j):
                m = REL * i + j
                if j % HALF == 0:
                    pe.wait_ge(s_oht, 2 + layer * 2 * IT + 2 * i + j // HALF + 1)
                if layer == 0:
                    pe.wait_ge(s_relc, m + 1)
                else:
                    pe.wait_ge(s_prod, RING * i + 2 * j + 2)
                for t in range(RK):
                    for part in range(3):
                        ins = nc.tensor.matmul(psR[j % 4][:, 0:DW], oht[0:RP, j // HALF, t, j % HALF, :],
                                               relb[0:RP, part, t, 0:DW], start=(t == part == 0),
                                               stop=(t == RK - 1 and part == 2))
                ins.then_inc(s_rel, 1)

            def edge_pass(layer):
                def iteration(i, last=False):
                    for k in range(RING):
                        n = layer * SLOTS + k + RING * i
                        if layer == 1 and k % 2 == 0 and k < RING - 2:
                            relation(1, i, k // 2 + 1)
                        elif layer == 1 and k == RING - 2 and not last:
                            relation(1, i + 1, 0)
                        pe.wait_ge(s_sel, n + 1)
                        if layer == 1:
                            pe.wait_ge(s_prod, 8 + RING * i + k + 1)
                        else:
                            pe.wait_ge(s_g[k], 16 * i + 16)
                        pe.wait_ge(s_add, n + 1)
                        nc.tensor.matmul(psE[:, k % 4, 0:DW], sel[:, k % 4, :], gath[:, k, 0:DW],
                                         start=True, stop=True).then_inc(s_mm, 1)
                        if layer == 0 and k % 2 == 0:
                            relation(0, i, k // 2)

                if layer == 1:
                    relation(1, 0, 0)
                with pe.Fori(0, IT - 1) as i:
                    iteration(i)
                iteration(IT - 1, last=True)

            any_drop = pe.alloc_register("any_drop_pe")

            def unordered(layer):
                pe.load(any_drop, unsorted[0:1, 0:1])
                with pe.If_ne(any_drop, 0):
                    with pe.Fori(0, SLOTS // SK) as i:
                        for k in range(SK):
                            n = layer * SLOTS + SK * i + k
                            pe.wait_ge(s_usel, n + 1)
                            if layer == 0:
                                pe.wait_ge(s_urows[k], 16 * i + 16)
                            else:
                                pe.wait_ge(s_uprod, SK * i + k + 1)
                            nc.tensor.matmul(psE[:, 0, 0:DW], sel[:, 0, :], u_rows[:, 0:DW],
                                             start=True, stop=True).then_inc(s_umm, 1)

            def dense(stage, nk, weights):
                first = stage * NB

                def turn(n, par, gap=1):
                    pe.wait_ge(s_z, n + 3)
                    pe.wait_ge(s_zts, n + gap)
                    for t in range(nk):
                        ins = nc.tensor.transpose(psT[:, par, t * P:t * P + P], zst[:, par, t * P:t * P + P], ident[:, :])
                    ins.then_inc(s_ztp, 1)

                def product(n, par, gap=1):
                    pe.wait_ge(s_zts, n + 3)
                    pe.wait_ge(s_yo, n + gap)
                    for t in range(nk):
                        ins = nc.tensor.matmul(psY[:, par, 0:D], zts[:, par, t * P:t * P + P], weights(t),
                                               start=(t == 0), stop=(t == nk - 1))
                    ins.then_inc(s_y, 1)

                turn(first, 0, gap=2)
                turn(first + 1, 1)
                product(first, 0, gap=2)
                turns = (NB - 1) // G - 1
                with pe.Fori(0, turns) as i:
                    for k in range(G):
                        n = first + 1 + G * i + k
                        turn(n + 1, k % 2)
                        product(n, (k + 1) % 2)
                for k in range(G):
                    n = first + 1 + G * turns + k
                    if k < G - 1:
                        turn(n + 1, k % 2)
                    product(n, (k + 1) % 2)

            pe.wait_ge(s_sc, SC + 2)
            edge_pass(0)
            unordered(0)
            pe.wait_ge(s_relc, REL * IT + 4)
            dense(0, 4, lambda t: (w1s if t < 2 else w2s)[:, t % 2, :])
            dense(1, 2, lambda t: wt[:, 0, t, :])
            pe.wait_ge(s_zts, 2 * NB + 2)
            pe.wait_ge(s_yo, 2 * NB + 2)
            edge_pass(1)
            unordered(1)

            base_m = 2 * NB

            def turn_m(j, r, gap=1):
                pe.wait_ge(s_z, base_m + j + 3)
                pe.wait_ge(s_zts, base_m + j + gap)
                for t in range(2):
                    ins = nc.tensor.transpose(psT[:, r, t * P:t * P + P], zst[:, r, t * P:t * P + P], ident[:, :])
                ins.then_inc(s_ztp, 1)

            def messages_and_update(j, r):
                if there(j + 1):
                    turn_m(j + 1, 1 - r)
                if there(j):
                    pe.wait_ge(s_zts, base_m + j + 3)
                    pe.wait_ge(s_yo, base_m + j + (2 if isinstance(j, int) and j == 0 else 1))
                    for t in range(2):
                        ins = nc.tensor.matmul(psY[:, r, 0:D], zts[:, r, t * P:t * P + P], wt[:, 1, t, :],
                                               start=(t == 0), stop=(t == 1))
                    ins.then_inc(s_y, 1)
                if there(j - 1):
                    pe.wait_ge(s_uz, j + 2)
                    pe.wait_ge(s_uzts, j)
                    for t in range(2):
                        ins = nc.tensor.transpose(psE[:, 1 - r, t * P:t * P + P], zst[:, 1 - r, D + t * P:D + t * P + P],
                                                  ident[:, :])
                    ins.then_inc(s_uztp, 1)
                if there(j - 2):
                    pe.wait_ge(s_uzts, j + 1)
                    pe.wait_ge(s_uyo, j - 1)
                    for t in range(2):
                        ins = nc.tensor.matmul(psE[:, 2 + r, 0:D], zts[:, r, D + t * P:D + t * P + P], wt[:, 2, t, :],
                                               start=(t == 0), stop=(t == 1))
                    ins.then_inc(s_uy, 1)

            turn_m(0, 0, gap=2)
            steps(pe, messages_and_update)

            with pe.Fori(0, COUNTS) as i:
                pe.wait_ge(s_hits, i + 1)
                nc.tensor.matmul(psE[:, 0, 0:TRIALS], ones[:, :], hits[:, :], start=True, stop=True).then_inc(s_total, 1)
            for n, marks in enumerate((tie, pick)):
                pe.wait_ge(s_hits, COUNTS + 1 + n)
                nc.tensor.matmul(psE[:, 1, 0:NB], tri[:, :], marks[:, :], start=True, stop=True)
                nc.tensor.matmul(psE[:, 2, 0:NB], ones[:, :], marks[:, :], start=True, stop=True).then_inc(s_total, 1)
            pe.wait_ge(s_place, 1)
            for b in range(NB):
                ins = nc.tensor.matmul(psE[:, 3, 0:2 * CB], place_lo[:, b, :],
                                       place_w[:, b, :, :].rearrange("p q h -> p (q h)"),
                                       start=(b == 0), stop=(b == NB - 1))
            ins.then_inc(s_list, 1)

            def turn(m, par, blocks=2):
                pe.wait_ge(s_fz, m + 3)
                pe.wait_ge(s_fts, m + 1)
                for t in range(2):
                    for q in range(blocks):
                        ins = nc.tensor.transpose(psT[:, par, (2 * t + q) * P:(2 * t + q) * P + P],
                                                  zst[:, par, q * D + t * P:q * D + t * P + P], ident[:, :])
                ins.then_inc(s_ftp, 1)

            def feed(m, par, blocks=2):
                w = blocks * P
                pe.wait_ge(s_fts, m + 3)
                for ht in range(HT):
                    pe.wait_ge(s_hs, HT * m + ht + 1)
                    for t in range(2):
                        ins = nc.tensor.matmul(psE[:, ht % 4, 0:w], f1[:, t, ht * P:ht * P + P],
                                               zts[:, par, 2 * t * P:2 * t * P + w], start=(t == 0), stop=(t == 1))
                    ins.then_inc(s_hp, 1)
                for q in range(blocks):
                    pe.wait_ge(s_fc, 2 * m + q + 1)
                    for ht in range(HT):
                        pe.wait_ge(s_hs, HT * m + ht + 5)
                        ins = nc.tensor.matmul(psY[:, q, 0:D], hid[:, par, ht, q * P:q * P + P], f2[:, ht, :],
                                               start=(ht == 0), stop=(ht == HT - 1))
                    ins.then_inc(s_fy, 1)

            pe.wait_ge(s_fw, 32)
            turn(0, 0)
            with pe.Fori(0, FI // 2 - 1) as i:
                turn(2 * i + 1, 1)
                feed(2 * i, 0)
                turn(2 * i + 2, 0)
                feed(2 * i + 1, 1)
            turn(FI - 2, 1)
            feed(FI - 3, 0)
            turn(FI - 1, 0, 1)
            feed(FI - 2, 1)
            feed(FI - 1, 0, 1)

        @block.scalar
        def _(act):
            act.sem_inc(s_sc, 2)
            act.sem_inc(s_zts, 2)
            act.sem_inc(s_uzts, 2)
            act.sem_inc(s_ssq, 1)
            act.sem_inc(s_hs, 4)
            act.sem_inc(s_relc, 4)
            act.wait_ge(s_const, 12)
            act.wait_ge(s_sq, 1)
            nc.scalar.activation(glog[0:RP, :], glog[0:RP, :], ACT.Sigmoid, bias=gb[0:RP, :]).then_inc(s_sqd, 1)
            act.wait_ge(s_slot, 16 * SC)
            act.wait_ge(s_hl, 1)
            for c in range(SC):
                nc.scalar.copy(slot_f[:, c, P:3 * P], slot_i[:, c, 0:2 * P]).then_inc(s_cvf, 1)
            nc.scalar.copy(types_h, slot_i[:, :, 2 * P:3 * P]).then_inc(s_typ, 1)
            act.wait_ge(s_sq, 2)
            nc.scalar.activation(degu[:, :], degu[:, :], ACT.Sqrt).then_inc(s_sqd, 1)
            act.wait_ge(s_hist, 1)
            nc.scalar.copy(srci[:, SLOTS:SLOTS + RING], zb[:, 0:RING])
            for c in range(SC):
                act.wait_ge(s_st, c + 3)
                nc.scalar.copy(srci[:, bass.ts(c, P)], psT[:, c % 2, 0:P])
                nc.scalar.copy(dstf[:, bass.ts(c, P)], psT[:, c % 2, P:2 * P]).then_inc(s_sc, 1)
            act.wait_ge(s_sq, 3)
            nc.scalar.activation(rstd[:, :], rstd[:, :], ACT.Sqrt).then_inc(s_sqd, 1)

            def edge_pass(layer):
                def indices(i, h):
                    act.wait_ge(s_mm, layer * SLOTS + 8 * h + 8 + RING * i)
                    nc.scalar.copy(idxs[:, 8 * h:8 * h + 8], srci[:, bass.ds(RING * i + 8 * h, 8)]).then_inc(s_idx, 1)

                indices(0, 0)
                indices(0, 1)
                act.wait_ge(s_td, (layer + 1) * 16 * (NB // 7))
                nc.scalar.copy(accf[:, ZW:NB * W], zb[:, 0:1].broadcast_to([P, NB * W - ZW])).then_inc(s_zero, 1)
                with act.Fori(0, IT) as i:
                    for h in range(2):
                        if layer == 0:
                            act.wait_ge(s_rfree, 2 * i + h + 1)
                            for j in range(HALF):
                                m = REL * i + HALF * h + j
                                act.wait_ge(s_rel, REL + m + 1)
                                nc.scalar.copy(relg[:, h, j, :], psR[j][:, 0:DW]).then_inc(s_relc, 1)
                        indices(i + 1, h)

            def squares(b):
                act.wait_ge(s_ssq, b + 1)
                act.wait_ge(s_emb, b + 1)
                nc.scalar.activation(sqj[:, :], acc[:, b, 0:D], ACT.Square,
                                     accum_out=ssq[:, bass.ds(b, 1)]).then_inc(s_ssq, 1)

            def dense(stage, nk):
                def copy(n, par, gap=1):
                    act.wait_ge(s_ztp, n + 3)
                    act.wait_ge(s_y, n + gap)
                    nc.scalar.copy(zts[:, par, 0:nk * P], psT[:, par, 0:nk * P]).then_inc(s_zts, 1)

                copy(stage * NB, 0, gap=2)
                copy(stage * NB + 1, 1)
                copy(stage * NB + 2, 0)
                with act.Fori(0, (NB - 1) // G - 1) as i:
                    for k in range(G):
                        copy(stage * NB + 3 + G * i + k, (k + 1) % 2)
                        if stage == 0:
                            squares(G * i + k)
                done = G * ((NB - 1) // G - 1)
                for b in range(done, NB):
                    if b + 3 < NB:
                        copy(stage * NB + b + 3, (b + 1) % 2)
                    if stage == 0:
                        squares(b)

            act.wait_ge(s_sc, SC + 2)
            edge_pass(0)
            act.wait_ge(s_sq, 4)
            nc.scalar.activation(inq[:, :], inq[:, :], ACT.Sqrt).then_inc(s_sqd, 1)
            dense(0, 4)
            act.wait_ge(s_sq, 5)
            nc.scalar.activation(ssq[:, :], ssq[:, :], ACT.Sqrt).then_inc(s_sqd, 1)
            act.wait_ge(s_sq, 6)
            nc.scalar.activation(rstd[:, :], rstd[:, :], ACT.Sqrt).then_inc(s_sqd, 1)
            dense(1, 2)
            act.wait_ge(s_sq, 7)
            nc.scalar.activation(rstd[:, :], rstd[:, :], ACT.Sqrt).then_inc(s_sqd, 1)
            edge_pass(1)

            base_m = 2 * NB

            def rows_m(j, r):
                act.wait_ge(s_ztp, base_m + j + 1)
                nc.scalar.copy(zst[:, r, 0:D], acc[:, j, 0:D]).then_inc(s_z, 1)

            def turned_m(j, r, gap=1):
                act.wait_ge(s_ztp, base_m + j + 3)
                act.wait_ge(s_y, base_m + j + gap)
                nc.scalar.copy(zts[:, r, 0:D], psT[:, r, 0:D]).then_inc(s_zts, 1)

            def messages_and_update(j, r):
                if there(j + 2):
                    rows_m(j + 2, r)
                if there(j + 1):
                    turned_m(j + 1, 1 - r)
                if there(j - 1):
                    act.wait_ge(s_uztp, j + 2)
                    act.wait_ge(s_uy, j)
                    nc.scalar.copy(zts[:, 1 - r, D:2 * D], psE[:, 1 - r, 0:D]).then_inc(s_uzts, 1)

            act.wait_ge(s_acc, 1)
            rows_m(0, 0)
            rows_m(1, 1)
            turned_m(0, 0, gap=2)
            steps(act, messages_and_update)
            act.wait_ge(s_sq, 8)
            nc.scalar.activation(rstd[:, :], rstd[:, :], ACT.Sqrt).then_inc(s_sqd, 1)

            def feed(m, par, blocks=2):
                w = blocks * P
                for ht in range(HT):
                    act.wait_ge(s_hp, HT * m + ht + 1)
                    nc.scalar.activation(hid[:, par, ht, 0:w], psE[:, ht % 4, 0:w], ACT.Gelu_apprx_tanh,
                                         bias=b1s[:, ht:ht + 1]).then_inc(s_hs, 1)

            with act.Fori(0, FI // 2) as i:
                feed(2 * i, 0)
                feed(2 * i + 1, 1)
            feed(FI - 1, 0, 1)

        @block.vector
        def _(dve):
            v = nc.vector
            link = Chain(dve, s_dve)
            roots = [0]
            places = [dve.alloc_register(f"place{k}") for k in range(RING)]

            def root(t, ahead):
                roots[0] += 1
                ahead.then_inc(s_sq, 1)
                dve.wait_ge(s_sqd, roots[0])
                link(v.reciprocal(t, t))

            dve.sem_inc(s_add, 4)
            dve.sem_inc(s_z, 2)
            dve.sem_inc(s_uz, 2)
            dve.sem_inc(s_uyo, 2)
            dve.sem_inc(s_yo, 2)
            dve.sem_inc(s_fz, 2)
            dve.sem_inc(s_fts, 2)
            dve.sem_inc(s_fo, 2)
            dve.sem_inc(s_fc, 2)
            dve.sem_inc(s_oht, 2)
            dve.sem_inc(s_prod, 8)
            v.memset(X[:, NB - 1, :], 0.0)
            v.memset(raw[:, FULLC, 0:P], PAD_SRC)
            v.memset(raw[:, FULLC, P:2 * P], PAD_DST)
            v.memset(raw[:, FULLC, 2 * P:3 * P], 0).then_inc(s_pad, 1)

            def moments():
                link(v.tensor_tensor(sm0[:, :], st[:, :, 1], st[:, :, 4], ALU.add))
                link(v.tensor_scalar(mean[:, :], sm0[:, :], 0.5, None, ALU.mult))
                link(v.tensor_tensor(sm0[:, :], st[:, :, 1], st[:, :, 4], ALU.subtract))
                link(v.tensor_tensor(sm0[:, :], sm0[:, :], sm0[:, :], ALU.mult))
                link(v.tensor_tensor(sm1[:, :], st[:, :, 2], st[:, :, 5], ALU.add))
                link(v.tensor_scalar(sm1[:, :], sm1[:, :], 1.0 / D, EPS, ALU.mult, ALU.add))
                root(rstd[:, :], v.scalar_tensor_tensor(rstd[:, :], sm0[:, :], 0.25, sm1[:, :], ALU.mult, ALU.add))

            def normed(out, b):
                return v.tensor_scalar(out, X[:, b, :], mean[:, bass.ds(b, 1)], rstd[:, bass.ds(b, 1)],
                                       ALU.subtract, ALU.mult)

            dve.wait_ge(s_gw, 16 * 3)
            q = RP
            for k in range(4):
                link(v.tensor_tensor(gprod[0:q, 0, :].rearrange("p (b c) -> p b c", b=4),
                                     rel_sb[0:q, k, 0:D].rearrange("p (b c) -> p b c", b=4),
                                     gw[0:q, :].rearrange("p (c b) -> p b c", b=4), ALU.mult))
                ins = v.tensor_reduce(glog[0:q, k:k + 1], gprod[0:q, 0, :], AX, ALU.add)
                if k < 3:
                    link(ins)
            ins.then_inc(s_sq, 1)
            roots[0] += 1
            dve.wait_ge(s_sqd, roots[0])
            for k in range(4):
                v.tensor_scalar(rel_sb[0:q, k, 0:D], rel_sb[0:q, k, 0:D], glog[0:q, k:k + 1], None, ALU.mult)
                ins = v.tensor_copy(rel_sb[0:q, k, D:DW], glog[0:q, k:k + 1])
            link(ins)
            v.memset(glog[0:1, 0:1], 0.0).then_inc(s_relw, 1)
            for part in range(3):
                link(v.tensor_copy(relb[0:q, part, :, 0:DW], rel_sb[0:q, :, :]))
                if part == 0:
                    dve.wait_ge(s_relwd, 16)
                if part < 2:
                    link(v.tensor_tensor(rel_sb[0:q, :, :], rel_sb[0:q, :, :], relb[0:q, part, :, 0:DW], ALU.subtract))

            v.memset(prv[0:1, 0:1].bitcast(I32), 0)
            dve.wait_ge(s_const, 12)
            dve.wait_ge(s_raw, 16 * 9)
            v.tensor_copy(last[:, :], raw[:, :, 2 * P - 1])
            link(v.tensor_scalar(b128[:, :], iof[:, 0:NB], float(P), None, ALU.mult))
            link(v.tensor_tensor(cmp1[:, :, :], last[:, :].unsqueeze(1).broadcast_to([P, NB, SC]),
                                 b128[:, :].unsqueeze(2).broadcast_to([P, NB, SC]), ALU.is_lt))
            v.tensor_reduce(cnt[:, 0:NB], cmp1[:, :, :], AX, ALU.add)
            heads = raw[:, :, P:2 * P]
            v.scalar_tensor_tensor(descent, heads[:, :, 1:P], 1.0, heads[:, :, 0:P - 1], ALU.mult, ALU.is_lt,
                                   accum_out=drops[:, 0:1])
            dve.wait_ge(s_prv, 32)
            link(v.scalar_tensor_tensor(tpf[:, :], heads[:, :, 0], 1.0, prv[:, :].bitcast(I32), ALU.mult, ALU.is_lt,
                                        accum_out=drops[:, 1:2]))
            v.tensor_tensor(cnt[:, NB:NB + 1], drops[:, 0:1], drops[:, 1:2], ALU.add).then_inc(s_cnt, 1)
            dve.wait_ge(s_lo, 1)
            v.tensor_copy(unsorted[:, :], psY[:, 1, NB:NB + 1])
            link(v.tensor_tensor(sbs[:, :], psY[:, 1, 0:NB], iof[:, 0:NB], ALU.add))
            link(v.tensor_tensor(cmp2[:, :, :], sbs[:, 1:NB].unsqueeze(1).broadcast_to([P, SC, NB - 1]),
                                 pidx[:, :].unsqueeze(2).broadcast_to([P, SC, NB - 1]), ALU.is_le))
            link(v.tensor_reduce(bp[:, :], cmp2[:, :, :], AX, ALU.add))
            link(v.tensor_tensor(tpf[:, :], pidx[:, :], bp[:, :], ALU.subtract))
            v.tensor_scalar(bp128[:, :], bp[:, :], float(P), None, ALU.mult)
            v.tensor_copy(tpi[:, :], tpf[:, :]).then_inc(s_tp, 1)
            dve.wait_ge(s_bt, 1)
            v.tensor_copy(bti[:, :], psE[0:SC, 3, 0:P]).then_inc(s_bti, 1)

            v.tensor_scalar(lo_i, raw[:, :, 0:P], P - 1, None, ALU.bitwise_and)
            link(v.tensor_scalar(hi_i, raw[:, :, 0:P], 7, None, ALU.logical_shift_right))
            v.tensor_copy(hhi, dstf[:, :].bitcast(I32))
            v.tensor_copy(hlo.rearrange("p (c e) -> p c e", e=P), lo_i).then_inc(s_hl, 1)
            dve.wait_ge(s_hl, 1)
            with dve.Fori(0, SLOTS // HG // 2) as i:
                for r in range(2):
                    n = 2 * i + r
                    dve.wait_ge(s_hmm, n + 1)
                    for one_hot, bits, wide in ((ohlo, hlo, P), (ohhi, hhi, NB)):
                        ins = v.tensor_tensor(one_hot[:, r, :, :],
                                              bits[:, bass.ds(HG * n, HG)].unsqueeze(1).broadcast_to([P, wide, HG]),
                                              counted[:, 0:wide, :], ALU.is_equal)
                    ins.then_inc(s_oh, 1)

            dve.wait_ge(s_hist, 1)
            root(degu[:, :], v.tensor_scalar(degu[:, :], psY[:, 0, 0:NB], 1.0, None, ALU.max))
            dve.wait_ge(s_w, 16 * (3 + 32 + 8))
            for m in (1, 2):
                for bo, bi in ((0, 3), (1, 2), (2, 3)):
                    p0 = 64 * (bo % 2)
                    a = wraw[p0:p0 + 64, m, bo // 2, 64 * bi:64 * bi + 64]
                    ins = v.tensor_scalar(a, a, -1.0, None, ALU.mult)
            ins.then_inc(s_kneg, 1)

            dve.wait_ge(s_x, 32)
            with dve.Fori(0, NB // U) as i:
                for k in range(U):
                    v.bn_stats(st[:, U * i + k, :], X[:, U * i + k, :])
            link(v.memset(junk[:, 0, 0:1], 0.0))
            moments()

            dve.wait_ge(s_wt, 1)
            v.tensor_copy(wt[:, :, :, :].rearrange("p m t i -> p m (t i)"), psE[:, 0:3, :]).then_inc(s_wc, 1)

            dve.wait_ge(s_sc, SC + 2)
            dve.wait_ge(s_wc, 1)
            dve.wait_ge(s_typd, 16)
            link(v.memset(acc[:, :, D:W], 1.0))
            link(v.tensor_tensor(rdeg[:, :], rstd[:, :], degu[:, :], ALU.mult))
            for b in range(NB):
                v.tensor_scalar(acc[:, b, 0:D], X[:, b, :], mean[:, b:b + 1], rdeg[:, b:b + 1],
                                ALU.subtract, ALU.mult).then_inc(s_trow, 1)
            dve.wait_ge(s_td, 16 * (NB // 7))
            v.memset(accf[:, 0:ZW], 0.0).then_inc(s_zero, 1)
            dve.wait_ge(s_zero, 2)
            dve.wait_ge(s_brow, 16)

            def edge_pass(layer):
                def one_hots(i, h):
                    dve.wait_ge(s_tb[h], 16 * (layer * IT + i + 1))
                    dve.wait_ge(s_rel, layer * REL * IT + REL * i + HALF * h + HALF)
                    for t in range(RK):
                        ins = v.tensor_scalar(oht[0:RP, h, t, :, :], types[0:RP, h, layer, :, :], tid[0:RP, t:t + 1],
                                              None, ALU.is_equal)
                    ins.then_inc(s_oht, 1)

                def ahead(i, k):
                    n = layer * SLOTS + k + RING * i
                    dve.wait_ge(s_mm, n - 4 + RING + 1)
                    v.tensor_scalar(sel[:, k % 4, :], iof[:, :], dstf[:, bass.ds(RING * i + k, 1)], None,
                                    ALU.is_equal).then_inc(s_sel, 1)
                    if layer == 1:
                        dve.wait_ge(s_g[k], 16 * IT + 16 * i + 16)
                        if k % 2 == 0:
                            dve.wait_ge(s_rl[k // REL], 16 * i + 16)
                            factor = relg[:, k // REL, k % REL // 2, :]
                        else:
                            dve.wait_ge(s_rel, REL + REL * IT + REL * i + k // 2 + 1)
                            factor = psR[k // 2 % 4][:, 0:DW]
                        v.tensor_tensor(gath[:, k, 0:DW], gath[:, k, 0:DW], factor, ALU.mult).then_inc(s_prod, 1)

                def iteration(i, last=False):
                    dve.load(places, brow[0:1, bass.ds(RING * i, RING)])
                    for k in range(RING):
                        if k < RING - LEAD:
                            ahead(i, k + LEAD)
                        elif not last:
                            ahead(i + 1, k + LEAD - RING)
                        n = layer * SLOTS + k + RING * i
                        b = dve.snap(places[k], min_val=0, max_val=NB - 1)
                        dve.wait_ge(s_mm, n + RING + 1)
                        dve.wait_ge(s_add, n + 4)
                        v.tensor_tensor(acc[:, b, 0:DW], acc[:, b, 0:DW], psE[:, k % 4, 0:DW],
                                        ALU.add).then_inc(s_add, 1)
                        if k == 1:
                            one_hots(i, 1)
                        if k == 9 and not last:
                            one_hots(i + 1, 0)

                one_hots(0, 0)
                for k in range(LEAD):
                    ahead(0, k)
                with dve.Fori(0, IT - 1) as i:
                    iteration(i)
                iteration(IT - 1, last=True)

            any_drop = dve.alloc_register("any_drop_dve")

            def unordered(layer):
                dve.load(any_drop, unsorted[0:1, 0:1])
                with dve.If_ne(any_drop, 0):
                    v.memset(accf[:, :], 0.0).then_inc(s_uzero, 1)
                    with dve.Fori(0, SLOTS // SK) as i:
                        for k in range(SK):
                            n = layer * SLOTS + SK * i + k
                            dve.wait_ge(s_uload[k], 32 * (layer * (SLOTS // SK) + i) + 32)
                            v.tensor_copy(u_dstf, u_dst)
                            v.tensor_copy(u_own, u_edge[:, 1:2]).then_inc(s_uown, 1)
                            dve.wait_ge(s_uown, n + 1)
                            v.tensor_scalar(u_edge[:, 1:2], u_edge[:, 1:2], PAD_SRC, None, ALU.min).then_inc(s_uto, 1)
                            v.tensor_scalar(sel[:, 0, :], u_dstf, u_own, None, ALU.is_equal).then_inc(s_usel, 1)
                            if layer == 1:
                                dve.wait_ge(s_urows[k], 16 * (SLOTS // SK) + 32 * i + 32)
                                v.tensor_tensor(u_rows[:, 0:DW], u_rows[:, 0:DW], u_rel[:, 0:DW],
                                                ALU.mult).then_inc(s_uprod, 1)
                            dve.wait_ge(s_uold[k], 16 * (layer * (SLOTS // SK) + i) + 16)
                            dve.wait_ge(s_umm, n + 1)
                            v.tensor_tensor(u_old[:, 0:DW], u_old[:, 0:DW], psE[:, 0, 0:DW], ALU.add).then_inc(s_uadd, 1)
                    dve.wait_ge(s_uacc, 32 * layer + 32)

            edge_pass(0)
            dve.wait_ge(s_add, SLOTS + 4)
            unordered(0)

            v.tensor_scalar(has[:, :], acc[:, :, D], 0.0, None, ALU.is_gt)
            root(inq[:, :], v.tensor_scalar(inq[:, :], acc[:, :, D], 1.0, None, ALU.max))

            def sweep(stage, rows, step, after=None):
                dve.wait_ge(s_ztp, stage * NB + 2)
                rows(0, 0)
                rows(1, 1)
                settle()
                if after:
                    after()
                    settle()
                step(0, 0, first=True)
                turns = (NB - 1) // G - 1
                with dve.Fori(0, turns) as i:
                    for k in range(G):
                        step(1 + G * i + k, (1 + k) % 2)
                for k in range(G):
                    step(1 + G * turns + k, (1 + k) % 2, left=G - 1 - k)

            def freed(stage, j):
                dve.wait_ge(s_ztp, stage * NB + j + 1)

            def product(stage, j):
                dve.wait_ge(s_y, stage * NB + j + 3)

            def taken(stage, j):
                dve.wait_ge(s_yo, stage * NB + j + 3)

            def settle():
                link(v.memset(glog[:, 0:1], 0.0))

            def rows0(j, r):
                deg_j = degu[:, bass.ds(j, 1)]
                v.scalar_tensor_tensor(zst[:, r, 0:D], acc[:, j, 0:D], deg_j, tmp[:, r, :], ALU.mult, ALU.add)
                v.scalar_tensor_tensor(zst[:, r, D:2 * D], acc[:, j, 0:D], deg_j, tmp[:, r, :],
                                       ALU.mult, ALU.mult).then_inc(s_z, 1)

            def step0(j, r, first=False, left=G):
                if left > 1:
                    freed(0, j + 2)
                    rows0(j + 2, r)
                if left > 2:
                    normed(tmp[:, 1 - r, :], j + 3)
                product(0, j)
                v.scalar_tensor_tensor(gprod[:, r, :], psY[:, r, 0:D], has[:, bass.ds(j, 1)], b0s[:, :],
                                       ALU.mult, ALU.add).then_inc(s_yo, 1)
                taken(0, j)
                v.scalar_tensor_tensor(acc[:, j, 0:D], gprod[:, r, :], 0.01, gprod[:, r, :],
                                       ALU.mult, ALU.max).then_inc(s_emb, 1)

            normed(tmp[:, 0, :], 0)
            normed(tmp[:, 1, :], 1)
            settle()
            sweep(0, rows0, step0, lambda: normed(tmp[:, 0, :], 2))
            settle()
            dve.wait_ge(s_ssq, NB + 1)

            roots[0] += 1
            dve.sem_inc(s_sq, 1)
            dve.wait_ge(s_sqd, roots[0])
            link(v.tensor_scalar(ssq[:, :], ssq[:, :], 1e-12, None, ALU.max))
            link(v.reciprocal(ssq[:, :], ssq[:, :]))
            with dve.Fori(0, NB // U) as i:
                link.enter(i, 1)
                for k in range(U):
                    b = U * i + k
                    ins = v.scalar_tensor_tensor(X[:, b, :], acc[:, b, 0:D], ssq[:, bass.ds(b, 1)], X[:, b, :],
                                                 ALU.mult, ALU.add)
                link(ins)
                for k in range(U):
                    v.bn_stats(st[:, U * i + k, :], X[:, U * i + k, :])
                link.leave(NB // U)
            settle()
            moments()

            def rows1(j, r):
                normed(zst[:, r, 0:D], j).then_inc(s_z, 1)

            def moments_of(j):
                v.bn_stats(st[:, j, :], X[:, j, :])

            def step1(j, r, first=False, left=G):
                if left > 1:
                    freed(1, j + 2)
                    rows1(j + 2, r)
                product(1, j)
                v.tensor_tensor(gprod[:, r, :], psY[:, r, 0:D], bfs[:, :], ALU.add).then_inc(s_yo, 1)
                taken(1, j)
                v.tensor_tensor(X[:, j, :], X[:, j, :], gprod[:, r, :], ALU.add)
                if not first:
                    moments_of(j - 1)

            sweep(1, rows1, step1)
            settle()
            moments_of(NB - 1)
            settle()
            moments()

            link(v.tensor_copy(acc[:, :, D], degu[:, :]))
            link(v.tensor_tensor(rdeg[:, :], rstd[:, :], degu[:, :], ALU.mult))
            for b in range(NB):
                v.tensor_scalar(acc[:, b, 0:D], X[:, b, :], mean[:, b:b + 1], rdeg[:, b:b + 1],
                                ALU.subtract, ALU.mult).then_inc(s_trow, 1)
            dve.wait_ge(s_td, 2 * 16 * (NB // 7))
            v.memset(accf[:, 0:ZW], 0.0).then_inc(s_zero, 1)
            dve.wait_ge(s_zero, 4)
            edge_pass(1)
            dve.wait_ge(s_add, 2 * SLOTS + 4)
            unordered(1)

            dve.sem_inc(s_acc, 1)

            def messages_and_update(j, r):
                if there(j):
                    product(2, j)
                    v.scalar_tensor_tensor(gprod[:, r, :], mbs[:, :], acc[:, j, D:DW], psY[:, r, 0:D],
                                           ALU.mult, ALU.add).then_inc(s_yo, 1)
                    if there(j + 1):
                        dve.wait_ge(s_uz, j + 2)
                        normed(tmp[:, 1 - r, :], j + 1)
                    dve.wait_ge(s_uztp, j + 1)
                    taken(2, j)
                    v.scalar_tensor_tensor(zst[:, r, D:2 * D], gprod[:, r, :], inq[:, bass.ds(j, 1)], tmp[:, r, :],
                                           ALU.mult, ALU.add).then_inc(s_uz, 1)
                if not there(j):
                    settle()
                if there(j - 2):
                    dve.wait_ge(s_uy, j + 1)
                    v.tensor_tensor(sqj[:, :], psE[:, 2 + r, 0:D], ubs[:, :], ALU.add).then_inc(s_uyo, 1)
                if there(j - 3):
                    moments_of(j - 3)
                if there(j - 2):
                    dve.wait_ge(s_uyo, j + 1)
                    xj = X[:, j - 2, :].rearrange("p (c a) -> p c a", a=4)
                    v.tensor_tensor(xj, xj, sqj[:, :].rearrange("p (a c) -> p c a", a=4), ALU.add)

            normed(tmp[:, 0, :], 0)
            settle()
            steps(dve, messages_and_update)
            settle()
            moments()

            with dve.Fori(0, NB // U) as i:
                link.enter(i, 1)
                for k in range(U):
                    ins = normed(acc[:, U * i + k, 0:D], U * i + k)
                link(ins)
                for k in range(U):
                    v.scalar_tensor_tensor((junk if k < 4 else junk2)[:, k % 4, :], acc[:, U * i + k, 0:D], 1.0, wrs[:, :],
                                           ALU.mult, ALU.mult, accum_out=score[:, bass.ds(U * i + k, 1)])
                link.leave(NB // U)
            settle()
            link(v.tensor_scalar(valid[:, :], valid[:, :], float(N), None, ALU.is_lt))
            link(v.tensor_scalar(score[:, :], score[:, :], brs[:, :], None, ALU.add))
            v.tensor_copy(acc[:, :, D], score[:, :]).then_inc(s_hrow, 1)
            v.memset(hits[:, :], 0.0)
            link(v.memset(thr[:, :], 0.0))
            link(v.tensor_tensor(digits[:, :, :], digit[:, :].unsqueeze(1).broadcast_to([P, DIGITS, TRIALS]),
                                 shift[:, :].unsqueeze(2).broadcast_to([P, DIGITS, TRIALS]), ALU.logical_shift_left))
            link(v.tensor_copy(unit[:, :], digits[:, :, 0]))

            v.scalar_tensor_tensor(flag[:, :], score[:, :], thr[:, :], valid[:, :], ALU.is_ge, ALU.mult,
                                   accum_out=hits[:, 0:1]).then_inc(s_hits, 1)
            dve.wait_ge(s_total, 1)
            link(v.tensor_scalar(need[:, :], psE[:, 0, 0:1], float(TOP), None, ALU.is_ge))
            v.tensor_scalar(sign[:, :], need[:, :], 2.0, -1.0, ALU.mult, ALU.add)
            link(v.tensor_scalar(want[:, :], need[:, :], float(2 * TOP - N - 1), float(N - TOP + 1), ALU.mult, ALU.add))
            v.tensor_scalar(flag[:, :], valid[:, :], 1.0, None, ALU.subtract)
            link(v.scalar_tensor_tensor(keyed[:, :], score[:, :], sign[:, :], valid[:, :], ALU.mult, ALU.mult))
            link(v.tensor_tensor(keyed[:, :], keyed[:, :], flag[:, :], ALU.add))
            v.tensor_scalar(flag[:, :], keyed[:, :], 2.0, 0.0, ALU.is_ge, ALU.add,
                            accum_out=hits[:, 0:1]).then_inc(s_hits, 1)
            dve.wait_ge(s_total, 2)
            link(v.tensor_scalar(gain[:, :], psE[:, 0, 0:1], want[:, :], None, ALU.is_ge))
            link(v.tensor_scalar(found[:, :], gain[:, :], 2.0, None, ALU.mult))
            found_i = found[:, :].bitcast(I32)
            with dve.Fori(0, DIGITS) as i:
                link.enter(i, 5)
                link(v.tensor_tensor(trial[:, :], found_i.broadcast_to([P, TRIALS]),
                                     digits[:, bass.ds(i, 1), :].rearrange("p o t -> p (o t)"), ALU.bitwise_or))
                link(v.tensor_tensor(reach, keyed[:, :].unsqueeze(1).broadcast_to([P, TRIALS, NB]),
                                     trial[:, :].bitcast(F32).unsqueeze(2).broadcast_to([P, TRIALS, NB]), ALU.is_ge))
                v.tensor_reduce(hits[:, :], reach, AX, ALU.add).then_inc(s_hits, 1)
                dve.wait_ge(s_total, i + 3)
                link(v.scalar_tensor_tensor(reach[:, :, 0], psE[:, 0, 0:TRIALS], want[:, :],
                                            unit[:, bass.ds(i, 1)].broadcast_to([P, TRIALS]),
                                            ALU.is_ge, ALU.mult, accum_out=gain[:, :]))
                link(v.tensor_copy(gain_i[:, :], gain[:, :]))
                link(v.tensor_tensor(found_i, found_i, gain_i[:, :], ALU.bitwise_or))
                link.leave(DIGITS)
            link(v.tensor_tensor(thr[:, :], found[:, :], sign[:, :], ALU.mult))
            v.scalar_tensor_tensor(pick[:, :], score[:, :], thr[:, :], valid[:, :], ALU.is_gt, ALU.mult,
                                   accum_out=hits[:, 0:1]).then_inc(s_hits, 1)
            dve.wait_ge(s_total, COUNTS)
            v.tensor_scalar(need[:, :], psE[:, 0, 0:1], -1.0, float(TOP), ALU.mult, ALU.add)
            v.scalar_tensor_tensor(tie[:, :], score[:, :], thr[:, :], valid[:, :], ALU.is_equal, ALU.mult).then_inc(s_hits, 1)
            dve.wait_ge(s_total, COUNTS + 1)
            link(v.tensor_copy(sm0[:, :], psE[:, 2, 0:NB]))
            link(v.tensor_tensor_scan(sm1[:, :], ones[:, 0:NB], sm0[:, :], 0.0, ALU.mult, ALU.add))
            link(v.tensor_tensor(sm1[:, :], sm1[:, :], sm0[:, :], ALU.subtract))
            link(v.tensor_tensor(sm1[:, :], sm1[:, :], psE[:, 1, 0:NB], ALU.add))
            link(v.scalar_tensor_tensor(sm1[:, :], sm1[:, :], need[:, :], tie[:, :], ALU.is_lt, ALU.mult))
            v.tensor_tensor(pick[:, :], pick[:, :], sm1[:, :], ALU.add).then_inc(s_hits, 1)

            dve.wait_ge(s_total, COUNTS + 2)
            link(v.tensor_copy(sm0[:, :], psE[:, 2, 0:NB]))
            link(v.tensor_tensor_scan(sm1[:, :], ones[:, 0:NB], sm0[:, :], 0.0, ALU.mult, ALU.add))
            link(v.tensor_tensor(sm1[:, :], sm1[:, :], sm0[:, :], ALU.subtract))
            link(v.tensor_tensor(sm1[:, :], sm1[:, :], psE[:, 1, 0:NB], ALU.add))
            link(v.scalar_tensor_tensor(sm1[:, :], pick[:, :], float(-OUT_OF_REACH), sm1[:, :], ALU.mult, ALU.add))
            link(v.tensor_scalar(place[:, :], sm1[:, :], float(OUT_OF_REACH), None, ALU.add))
            v.tensor_scalar(part_i[:, 0, :], place[:, :], P - 1, None, ALU.bitwise_and)
            link(v.tensor_scalar(part_i[:, 1, :], place[:, :], 7, None, ALU.logical_shift_right))
            link(v.tensor_copy(part_b[:, :, :], part_i[:, :, :]))
            link(v.tensor_tensor(place_hi, part_b[:, 1, :].unsqueeze(2).broadcast_to([P, NB, CB]),
                                 iob[:, 0:CB].unsqueeze(1).broadcast_to([P, NB, CB]), ALU.is_equal))
            v.tensor_scalar(place_w[:, :, 0, :], place_hi, pidx[:, 0:1], None, ALU.mult)
            v.tensor_tensor(place_w[:, :, 1, :], place_hi, iob[:, 0:NB].unsqueeze(2).broadcast_to([P, NB, CB]), ALU.mult)
            v.tensor_tensor(place_lo, part_b[:, 0, :].unsqueeze(2).broadcast_to([P, NB, P]),
                            iob[:, :].unsqueeze(1).broadcast_to([P, NB, P]), ALU.is_equal).then_inc(s_place, 1)
            dve.wait_ge(s_list, 1)
            link(v.tensor_scalar(sm0[:, 0:CB], psE[:, 3, CB:2 * CB], float(P), None, ALU.mult))
            v.tensor_tensor(picked[:, :], sm0[:, 0:CB], psE[:, 3, 0:CB], ALU.add).then_inc(s_picked, 1)

            def rows(m, r, i, blocks=2):
                for q in range(blocks):
                    dve.wait_ge(s_h[2 * r + q], 16 * i + 16)
                dve.wait_ge(s_ftp, m + 1)
                v.tensor_copy(zst[:, r, 0:blocks * D].rearrange("p (q d) -> p q d", d=D),
                              hg[:, bass.ds(2 * m, blocks), 0:D]).then_inc(s_fz, 1)

            def turned(m, r, blocks=2):
                dve.wait_ge(s_ftp, m + 3)
                dve.wait_ge(s_fy, 2 * m + 1)
                w = blocks * P
                v.tensor_copy(zts[:, r, :].rearrange("p (t n) -> p t n", t=2)[:, :, 0:w],
                              psT[:, r, :].rearrange("p (t n) -> p t n", t=2)[:, :, 0:w]).then_inc(s_fts, 1)

            def finish(m, r, i, blocks=2):
                for q in range(blocks):
                    dve.wait_ge(s_base[2 * r + q], 16 * i + 16)
                    dve.wait_ge(s_fy, 2 * m + q + 3)
                    v.tensor_tensor(gprod[:, q, :], psY[:, q, 0:D], b2s[:, :], ALU.add).then_inc(s_fc, 1)
                    c = 2 * m + q
                    dve.wait_ge(s_fc, c + 3)
                    v.scalar_tensor_tensor(base[:, c, :], gprod[:, q, :], hg[:, c, D:DW], base[:, c, :],
                                           ALU.mult, ALU.add).then_inc(s_fo, 1)
                dve.wait_ge(s_fo, 2 * m + blocks + 2)

            rows(0, 0, 0)
            turned(0, 0)
            rows(1, 1, 0)
            with dve.Fori(0, FI // 2 - 1) as i:
                turned(2 * i + 1, 1)
                rows(2 * i + 2, 0, i + 1)
                finish(2 * i, 0, i)
                turned(2 * i + 2, 0)
                rows(2 * i + 3, 1, i + 1)
                finish(2 * i + 1, 1, i)
            turned(FI - 2, 1)
            rows(FI - 1, 0, FI // 2, 1)
            finish(FI - 3, 0, FI // 2 - 1)
            turned(FI - 1, 0, 1)
            finish(FI - 2, 1, FI // 2 - 1)
            finish(FI - 1, 0, FI // 2, 1)


_INS = ['x', 'src', 'dst', 'edge_type_500', 'L0_gnn_W1', 'L0_gnn_W2', 'L0_gnn_b', 'L0_ffn_weight', 'L0_ffn_bias',
        'L1_gnn_relation_emb', 'L1_gnn_msg_w', 'L1_gnn_msg_b', 'L1_gnn_upd_w', 'L1_gnn_upd_b', 'L1_gnn_gate_w',
        'L1_gnn_gate_b', 'L1_ffn_wr', 'L1_ffn_br', 'L1_ffn_w1', 'L1_ffn_b1', 'L1_ffn_w2', 'L1_ffn_b2']


def kernel(**inputs):
    import numpy as _np
    import concourse.bacc as _bacc
    from concourse.bass_utils import run_bass_kernel_spmd as _run

    nc = _bacc.Bacc("TRN2", target_bir_lowering=False, num_devices=1)
    arrays, args = {}, []
    for name in _INS:
        a = _np.ascontiguousarray(inputs[name])
        arrays[f"in_{name}"] = a
        args.append(nc.dram_tensor(f"in_{name}", a.shape, mybir.dt.from_np(a.dtype), kind="ExternalInput").ap())
    args.append(nc.dram_tensor("out_0", (N, D), F32, kind="ExternalOutput").ap())
    program(nc, *args)
    r = _run(nc, [arrays], core_ids=[0])
    return r.results[0]["out_0"]
```
